# Optimizing a Trainium2 kernel written in Bass

```python
import numpy as np
import jax
import jax.numpy as jnp

def _softmax(x, axis=-1):
    return jax.nn.softmax(x, axis=axis)

def _gelu(x):
    return jax.nn.gelu(x, approximate=True)

def _silu(x):
    return jax.nn.silu(x)

def _sigmoid(x):
    return jax.nn.sigmoid(x)

def _layernorm(x, axis=-1, eps=1e-05):
    m = jnp.mean(x, axis=axis, keepdims=True)
    v = jnp.var(x, axis=axis, keepdims=True)
    return (x - m) / jnp.sqrt(v + eps)

def _scatter_add(tgt, idx, src, axis=0):
    return tgt.at[idx].add(src)

def _segment_sum(src, seg, n):
    return jax.ops.segment_sum(src, seg, n)
kernel_name = 'mk_adj_ffn_d4_adj_r2_802263'

def setup_inputs(seed: int=0):
    np.random.seed(seed)
    _w = jnp.asarray

    def _rec_inputs():
        import jax
        import jax.numpy as jnp
        _gk = jax.random.key(seed)
        x = -0.0002928 + 1 * jax.random.normal(jax.random.fold_in(_gk, 1), (64, 128, 128), jnp.float32)
        _a = jax.random.bernoulli(jax.random.fold_in(_gk, 2), 0.03125, (64, 128, 128))
        _a = jnp.logical_or(_a, jnp.eye(128, dtype=bool))
        _af = _a.astype(jnp.float32)
        _af = _af * jax.random.uniform(jax.random.fold_in(_gk, 3), (64, 128, 128), jnp.float32, 0.05, 1)
        adj = _af
        _nm = jnp.ones((64, 128), dtype=bool)
        nodemask = jnp.where(_nm, 1.0, 0.0).astype(jnp.int32)
        return (x, adj, nodemask)
    x, adj, nodemask = _rec_inputs()

    def _L0_gnn_setup():
        import jax, jax.numpy as jnp
        import numpy as np
        D_IN = 128
        D_OUT = 128
        key = jax.random.key(seed)
        k1, k2, k3 = jax.random.split(key, 3)
        B, N = (4, 2048)
        seq = jax.random.normal(k1, (B, N, D_IN), dtype=jnp.float32)
        adj = jax.random.uniform(k2, (B, N, N), dtype=jnp.float32)
        limit = float(np.sqrt(6.0 / (D_IN + D_OUT)))
        W = jax.random.uniform(k3, (D_IN, D_OUT), dtype=jnp.float32, minval=-limit, maxval=limit)
        bias = jnp.zeros((D_OUT,), dtype=jnp.float32)
        prelu_a = jnp.array(0.25, dtype=jnp.float32)
        return {'seq': seq, 'adj': adj, 'W': W, 'bias': bias, 'prelu_a': prelu_a}
    _L0_gnn_all = _L0_gnn_setup()
    _L0_gnn_in = {k: v for k, v in _L0_gnn_all.items() if k in ('W', 'bias', 'prelu_a')}
    del _L0_gnn_all

    def _L0_ffn_setup():
        import jax, jax.numpy as jnp
        import numpy as np
        E, D, H, TOP_K = (6, 128, 128, 2)
        ROUTER_H = D // 2
        key = jax.random.key(seed)
        ks = jax.random.split(key, 12)
        s = 1.0 / np.sqrt(D)
        sh = 1.0 / np.sqrt(H)
        sr = 1.0 / np.sqrt(ROUTER_H)
        return {'features': jax.random.normal(ks[0], (8, 2048, D), dtype=jnp.float32), 'router_w1': jax.random.uniform(ks[1], (D, ROUTER_H), jnp.float32, -s, s), 'router_b1': jnp.zeros((ROUTER_H,), jnp.float32), 'router_w2': jax.random.uniform(ks[2], (ROUTER_H, E), jnp.float32, -sr, sr), 'router_b2': jnp.zeros((E,), jnp.float32), 'expert_w1': jax.random.uniform(ks[3], (E, D, H), jnp.float32, -s, s), 'expert_b1': jnp.zeros((E, H), jnp.float32), 'expert_w2': jax.random.uniform(ks[4], (E, H, H), jnp.float32, -sh, sh), 'expert_b2': jnp.zeros((E, H), jnp.float32), 'expert_w3': jax.random.uniform(ks[5], (E, H, D), jnp.float32, -sh, sh), 'expert_b3': jnp.zeros((E, D), jnp.float32)}
    _L0_ffn_all = _L0_ffn_setup()
    _L0_ffn_in = {k: v for k, v in _L0_ffn_all.items() if k in ('router_w1', 'router_b1', 'router_w2', 'router_b2', 'expert_w1', 'expert_b1', 'expert_w2', 'expert_b2', 'expert_w3', 'expert_b3')}
    del _L0_ffn_all

    def _L1_gnn_setup():
        import jax, jax.numpy as jnp
        import numpy as np
        from jax import lax
        DIM = 128
        EPS = 1e-05

        def _bn(h, g, b, m, v):
            scale = g / jnp.sqrt(v + EPS)
            return h * scale[None, :, None] + (b - m * scale)[None, :, None]

        def _conv1d(h, w, pad):
            return lax.conv_general_dilated(h, w, window_strides=(1,), padding=[(pad, pad)], dimension_numbers=('NCH', 'OIH', 'NCH'))
        key = jax.random.key(seed)
        ks = jax.random.split(key, 16)
        bs, n, d = (16, 1024, DIM)
        s = 0.05
        return {'x': jax.random.normal(ks[0], (bs, n, d), jnp.float32), 'mask': jnp.ones((bs, n, n), jnp.float32), 'w_se': jax.random.normal(ks[1], (3, d), jnp.float32) * s, 'b_se': jnp.zeros((3,), jnp.float32), 'conv1_w': jax.random.normal(ks[2], (d, d, 1), jnp.float32) * s, 'bn1_g': jnp.ones((d,), jnp.float32), 'bn1_b': jnp.zeros((d,), jnp.float32), 'bn1_m': jnp.zeros((d,), jnp.float32), 'bn1_v': jnp.ones((d,), jnp.float32), 'conv2_w': jax.random.normal(ks[3], (d, d, 17), jnp.float32) * s, 'bn2_g': jnp.ones((d,), jnp.float32), 'bn2_b': jnp.zeros((d,), jnp.float32), 'bn2_m': jnp.zeros((d,), jnp.float32), 'bn2_v': jnp.ones((d,), jnp.float32), 'w_msg': jax.random.normal(ks[4], (d, d), jnp.float32) * s, 'b_msg': jnp.zeros((d,), jnp.float32), 'w_ih': jax.random.normal(ks[5], (3 * d, 2 * d), jnp.float32) * s, 'b_ih': jnp.zeros((3 * d,), jnp.float32), 'w_hh': jax.random.normal(ks[6], (3 * d, d), jnp.float32) * s, 'b_hh': jnp.zeros((3 * d,), jnp.float32)}
    _L1_gnn_all = _L1_gnn_setup()
    _L1_gnn_in = {k: v for k, v in _L1_gnn_all.items() if k in ('w_se', 'b_se', 'conv1_w', 'bn1_g', 'bn1_b', 'bn1_m', 'bn1_v', 'conv2_w', 'bn2_g', 'bn2_b', 'bn2_m', 'bn2_v', 'w_msg', 'b_msg', 'w_ih', 'b_ih', 'w_hh', 'b_hh')}
    del _L1_gnn_all

    def _L1_ffn_setup():
        import jax, jax.numpy as jnp
        import numpy as np
        B, N, D = (16, 2048, 128)
        NUM_EXPERTS, TOP_K, HEADS = (4, 2, 4)
        N_EDGES = 524288
        LN_EPS = 1e-05

        def _layernorm(x, g, b):
            mu = x.mean(-1, keepdims=True)
            var = ((x - mu) ** 2).mean(-1, keepdims=True)
            return (x - mu) * jax.lax.rsqrt(var + LN_EPS) * g + b

        def _forward(x, edge_index, W_gat, att_src, att_dst, b_gat, ln_gamma, ln_beta, W1, b1, W2, b2):
            Bc, Nc, Dc = x.shape
            M = Bc * Nc
            x_flat = x.reshape(M, Dc)
            h = (x_flat @ W_gat).reshape(M, HEADS, NUM_EXPERTS)
            loops = jnp.arange(M, dtype=edge_index.dtype)
            src = jnp.concatenate([edge_index[0], loops])
            dst = jnp.concatenate([edge_index[1], loops])
            a_src = (h * att_src).sum(-1)
            a_dst = (h * att_dst).sum(-1)
            e = jax.nn.leaky_relu(a_src[src] + a_dst[dst], negative_slope=0.2)
            e_max = jax.ops.segment_max(e, dst, num_segments=M)
            ee = jnp.exp(e - e_max[dst])
            denom = jax.ops.segment_sum(ee, dst, num_segments=M)
            alpha = ee / (denom[dst] + 1e-16)
            msg = h[src] * alpha[:, :, None]
            agg = jax.ops.segment_sum(msg, dst, num_segments=M).reshape(M, HEADS * NUM_EXPERTS) + b_gat
            scores = _layernorm(agg, ln_gamma, ln_beta).reshape(M, HEADS, NUM_EXPERTS).mean(1)
            scores = scores.reshape(Bc, Nc, NUM_EXPERTS)
            topk_s, topk_i = jax.lax.top_k(scores, TOP_K)
            w = jax.nn.softmax(topk_s, axis=-1)
            out = jnp.zeros_like(x)
            for ei in range(NUM_EXPERTS):
                g = jnp.where(topk_i == ei, w, 0.0).sum(-1)
                hh = jax.nn.gelu(x @ W1[ei] + b1[ei], approximate=False)
                out = out + g[..., None] * (hh @ W2[ei] + b2[ei])
            return out
        key = jax.random.key(seed)
        ks = jax.random.split(key, 8)
        s = 0.05
        return {'x': jax.random.normal(ks[0], (B, N, D), jnp.float32), 'W_gat': jax.random.normal(ks[1], (D, HEADS * NUM_EXPERTS), jnp.float32) * s, 'att_src': jax.random.normal(ks[2], (HEADS, NUM_EXPERTS), jnp.float32) * s, 'att_dst': jax.random.normal(ks[3], (HEADS, NUM_EXPERTS), jnp.float32) * s, 'b_gat': jnp.zeros((HEADS * NUM_EXPERTS,), jnp.float32), 'ln_gamma': jnp.ones((HEADS * NUM_EXPERTS,), jnp.float32), 'ln_beta': jnp.zeros((HEADS * NUM_EXPERTS,), jnp.float32), 'W1': jax.random.normal(ks[4], (NUM_EXPERTS, D, 2 * D), jnp.float32) * s, 'b1': jnp.zeros((NUM_EXPERTS, 2 * D), jnp.float32), 'W2': jax.random.normal(ks[5], (NUM_EXPERTS, 2 * D, D), jnp.float32) * s, 'b2': jnp.zeros((NUM_EXPERTS, D), jnp.float32), 'edge_index': jax.random.randint(ks[6], (2, N_EDGES), 0, B * N, jnp.int32)}
    _L1_ffn_all = _L1_ffn_setup()
    _L1_ffn_in = {k: v for k, v in _L1_ffn_all.items() if k in ('W_gat', 'att_src', 'att_dst', 'b_gat', 'ln_gamma', 'ln_beta', 'W1', 'b1', 'W2', 'b2', 'edge_index')}
    del _L1_ffn_all

    def _L2_gnn_setup():
        import jax, jax.numpy as jnp
        import numpy as np
        B, K, H = (32, 512, 128)
        LN_EPS = 1e-05

        def layer_norm(x, gamma, beta):
            mu = jnp.mean(x, axis=-1, keepdims=True)
            var = jnp.mean(jnp.square(x - mu), axis=-1, keepdims=True)
            return (x - mu) * jax.lax.rsqrt(var + LN_EPS) * gamma + beta
        key = jax.random.key(seed)
        k1, k2, k3, k4 = jax.random.split(key, 4)
        x = jax.random.normal(k1, (B, K, H), dtype=jnp.float32)
        adj = jax.random.uniform(k2, (B, K, K), dtype=jnp.float32)
        s = 1.0 / np.sqrt(H)
        W_rel = jax.random.normal(k3, (H, H), dtype=jnp.float32) * s
        b_rel = jnp.zeros((H,), dtype=jnp.float32)
        W_root = jax.random.normal(k4, (H, H), dtype=jnp.float32) * s
        ln_gamma = jnp.ones((H,), dtype=jnp.float32)
        ln_beta = jnp.zeros((H,), dtype=jnp.float32)
        return {'x': x, 'adj': adj, 'W_rel': W_rel, 'b_rel': b_rel, 'W_root': W_root, 'ln_gamma': ln_gamma, 'ln_beta': ln_beta}
    _L2_gnn_all = _L2_gnn_setup()
    _L2_gnn_in = {k: v for k, v in _L2_gnn_all.items() if k in ('W_rel', 'b_rel', 'W_root', 'ln_gamma', 'ln_beta')}
    del _L2_gnn_all

    def _L2_ffn_setup():
        import jax, jax.numpy as jnp
        import numpy as np
        B, S, D, F, E, K = (8, 1024, 128, 512, 8, 2)
        key = jax.random.key(seed)
        ks = jax.random.split(key, 10)
        s = 0.02
        return {'x': jax.random.normal(ks[0], (B, S, D), dtype=jnp.float32), 'Wr': jax.random.normal(ks[1], (D, E), dtype=jnp.float32) * s, 'W1s': jax.random.normal(ks[2], (D, F), dtype=jnp.float32) * s, 'b1s': jnp.zeros((F,), dtype=jnp.float32), 'W2s': jax.random.normal(ks[3], (F, D), dtype=jnp.float32) * s, 'b2s': jnp.zeros((D,), dtype=jnp.float32), 'W1p': jax.random.normal(ks[4], (E, D, F), dtype=jnp.float32) * s, 'b1p': jnp.zeros((E, F), dtype=jnp.float32), 'W2p': jax.random.normal(ks[5], (E, F, D), dtype=jnp.float32) * s, 'b2p': jnp.zeros((E, D), dtype=jnp.float32)}
    _L2_ffn_all = _L2_ffn_setup()
    _L2_ffn_in = {k: v for k, v in _L2_ffn_all.items() if k in ('Wr', 'W1s', 'b1s', 'W2s', 'b2s', 'W1p', 'b1p', 'W2p', 'b2p')}
    del _L2_ffn_all

    def _L3_gnn_setup():
        import jax, jax.numpy as jnp
        import numpy as np
        HIDDEN = 128
        NEG_INF = -1e+30
        key = jax.random.key(seed)
        k1, k2, k3, k4 = jax.random.split(key, 4)
        B, S, H = (4, 2048, HIDDEN)
        matrix = jax.random.normal(k1, (B, S, H), dtype=jnp.float32)
        mask = jax.random.randint(k2, (B, S), 0, 2, dtype=jnp.int32)
        adj = jax.random.uniform(k3, (B, S, S), dtype=jnp.float32)
        limit = float(np.sqrt(6.0 / (H + H)))
        W = jax.random.uniform(k4, (H, H), dtype=jnp.float32, minval=-limit, maxval=limit)
        return {'matrix': matrix, 'mask': mask, 'adj': adj, 'W': W}
    _L3_gnn_all = _L3_gnn_setup()
    _L3_gnn_in = {k: v for k, v in _L3_gnn_all.items() if k in ('W',)}
    del _L3_gnn_all

    def _L3_ffn_setup():
        import jax, jax.numpy as jnp
        import numpy as np
        B, S, D, H, E, K = (8, 4096, 128, 512, 8, 2)
        key = jax.random.key(seed)
        ks = jax.random.split(key, 7)
        s_in = 1.0 / np.sqrt(D)
        s_hid = 1.0 / np.sqrt(H)
        return {'x': jax.random.normal(ks[0], (B, S, D), dtype=jnp.float32), 'Wg': jax.random.uniform(ks[1], (E, D), jnp.float32, -s_in, s_in), 'bg': jax.random.uniform(ks[2], (E,), jnp.float32, -s_in, s_in), 'W1': jax.random.uniform(ks[3], (E, H, D), jnp.float32, -s_in, s_in), 'b1': jax.random.uniform(ks[4], (E, H), jnp.float32, -s_in, s_in), 'W2': jax.random.uniform(ks[5], (E, D, H), jnp.float32, -s_hid, s_hid), 'b2': jax.random.uniform(ks[6], (E, D), jnp.float32, -s_hid, s_hid)}
    _L3_ffn_all = _L3_ffn_setup()
    _L3_ffn_in = {k: v for k, v in _L3_ffn_all.items() if k in ('Wg', 'bg', 'W1', 'b1', 'W2', 'b2')}
    del _L3_ffn_all
    return {'x': x, 'adj': adj, 'nodemask': nodemask, 'L0_gnn_W': _L0_gnn_in['W'], 'L0_gnn_bias': _L0_gnn_in['bias'], 'L0_gnn_prelu_a': _L0_gnn_in['prelu_a'], 'L0_ffn_router_w1': _L0_ffn_in['router_w1'], 'L0_ffn_router_b1': _L0_ffn_in['router_b1'], 'L0_ffn_router_w2': _L0_ffn_in['router_w2'], 'L0_ffn_router_b2': _L0_ffn_in['router_b2'], 'L0_ffn_expert_w1': _L0_ffn_in['expert_w1'], 'L0_ffn_expert_b1': _L0_ffn_in['expert_b1'], 'L0_ffn_expert_w2': _L0_ffn_in['expert_w2'], 'L0_ffn_expert_b2': _L0_ffn_in['expert_b2'], 'L0_ffn_expert_w3': _L0_ffn_in['expert_w3'], 'L0_ffn_expert_b3': _L0_ffn_in['expert_b3'], 'L1_gnn_w_se': _L1_gnn_in['w_se'], 'L1_gnn_b_se': _L1_gnn_in['b_se'], 'L1_gnn_conv1_w': _L1_gnn_in['conv1_w'], 'L1_gnn_bn1_g': _L1_gnn_in['bn1_g'], 'L1_gnn_bn1_b': _L1_gnn_in['bn1_b'], 'L1_gnn_bn1_m': _L1_gnn_in['bn1_m'], 'L1_gnn_bn1_v': _L1_gnn_in['bn1_v'], 'L1_gnn_conv2_w': _L1_gnn_in['conv2_w'], 'L1_gnn_bn2_g': _L1_gnn_in['bn2_g'], 'L1_gnn_bn2_b': _L1_gnn_in['bn2_b'], 'L1_gnn_bn2_m': _L1_gnn_in['bn2_m'], 'L1_gnn_bn2_v': _L1_gnn_in['bn2_v'], 'L1_gnn_w_msg': _L1_gnn_in['w_msg'], 'L1_gnn_b_msg': _L1_gnn_in['b_msg'], 'L1_gnn_w_ih': _L1_gnn_in['w_ih'], 'L1_gnn_b_ih': _L1_gnn_in['b_ih'], 'L1_gnn_w_hh': _L1_gnn_in['w_hh'], 'L1_gnn_b_hh': _L1_gnn_in['b_hh'], 'L1_ffn_W_gat': _L1_ffn_in['W_gat'], 'L1_ffn_att_src': _L1_ffn_in['att_src'], 'L1_ffn_att_dst': _L1_ffn_in['att_dst'], 'L1_ffn_b_gat': _L1_ffn_in['b_gat'], 'L1_ffn_ln_gamma': _L1_ffn_in['ln_gamma'], 'L1_ffn_ln_beta': _L1_ffn_in['ln_beta'], 'L1_ffn_W1': _L1_ffn_in['W1'], 'L1_ffn_b1': _L1_ffn_in['b1'], 'L1_ffn_W2': _L1_ffn_in['W2'], 'L1_ffn_b2': _L1_ffn_in['b2'], 'L1_ffn_edge_index': _L1_ffn_in['edge_index'], 'L2_gnn_W_rel': _L2_gnn_in['W_rel'], 'L2_gnn_b_rel': _L2_gnn_in['b_rel'], 'L2_gnn_W_root': _L2_gnn_in['W_root'], 'L2_gnn_ln_gamma': _L2_gnn_in['ln_gamma'], 'L2_gnn_ln_beta': _L2_gnn_in['ln_beta'], 'L2_ffn_Wr': _L2_ffn_in['Wr'], 'L2_ffn_W1s': _L2_ffn_in['W1s'], 'L2_ffn_b1s': _L2_ffn_in['b1s'], 'L2_ffn_W2s': _L2_ffn_in['W2s'], 'L2_ffn_b2s': _L2_ffn_in['b2s'], 'L2_ffn_W1p': _L2_ffn_in['W1p'], 'L2_ffn_b1p': _L2_ffn_in['b1p'], 'L2_ffn_W2p': _L2_ffn_in['W2p'], 'L2_ffn_b2p': _L2_ffn_in['b2p'], 'L3_gnn_W': _L3_gnn_in['W'], 'L3_ffn_Wg': _L3_ffn_in['Wg'], 'L3_ffn_bg': _L3_ffn_in['bg'], 'L3_ffn_W1': _L3_ffn_in['W1'], 'L3_ffn_b1': _L3_ffn_in['b1'], 'L3_ffn_W2': _L3_ffn_in['W2'], 'L3_ffn_b2': _L3_ffn_in['b2']}

def reference(x, adj, nodemask, L0_gnn_W, L0_gnn_bias, L0_gnn_prelu_a, L0_ffn_router_w1, L0_ffn_router_b1, L0_ffn_router_w2, L0_ffn_router_b2, L0_ffn_expert_w1, L0_ffn_expert_b1, L0_ffn_expert_w2, L0_ffn_expert_b2, L0_ffn_expert_w3, L0_ffn_expert_b3, L1_gnn_w_se, L1_gnn_b_se, L1_gnn_conv1_w, L1_gnn_bn1_g, L1_gnn_bn1_b, L1_gnn_bn1_m, L1_gnn_bn1_v, L1_gnn_conv2_w, L1_gnn_bn2_g, L1_gnn_bn2_b, L1_gnn_bn2_m, L1_gnn_bn2_v, L1_gnn_w_msg, L1_gnn_b_msg, L1_gnn_w_ih, L1_gnn_b_ih, L1_gnn_w_hh, L1_gnn_b_hh, L1_ffn_W_gat, L1_ffn_att_src, L1_ffn_att_dst, L1_ffn_b_gat, L1_ffn_ln_gamma, L1_ffn_ln_beta, L1_ffn_W1, L1_ffn_b1, L1_ffn_W2, L1_ffn_b2, L1_ffn_edge_index, L2_gnn_W_rel, L2_gnn_b_rel, L2_gnn_W_root, L2_gnn_ln_gamma, L2_gnn_ln_beta, L2_ffn_Wr, L2_ffn_W1s, L2_ffn_b1s, L2_ffn_W2s, L2_ffn_b2s, L2_ffn_W1p, L2_ffn_b1p, L2_ffn_W2p, L2_ffn_b2p, L3_gnn_W, L3_ffn_Wg, L3_ffn_bg, L3_ffn_W1, L3_ffn_b1, L3_ffn_W2, L3_ffn_b2):
    import jax
    import jax.numpy as jnp

    def _L0_gnn_ref(seq, adj, W, bias, prelu_a):
        import jax, jax.numpy as jnp
        import numpy as np
        D_IN = 128
        D_OUT = 128
        seq_fts = jnp.einsum('bnd,de->bne', seq, W)
        out = jnp.einsum('bnm,bme->bne', adj, seq_fts) + bias
        return jnp.where(out >= 0, out, prelu_a * out)

    def _L0_ffn_ref(features, router_w1, router_b1, router_w2, router_b2, expert_w1, expert_b1, expert_w2, expert_b2, expert_w3, expert_b3):
        import jax, jax.numpy as jnp
        import numpy as np
        E, D, H, TOP_K = (6, 128, 128, 2)
        ROUTER_H = D // 2
        rh = jax.nn.relu(features @ router_w1 + router_b1)
        expert_logits = jax.nn.softmax(rh @ router_w2 + router_b2, axis=-1)
        top_w, top_i = jax.lax.top_k(expert_logits, TOP_K)
        routing_weights = jax.nn.softmax(top_w, axis=-1)
        h1 = jax.nn.relu(jnp.einsum('bsd,edh->bseh', features, expert_w1) + expert_b1)
        h2 = jax.nn.relu(jnp.einsum('bseh,ehf->bsef', h1, expert_w2) + expert_b2)
        expert_out = jnp.einsum('bsef,efo->bseo', h2, expert_w3) + expert_b3
        sel = jnp.take_along_axis(expert_out, top_i[:, :, :, None], axis=2)
        combined = jnp.sum(sel * routing_weights[..., None], axis=2)
        return combined

    def _L1_gnn_ref(x, mask, w_se, b_se, conv1_w, bn1_g, bn1_b, bn1_m, bn1_v, conv2_w, bn2_g, bn2_b, bn2_m, bn2_v, w_msg, b_msg, w_ih, b_ih, w_hh, b_hh):
        import jax, jax.numpy as jnp
        import numpy as np
        from jax import lax
        DIM = 128
        EPS = 1e-05

        def _bn(h, g, b, m, v):
            scale = g / jnp.sqrt(v + EPS)
            return h * scale[None, :, None] + (b - m * scale)[None, :, None]

        def _conv1d(h, w, pad):
            return lax.conv_general_dilated(h, w, window_strides=(1,), padding=[(pad, pad)], dimension_numbers=('NCH', 'OIH', 'NCH'))
        d = x.shape[-1]
        xc = jnp.transpose(x, (0, 2, 1))
        h = _bn(_conv1d(xc, conv1_w, 0), bn1_g, bn1_b, bn1_m, bn1_v)
        h = jax.nn.relu(h)
        h = _bn(_conv1d(h, conv2_w, 8), bn2_g, bn2_b, bn2_m, bn2_v)
        x_conv = jnp.transpose(jax.nn.relu(h + xc), (0, 2, 1))
        s = x @ w_se.T + b_se
        sq = jnp.sum(s * s, axis=-1)
        dist = sq[:, :, None] + sq[:, None, :] - 2.0 * jnp.einsum('bnd,bmd->bnm', s, s)
        A = jnp.exp(-dist) * mask
        msg = jax.nn.relu(x @ w_msg.T + b_msg)
        x_nmp = jnp.einsum('bnm,bmd->bnd', A, msg)
        x_in = jnp.concatenate([x_conv, x_nmp], axis=-1)
        gi = x_in @ w_ih.T + b_ih
        gh = x @ w_hh.T + b_hh
        gi_r, gi_z, gi_n = (gi[..., :d], gi[..., d:2 * d], gi[..., 2 * d:])
        gh_r, gh_z, gh_n = (gh[..., :d], gh[..., d:2 * d], gh[..., 2 * d:])
        r = jax.nn.sigmoid(gi_r + gh_r)
        z = jax.nn.sigmoid(gi_z + gh_z)
        nn_ = jnp.tanh(gi_n + r * gh_n)
        return (1.0 - z) * nn_ + z * x

    def _L1_ffn_ref(x, W_gat, att_src, att_dst, b_gat, ln_gamma, ln_beta, W1, b1, W2, b2, edge_index):
        import jax, jax.numpy as jnp
        import numpy as np
        B, N, D = (16, 2048, 128)
        NUM_EXPERTS, TOP_K, HEADS = (4, 2, 4)
        N_EDGES = 524288
        LN_EPS = 1e-05

        def _layernorm(x, g, b):
            mu = x.mean(-1, keepdims=True)
            var = ((x - mu) ** 2).mean(-1, keepdims=True)
            return (x - mu) * jax.lax.rsqrt(var + LN_EPS) * g + b

        def _forward(x, edge_index, W_gat, att_src, att_dst, b_gat, ln_gamma, ln_beta, W1, b1, W2, b2):
            Bc, Nc, Dc = x.shape
            M = Bc * Nc
            x_flat = x.reshape(M, Dc)
            h = (x_flat @ W_gat).reshape(M, HEADS, NUM_EXPERTS)
            loops = jnp.arange(M, dtype=edge_index.dtype)
            src = jnp.concatenate([edge_index[0], loops])
            dst = jnp.concatenate([edge_index[1], loops])
            a_src = (h * att_src).sum(-1)
            a_dst = (h * att_dst).sum(-1)
            e = jax.nn.leaky_relu(a_src[src] + a_dst[dst], negative_slope=0.2)
            e_max = jax.ops.segment_max(e, dst, num_segments=M)
            ee = jnp.exp(e - e_max[dst])
            denom = jax.ops.segment_sum(ee, dst, num_segments=M)
            alpha = ee / (denom[dst] + 1e-16)
            msg = h[src] * alpha[:, :, None]
            agg = jax.ops.segment_sum(msg, dst, num_segments=M).reshape(M, HEADS * NUM_EXPERTS) + b_gat
            scores = _layernorm(agg, ln_gamma, ln_beta).reshape(M, HEADS, NUM_EXPERTS).mean(1)
            scores = scores.reshape(Bc, Nc, NUM_EXPERTS)
            topk_s, topk_i = jax.lax.top_k(scores, TOP_K)
            w = jax.nn.softmax(topk_s, axis=-1)
            out = jnp.zeros_like(x)
            for ei in range(NUM_EXPERTS):
                g = jnp.where(topk_i == ei, w, 0.0).sum(-1)
                hh = jax.nn.gelu(x @ W1[ei] + b1[ei], approximate=False)
                out = out + g[..., None] * (hh @ W2[ei] + b2[ei])
            return out
        return _forward(x, edge_index, W_gat, att_src, att_dst, b_gat, ln_gamma, ln_beta, W1, b1, W2, b2)

    def _L2_gnn_ref(x, adj, W_rel, b_rel, W_root, ln_gamma, ln_beta):
        import jax, jax.numpy as jnp
        import numpy as np
        B, K, H = (32, 512, 128)
        LN_EPS = 1e-05

        def layer_norm(x, gamma, beta):
            mu = jnp.mean(x, axis=-1, keepdims=True)
            var = jnp.mean(jnp.square(x - mu), axis=-1, keepdims=True)
            return (x - mu) * jax.lax.rsqrt(var + LN_EPS) * gamma + beta
        h = layer_norm(x, ln_gamma, ln_beta)
        agg = jnp.einsum('bij,bjh->bih', adj, h)
        conv = jnp.einsum('bkh,ho->bko', agg, W_rel) + b_rel + jnp.einsum('bkh,ho->bko', h, W_root)
        return x + jax.nn.relu(conv)

    def _L2_ffn_ref(x, Wr, W1s, b1s, W2s, b2s, W1p, b1p, W2p, b2p):
        import jax, jax.numpy as jnp
        import numpy as np
        B, S, D, F, E, K = (8, 1024, 128, 512, 8, 2)
        gelu = lambda t: jax.nn.gelu(t, approximate=False)
        shared = gelu(x @ W1s + b1s) @ W2s + b2s
        rw = jax.nn.softmax(x @ Wr, axis=-1)
        topw, topi = jax.lax.top_k(rw, K)
        topw = topw / jnp.sum(topw, axis=-1, keepdims=True)
        mask = jnp.sum(jax.nn.one_hot(topi, E, dtype=topw.dtype) * topw[..., None], axis=-2)
        h = gelu(jnp.einsum('bsd,edf->bsef', x, W1p) + b1p)
        priv = jnp.einsum('bsef,efd->bsed', h, W2p) + b2p
        routed = jnp.einsum('bsed,bse->bsd', priv, mask)
        return shared + routed

    def _L3_gnn_ref(matrix, mask, adj, W):
        import jax, jax.numpy as jnp
        import numpy as np
        HIDDEN = 128
        NEG_INF = -1e+30
        intermediate = jnp.einsum('bsh,hd->bsd', matrix, W)
        similarities = jnp.einsum('bsd,btd->bst', intermediate, matrix)
        similarities = similarities * adj
        key_mask = mask[:, None, :].astype(bool)
        masked = jnp.where(key_mask, similarities, NEG_INF)
        attn = jax.nn.softmax(masked, axis=-1)
        output = jnp.einsum('bst,bth->bsh', attn, matrix)
        return output

    def _L3_ffn_ref(x, Wg, bg, W1, b1, W2, b2):
        import jax, jax.numpy as jnp
        import numpy as np
        B, S, D, H, E, K = (8, 4096, 128, 512, 8, 2)
        gate_scores = jnp.einsum('bsd,ed->bse', x, Wg) + bg
        topk_scores, topk_idx = jax.lax.top_k(gate_scores, K)
        topk_probs = jax.nn.softmax(topk_scores, axis=-1)
        combine = jnp.sum(topk_probs[..., None] * jax.nn.one_hot(topk_idx, E, dtype=x.dtype), axis=-2)
        out = jnp.zeros_like(x)
        for e in range(E):
            h = jax.nn.relu(jnp.einsum('bsd,hd->bsh', x, W1[e]) + b1[e])
            y = jnp.einsum('bsh,dh->bsd', h, W2[e]) + b2[e]
            out = out + combine[..., e:e + 1] * y
        return out
    x = x + _L0_gnn_ref(_layernorm(x, axis=-1), adj, L0_gnn_W, L0_gnn_bias, L0_gnn_prelu_a)
    x = x + _L0_ffn_ref(_layernorm(x, axis=-1), L0_ffn_router_w1, L0_ffn_router_b1, L0_ffn_router_w2, L0_ffn_router_b2, L0_ffn_expert_w1, L0_ffn_expert_b1, L0_ffn_expert_w2, L0_ffn_expert_b2, L0_ffn_expert_w3, L0_ffn_expert_b3)
    x = x + _L1_gnn_ref(_layernorm(x, axis=-1), adj, L1_gnn_w_se, L1_gnn_b_se, L1_gnn_conv1_w, L1_gnn_bn1_g, L1_gnn_bn1_b, L1_gnn_bn1_m, L1_gnn_bn1_v, L1_gnn_conv2_w, L1_gnn_bn2_g, L1_gnn_bn2_b, L1_gnn_bn2_m, L1_gnn_bn2_v, L1_gnn_w_msg, L1_gnn_b_msg, L1_gnn_w_ih, L1_gnn_b_ih, L1_gnn_w_hh, L1_gnn_b_hh)
    x = x + _L1_ffn_ref(_layernorm(x, axis=-1), L1_ffn_W_gat, L1_ffn_att_src, L1_ffn_att_dst, L1_ffn_b_gat, L1_ffn_ln_gamma, L1_ffn_ln_beta, L1_ffn_W1, L1_ffn_b1, L1_ffn_W2, L1_ffn_b2, L1_ffn_edge_index)
    x = x + _L2_gnn_ref(_layernorm(x, axis=-1), adj, L2_gnn_W_rel, L2_gnn_b_rel, L2_gnn_W_root, L2_gnn_ln_gamma, L2_gnn_ln_beta)
    x = x + _L2_ffn_ref(_layernorm(x, axis=-1), L2_ffn_Wr, L2_ffn_W1s, L2_ffn_b1s, L2_ffn_W2s, L2_ffn_b2s, L2_ffn_W1p, L2_ffn_b1p, L2_ffn_W2p, L2_ffn_b2p)
    x = x + _L3_gnn_ref(_layernorm(x, axis=-1), nodemask, adj, L3_gnn_W)
    x = x + _L3_ffn_ref(_layernorm(x, axis=-1), L3_ffn_Wg, L3_ffn_bg, L3_ffn_W1, L3_ffn_b1, L3_ffn_W2, L3_ffn_b2)
    return x

_drawn_inputs = setup_inputs


def setup_inputs(seed=0):
    import zlib

    import numpy as np

    out = dict(_drawn_inputs(seed))
    spreads = {'L0_gnn_bias': (0.0, 0.1),
     'L0_ffn_router_b1': (0.0, 0.1),
     'L0_ffn_router_b2': (0.0, 0.1),
     'L0_ffn_expert_b1': (0.0, 0.8),
     'L0_ffn_expert_b2': (0.0, 0.321),
     'L0_ffn_expert_b3': (0.0, 0.1),
     'L1_gnn_b_se': (0.0, 2.0),
     'L1_gnn_bn1_g': (1.0, 0.6),
     'L1_gnn_bn1_b': (0.0, 0.481),
     'L1_gnn_bn1_m': (0.0, 0.449),
     'L1_gnn_bn1_v': (1.0, 0.6),
     'L1_gnn_bn2_g': (1.0, 0.575),
     'L1_gnn_bn2_b': (0.0, 0.8),
     'L1_gnn_bn2_m': (0.0, 0.613),
     'L1_gnn_bn2_v': (1.0, 0.6),
     'L1_gnn_b_msg': (0.0, 0.664),
     'L1_gnn_b_ih': (0.0, 0.289),
     'L1_gnn_b_hh': (0.0, 0.419),
     'L1_ffn_b_gat': (0.0, 0.417),
     'L1_ffn_ln_gamma': (1.0, 0.6),
     'L1_ffn_ln_beta': (0.0, 0.8),
     'L1_ffn_b1': (0.0, 0.402),
     'L1_ffn_b2': (0.0, 0.1),
     'L2_gnn_b_rel': (0.0, 0.358),
     'L2_gnn_ln_gamma': (1.0, 0.2),
     'L2_gnn_ln_beta': (0.0, 0.1),
     'L2_ffn_b1s': (0.0, 0.8),
     'L2_ffn_b2s': (0.0, 0.288),
     'L2_ffn_b1p': (0.0, 0.8),
     'L2_ffn_b2p': (0.0, 0.341)}
    factors = {'L1_gnn_w_se': 9.872,
     'L1_ffn_att_src': 8.0,
     'L1_ffn_att_dst': 24.742,
     'L2_ffn_W1s': 3.306,
     'L2_ffn_W2s': 2.974,
     'L2_ffn_W1p': 4.735,
     'L2_ffn_W2p': 4.276,
     'L3_ffn_bg': 5.743,
     'L3_ffn_b1': 8.0,
     'L3_ffn_b2': 8.0}
    for name, (base, spread) in spreads.items():
        noise = np.random.default_rng([zlib.crc32(name.encode()), seed]).standard_normal(out[name].shape)
        drawn = base * np.exp(spread * noise) if base else spread * noise
        out[name] = jnp.asarray(drawn.astype(out[name].dtype))
    for name, factor in factors.items():
        out[name] = (out[name] * factor).astype(out[name].dtype)
    return out
```

```python
from contextlib import ExitStack

import concourse.bass as bass
from concourse import mybir

F32, I32, U32 = mybir.dt.float32, mybir.dt.int32, mybir.dt.uint32
ALU, ACT, AX = mybir.AluOpType, mybir.ActivationFunctionType, mybir.AxisListType
RMAX = bass.bass_isa.ReduceOp.max

P = 128
D = 128
NODES = 64 * P
NT = NODES // P
NT1 = NT + 1
GT = 4
GROUPS = NT // GT
LN_EPS = 1e-5
BIG = 1e30

EXPERTS0, ROUTER_H = 6, 64
CONV_K, CONV_PAD = 17, 8
HEADS, EXPERTS1 = 4, 4
EXPERTS2, EXPERTS3 = 8, 8
EMAX = 9
ROW = HEADS * EXPERTS1 + HEADS
SLOPE = 0.2

E_TOTAL = 524288
SRC_BITS, DST_BITS = 13, 14
KEY_BASE = 0x10000000
SLOT_BITS = 5
SLOTS = 1 << SLOT_BITS
GROUP_BITS = 2
SLOT_GROUP = 1 << GROUP_BITS


def sort_edges(nc, env, edge_index):
    KA, KB = env.keys_a, env.keys_b
    start_of = env.start_of
    PER = E_TOTAL // P
    ROWBITS = PER.bit_length() - 1
    ALLBITS = E_TOTAL.bit_length() - 1

    with ExitStack() as ctx:
        sem = lambda n: ctx.enter_context(nc.semaphore(n))
        loaded, iota_done = sem("edges_loaded"), sem("iota_done")
        dve_step, flipped = sem("sort_dve_step"), sem("sort_flipped")
        trans, evac = sem("sort_blocks_transposed"), sem("sort_blocks_copied")
        stage_done = sem("sort_half_done")
        stored, first_loaded = sem("sorted_stored"), sem("row_firsts_loaded")
        want_l2, got_l2, want_l3, got_l3 = sem("l2_rows_ready"), sem("l2_rows_loaded"), sem("l3_rows_ready"), sem("l3_rows_loaded")
        start_ready, start_stored, start_loaded = sem("start_ready"), sem("start_stored"), sem("start_loaded")
        want_keys, got_keys, deg_ready, maxdeg_done = sem("key_rows_ready"), sem("key_rows_loaded"), sem("deg_ready"), sem("maxdeg_done")
        tail_set = sem("tail_keys_set")
        block = ctx.enter_context(nc.Block())

        phases = [("row", [(b, k) for k in range(1, ROWBITS) for b in range(k - 1, -1, -1)], None)]
        phases.append(("flip", None, 0))
        phases.append(("row", [(b, None) for b in range(ROWBITS - 1, -1, -1)], None))
        phases.append(("unflip", None, 0))
        for k in range(ROWBITS + 1, ALLBITS + 1):
            last = k == ALLBITS
            phases.append(("to_column", None, None))
            dirbit = None if last else k - ROWBITS
            phases.append(("column", [(b - ROWBITS, dirbit) for b in range(k - 1, ROWBITS - 1, -1)]
                           + [(b, dirbit) for b in range(ROWBITS - 1, 6, -1)], None))
            phases.append(("to_row", None, dirbit))
            phases.append(("row", [(b, None) for b in range(6, -1, -1)], None))
            if not last:
                phases.append(("unflip", None, dirbit))

        bufs = [KA, KB]
        plan, cur = [], 0
        for kind, steps, bit in phases:
            plan.append((kind, steps, bit, cur))
            cur ^= (len(steps) if steps else 1) & 1
        final = bufs[cur]

        def free_view(buf, a, b):
            hi, lo = max(a, b), min(a, b)
            v = buf[:, :].rearrange("p (h x m y l) -> p h x m y l", x=2, m=1 << (hi - lo - 1), y=2, l=1 << lo)
            if b > a:
                return lambda side, up: v[:, :, 1 - up, :, side, :]
            return lambda side, up: v[:, :, side, :, 1 - up, :]

        NBLK = PER // P
        GRP = 4

        @block.sync
        def _(sp):
            sp.dma_start(KA[:, :].bitcast(I32), edge_index[0, :].rearrange("(p f) -> p f", p=P)).then_inc(loaded, 16)
            sp.dma_start(KB[:, :].bitcast(I32), edge_index[1, :].rearrange("(p f) -> p f", p=P)).then_inc(loaded, 16)
            sp.wait_ge(stage_done, 1)
            sp.dma_start(env.sorted_dram[0:E_TOTAL].rearrange("(p f) -> p f", p=P), final[:, :]).then_inc(stored, 16)
            sp.dma_start(env.row_first_dram.rearrange("(p o) -> p o", o=1), final[:, 0:1]).then_inc(stored, 16)
            sp.dma_start(env.chunk_first_dram, env.chunk_first[:, :]).then_inc(stored, 16)
            sp.wait_ge(tail_set, 1)
            sp.dma_start(env.sorted_dram[E_TOTAL:E_TOTAL + SLOTS].rearrange("(o f) -> o f", o=1), env.tail_keys[0:1, :]).then_inc(stored, 16)
            sp.wait_ge(stored, 64)
            sp.dma_start(env.row_first[:, :], env.row_first_dram.partition_broadcast(P)).then_inc(first_loaded, 16)
            sp.wait_ge(start_ready, 1)
            sp.dma_start(env.start_dram[0:NT1 * P].rearrange("(t p) -> p t", p=P), start_of[:, :], allow_slow_non_contiguous=True).then_inc(start_stored, 16)
            sp.wait_ge(start_stored, 16)
            sp.dma_start(env.end_of[:, :], env.start_dram[1:NT * P + 1].rearrange("(t p) -> p t", p=P), allow_slow_non_contiguous=True).then_inc(start_loaded, 16)

        @block.gpsimd
        def _(pool):
            nc.gpsimd.iota(env.node_id[:, :], pattern=[[P, NT1]], base=0, channel_multiplier=1).then_inc(iota_done, 1)
            nc.gpsimd.iota(env.part_id[:, :], pattern=[[0, 1]], base=0, channel_multiplier=1).then_inc(iota_done, 1)
            pool.wait_ge(want_l2, 1)
            pool.wait_ge(stored, 64)
            for t in range(NT1):
                pool.indirect_dma_start(out=env.l2_rows[:, t, :], out_offset=None, in_=env.chunk_first_dram,
                                        in_offset=bass.IndirectOffsetOnAxis(ap=env.row_index[:, t:t + 1].bitcast(U32), axis=0),
                                        bounds_check=P - 1, oob_is_err=False).then_inc(got_l2, 16)
            pool.wait_ge(want_l3, 1)
            for t in range(NT1):
                pool.indirect_dma_start(out=env.l3_rows[:, t, :], out_offset=None,
                                        in_=env.sorted_dram[0:E_TOTAL].rearrange("(c f) -> c f", f=P),
                                        in_offset=bass.IndirectOffsetOnAxis(ap=env.chunk_index[:, t:t + 1].bitcast(U32), axis=0),
                                        bounds_check=E_TOTAL // P - 1, oob_is_err=False).then_inc(got_l3, 16)
            pool.wait_ge(want_keys, 1)
            for t in range(NT):
                for side in range(2):
                    pool.indirect_dma_start(out=env.key_rows[:, t, side * SLOTS:(side + 1) * SLOTS], out_offset=None,
                                            in_=env.sorted_dram.rearrange("(c f) -> c f", f=SLOTS),
                                            in_offset=bass.IndirectOffsetOnAxis(ap=env.key_row_index[:, side, t:t + 1].bitcast(U32), axis=0),
                                            bounds_check=E_TOTAL // SLOTS, oob_is_err=False).then_inc(got_keys, 16)
            pool.wait_ge(deg_ready, 1)
            nc.gpsimd.partition_all_reduce(env.deg_max[:, :], env.degree[:, :], P, RMAX).then_inc(maxdeg_done, 1)

        @block.tensor
        def _(pe):
            n = 0
            turns = 0
            for kind, steps, bit, at in plan:
                if kind not in ("to_column", "to_row"):
                    continue
                pe.wait_ge(flipped, turns + 1)
                turns += 1
                for g in range(NBLK // GRP):
                    if n >= 4:
                        pe.wait_ge(evac, n - 3)
                    for b in range(GRP):
                        c = g * GRP + b
                        ins = nc.tensor.transpose(env.bank[n % 4][:, b * P:(b + 1) * P], bufs[at][:, c * P:(c + 1) * P], env.ident[:, :])
                    ins.then_inc(trans, 1)
                    n += 1

        @block.scalar
        def _(act):
            n = 0
            act.wait_ge(sign_ready := env.sign_ready, 1)
            for kind, steps, bit, at in plan:
                if kind not in ("to_column", "to_row"):
                    continue
                for g in range(NBLK // GRP):
                    act.wait_ge(trans, n + 1)
                    dst = bufs[at ^ 1][:, g * GRP * P:(g + 1) * GRP * P]
                    if kind == "to_row" and bit is not None:
                        nc.scalar.activation(dst, env.bank[n % 4][:, :], ACT.Copy, scale=env.sign[:, bit:bit + 1]).then_inc(evac, 1)
                    else:
                        nc.scalar.activation(dst, env.bank[n % 4][:, :], ACT.Copy).then_inc(evac, 1)
                    n += 1

        @block.vector
        def _(dve):
            done = [0]

            def link(ins, count=1):
                done[0] += count
                ins.then_inc(dve_step, count)
                dve.wait_ge(dve_step, done[0])

            dve.wait_ge(iota_done, 2)
            for b in range(7):
                nc.vector.tensor_scalar(env.sign_i[:, b:b + 1], env.part_id[:, :], b, 1, ALU.logical_shift_right, ALU.bitwise_and).then_inc(dve_step, 1)
                done[0] += 1
            dve.wait_ge(dve_step, done[0])
            nc.vector.tensor_scalar(env.sign[:, :], env.sign_i[:, :], -2.0, 1.0, ALU.mult, ALU.add).then_inc(env.sign_ready, 1)
            nc.vector.memset(env.tail_i[:, :], (NODES << SRC_BITS) | KEY_BASE)
            dve.wait_ge(env.sign_ready, 1)
            ai, bi = KA[:, :].bitcast(I32), KB[:, :].bitcast(I32)
            dve.wait_ge(loaded, 32)
            link(nc.vector.tensor_scalar(ai, ai, NODES - 1, None, ALU.min))
            link(nc.vector.tensor_scalar(bi, bi, NODES, None, ALU.min))
            link(nc.vector.tensor_scalar(bi, bi, SRC_BITS, KEY_BASE, ALU.logical_shift_left, ALU.bitwise_or))
            link(nc.vector.tensor_tensor(ai, ai, bi, ALU.bitwise_or))
            turns = 0
            for kind, steps, bit, at in plan:
                if kind in ("row", "column"):
                    for a, b in steps:
                        src, dst = bufs[at], bufs[at ^ 1]
                        if b is None:
                            s = src[:, :].rearrange("p (h x l) -> p h x l", x=2, l=1 << a)
                            d = dst[:, :].rearrange("p (h x l) -> p h x l", x=2, l=1 << a)
                            nc.vector.tensor_tensor(d[:, :, 0, :], s[:, :, 0, :], s[:, :, 1, :], ALU.min).then_inc(dve_step, 1)
                            nc.vector.tensor_tensor(d[:, :, 1, :], s[:, :, 0, :], s[:, :, 1, :], ALU.max).then_inc(dve_step, 1)
                            done[0] += 2
                        else:
                            s, d = free_view(src, a, b), free_view(dst, a, b)
                            for up in (1, 0):
                                nc.vector.tensor_tensor(d(0, up), s(0, up), s(1, up), ALU.min if up else ALU.max).then_inc(dve_step, 1)
                                nc.vector.tensor_tensor(d(1, up), s(0, up), s(1, up), ALU.max if up else ALU.min).then_inc(dve_step, 1)
                            done[0] += 4
                        dve.wait_ge(dve_step, done[0])
                        at ^= 1
                elif kind in ("flip", "unflip"):
                    link(nc.vector.tensor_scalar(bufs[at ^ 1][:, :], bufs[at][:, :], env.sign[:, bit:bit + 1], None, ALU.mult))
                else:
                    dve.nop().then_inc(flipped, 1)
                    turns += 1
                    dve.wait_ge(evac, turns * NBLK // GRP)
            nc.vector.tensor_copy(env.chunk_first[:, :], final[:, ::P]).then_inc(stage_done, 1)
            dve.wait_ge(stage_done, 1)
            nc.vector.tensor_copy(env.tail_keys[:, :].bitcast(I32), env.tail_i[:, :]).then_inc(tail_set, 1)

            link(nc.vector.tensor_scalar(env.node_key[:, :], env.node_id[:, :], SRC_BITS, KEY_BASE, ALU.logical_shift_left, ALU.bitwise_or))
            key = env.node_key[:, :].bitcast(F32)

            def below(rows, width, count):
                cmp = env.search_cmp[:, :, 0:width]
                link(nc.vector.tensor_tensor(cmp, rows, key.unsqueeze(2).to_broadcast([P, NT1, width]), ALU.is_lt))
                link(nc.vector.tensor_reduce(count, cmp, AX.X, ALU.add))

            dve.wait_ge(first_loaded, 16)
            below(env.row_first[:, :].unsqueeze(1).to_broadcast([P, NT1, P]), P, env.cnt[:, :])
            link(nc.vector.tensor_scalar(env.row_f[:, :], env.cnt[:, :], -1.0, 0.0, ALU.add, ALU.max))
            nc.vector.tensor_copy(env.row_index[:, :], env.row_f[:, :]).then_inc(want_l2, 1)
            dve.wait_ge(got_l2, 16 * NT1)
            below(env.l2_rows[:, :, :], NBLK, env.cnt[:, :])
            link(nc.vector.tensor_scalar(env.cnt[:, :], env.cnt[:, :], -1.0, 0.0, ALU.add, ALU.max))
            link(nc.vector.scalar_tensor_tensor(env.row_f[:, :], env.row_f[:, :], float(NBLK), env.cnt[:, :], ALU.mult, ALU.add))
            nc.vector.tensor_copy(env.chunk_index[:, :], env.row_f[:, :]).then_inc(want_l3, 1)
            dve.wait_ge(got_l3, 16 * NT1)
            below(env.l3_rows[:, :, :], P, env.cnt[:, :])
            link(nc.vector.scalar_tensor_tensor(env.start_f[:, :], env.row_f[:, :], float(P), env.cnt[:, :], ALU.mult, ALU.add))
            link(nc.vector.tensor_copy(start_of[:, :], env.start_f[:, :]))
            dve.nop().then_inc(start_ready, 1)

            link(nc.vector.tensor_scalar(env.key_row_index[:, 0, :], start_of[:, 0:NT], SLOT_BITS, None, ALU.logical_shift_right))
            nc.vector.tensor_scalar(env.key_row_index[:, 1, :], env.key_row_index[:, 0, :], 1, None, ALU.add).then_inc(want_keys, 1)
            dve.wait_ge(got_keys, 16 * 2 * NT)
            rows, shift_bit = env.key_rows, env.shift_bit
            for b in range(SLOT_BITS - 1, -1, -1):
                link(nc.vector.tensor_scalar(shift_bit[:, :], start_of[:, 0:NT], b, 1, ALU.logical_shift_right, ALU.bitwise_and))
                w = SLOTS + (1 << b) - 1
                link(nc.vector.tensor_copy(env.shifted[:, :, 0:w], rows[:, :, (1 << b):(1 << b) + w]))
                link(nc.vector.copy_predicated(rows[:, :, 0:w], shift_bit[:, :].unsqueeze(2).to_broadcast([P, NT, w]), env.shifted[:, :, 0:w]))
            keyi = rows[:, :, 0:SLOTS].bitcast(I32)
            dst_i, src_i = env.slot_dst, env.slot_row
            link(nc.vector.tensor_scalar(dst_i[:, :, :], keyi, SRC_BITS, (1 << DST_BITS) - 1, ALU.logical_shift_right, ALU.bitwise_and))
            link(nc.vector.tensor_scalar(src_i[:, :, :], keyi, NODES - 1, None, ALU.bitwise_and))
            link(nc.vector.tensor_tensor(env.slot_penalty[:, :, :], dst_i[:, :, :], env.node_id[:, 0:NT].unsqueeze(2).to_broadcast([P, NT, SLOTS]), ALU.not_equal))
            link(nc.vector.scalar_tensor_tensor(src_i[:, :, :], env.slot_penalty[:, :, :], float(NODES), src_i[:, :, :], ALU.mult, ALU.add))
            link(nc.vector.tensor_scalar(env.slot_penalty[:, :, :], env.slot_penalty[:, :, :], -BIG, None, ALU.mult))
            dve.wait_ge(start_loaded, 16)
            link(nc.vector.tensor_tensor(env.degree[:, :], env.end_of[:, :], start_of[:, 0:NT], ALU.subtract))
            dve.nop().then_inc(deg_ready, 1)
            dve.wait_ge(maxdeg_done, 1)
            link(nc.vector.tensor_scalar(env.tile_groups_f[:, :], env.deg_max[:, :], float(SLOTS), 1.0, ALU.min, ALU.max))
            link(nc.vector.tensor_scalar(env.tile_groups_f[:, :], env.tile_groups_f[:, :], float(SLOT_GROUP - 1), None, ALU.add))
            link(nc.vector.tensor_copy(env.tile_groups[:, :], env.tile_groups_f[:, :]))
            link(nc.vector.tensor_scalar(env.tile_groups[:, :], env.tile_groups[:, :], GROUP_BITS, None, ALU.logical_shift_right))
            link(nc.vector.tensor_scalar(env.tile_groups_f[:, :], env.deg_max[:, :], float(SLOTS - 1), None, ALU.add))
            link(nc.vector.tensor_copy(env.tile_rounds[:, :], env.tile_groups_f[:, :]))
            link(nc.vector.tensor_scalar(env.tile_rounds[:, :], env.tile_rounds[:, :], SLOT_BITS, None, ALU.logical_shift_right))


class Chain:
    def __init__(self, eng, sem, base, per):
        self.eng, self.sem, self.base, self.per, self.n = eng, sem, base, per, 0

    def __call__(self, ins):
        self.n += 1
        ins.then_inc(self.sem, 1)
        self.eng.wait_ge(self.sem, self.base + self.n)

    def end(self):
        assert self.n == self.per, (self.n, self.per)


ROUND_STEPS = 16
ROUNDS_IN = 128
ROUNDS_OUT = E_TOTAL // SLOTS // ROUNDS_IN


def attend(nc, env):
    with ExitStack() as ctx:
        sb = lambda n, s, d: ctx.enter_context(nc.sbuf_tensor(n, s, d))
        sem = lambda n: ctx.enter_context(nc.semaphore(n))
        G = sb("gathered", [P, 2, SLOTS, ROW], F32)
        E = sb("edge_logits", [P, 2, SLOTS + 1, HEADS], F32)
        W = sb("edge_weights", [P, 2, SLOTS + 1, HEADS], F32)
        PR = sb("weighted_rows", [P, SLOTS, HEADS * EXPERTS1], F32)
        mr, mn, ds_, s16 = (sb(n, [P, w], F32) for n, w in (("round_max", HEADS), ("new_max", HEADS), ("round_den", HEADS), ("round_sum", 16)))
        of_row = sb("of_row", [P, 2], I32)
        of_bits = sb("of_bits", [P, SLOT_BITS], I32)
        of_keys = sb("of_keys", [P, 2 * SLOTS], F32)
        of_tmp = sb("of_shifted", [P, 2 * SLOTS], F32)
        of_slot, of_pen = sb("of_slot_row", [P, SLOTS], I32), sb("of_penalty", [P, SLOTS], F32)
        of_dst = sb("of_dst", [P, SLOTS], I32)
        rows_in = [sem("rows_in_0"), sem("rows_in_1")]
        rows_used = [sem("rows_used_0"), sem("rows_used_1")]
        turn = sem("pool_turn")
        cleared, began, step, logits, weights = sem("gathered_cleared"), sem("state_ready"), sem("attend_step"), sem("logits_ready"), sem("weights_ready")
        of_index, of_keys_in, of_slots, of_rows_in = sem("of_index_ready"), sem("of_keys_in"), sem("of_slots_ready"), sem("of_rows_in")
        of_dma, of_step, of_logits, of_weights, of_done = sem("of_dma"), sem("of_step"), sem("of_logits_ready"), sem("of_weights_ready"), sem("of_round_done")
        block = ctx.enter_context(nc.Block())
        M, DEN, ACC = env.att_max, env.att_den, env.att_acc

        def gather(pool, dst, index, s):
            pool.indirect_dma_start(out=dst, out_offset=None, in_=env.table_dram,
                                    in_offset=bass.IndirectOffsetOnAxis(ap=index, axis=0),
                                    bounds_check=NODES - 1, oob_is_err=False).then_inc(s, 16)

        @block.gpsimd
        def _(pool):
            nc.gpsimd.memset(G[:, :, :, :], 0.0).then_inc(cleared, 1)
            pool.wait_ge(cleared, 1)
            with pool.Fori(0, NT // 2) as i:
                for u in range(2):
                    t = i * 2 + u
                    pool.wait_ge(rows_used[u], i + 1)
                    pool.sem_inc(turn, 1)
                    n = pool.value_load(env.tile_groups[0:1, bass.ds(t, 1)], min_val=0, max_val=SLOTS // SLOT_GROUP)
                    nc.gpsimd.tensor_copy(env.idx_now[:, u, :], env.slot_row[:, bass.ds(t, 1), :].rearrange("p o s -> p (o s)")).then_inc(env.idx_sem, 1)
                    pool.wait_ge(env.idx_sem, i * 2 + (u + 1))
                    pool.sem_inc(turn, 1)
                    for q in range(SLOTS // SLOT_GROUP):
                        with pool.If(n > q):
                            for j in range(q * SLOT_GROUP, (q + 1) * SLOT_GROUP):
                                gather(pool, G[:, u, j, :], env.idx_now[:, u, j:j + 1].bitcast(U32), rows_in[u])
            with pool.Fori(0, NT) as t:
                n = pool.value_load(env.tile_rounds[0:1, bass.ds(t, 1)], min_val=0, max_val=E_TOTAL // SLOTS)
                before = pool.value_load(env.rounds_before[0:1, bass.ds(t, 1)], min_val=0, max_val=E_TOTAL // SLOTS)
                with pool.If(n > 1):
                    with pool.Fori(0, ROUNDS_OUT) as ro:
                      with pool.If(n > ro * ROUNDS_IN + 1):
                       with pool.Fori(0, ROUNDS_IN) as ri:
                        r = ro * ROUNDS_IN + ri + 1
                        with pool.If(n > r):
                            c = before + r
                            pool.wait_ge(of_index, c)
                            pool.sem_inc(turn, 1)
                            for side in range(2):
                                pool.indirect_dma_start(out=of_keys[:, side * SLOTS:(side + 1) * SLOTS], out_offset=None,
                                                        in_=env.sorted_dram.rearrange("(c f) -> c f", f=SLOTS),
                                                        in_offset=bass.IndirectOffsetOnAxis(ap=of_row[:, side:side + 1].bitcast(U32), axis=0),
                                                        bounds_check=E_TOTAL // SLOTS, oob_is_err=False).then_inc(of_dma, 16)
                            pool.wait_ge(of_dma, 32)
                            pool.dma_reset(range(of_dma.num, of_dma.num + 1))
                            pool.sem_clear(of_dma)
                            pool.sem_inc(of_keys_in, 1)
                            pool.wait_ge(of_slots, c)
                            pool.sem_inc(turn, 1)
                            for j in range(SLOTS):
                                gather(pool, G[:, 0, j, :], of_slot[:, j:j + 1].bitcast(U32), of_dma)
                            pool.wait_ge(of_dma, 16 * SLOTS)
                            pool.dma_reset(range(of_dma.num, of_dma.num + 1))
                            pool.sem_clear(of_dma)
                            pool.sem_inc(of_rows_in, 1)

        @block.scalar
        def _(act):
            with act.Fori(0, NT // 2) as i:
                for u in range(2):
                    act.wait_ge(logits, i * 2 + (u + 1))
                    nc.scalar.activation(W[:, u, :, :], E[:, u, :, :], ACT.Exp).then_inc(weights, 1)
            with act.Fori(0, NT) as t:
                n = act.value_load(env.tile_rounds[0:1, bass.ds(t, 1)], min_val=0, max_val=E_TOTAL // SLOTS)
                before = act.value_load(env.rounds_before[0:1, bass.ds(t, 1)], min_val=0, max_val=E_TOTAL // SLOTS)
                with act.If(n > 1):
                    with act.Fori(0, ROUNDS_OUT) as ro:
                      with act.If(n > ro * ROUNDS_IN + 1):
                       with act.Fori(0, ROUNDS_IN) as ri:
                        r = ro * ROUNDS_IN + ri + 1
                        with act.If(n > r):
                            act.wait_ge(of_logits, before + r)
                            nc.scalar.activation(W[:, 0, :, :], E[:, 0, :, :], ACT.Exp).then_inc(of_weights, 1)

        @block.vector
        def _(dve):
            setup = Chain(dve, began, 0, 12)
            own = env.own_rows
            setup(nc.vector.tensor_tensor(M[:, :, :], own[:, :, 16:ROW], env.a_dst[:, :, :], ALU.add))
            setup(nc.vector.scalar_tensor_tensor(M[:, :, :], M[:, :, :], SLOPE, M[:, :, :], ALU.mult, ALU.max))
            setup(nc.vector.memset(DEN[:, :, :], 1.0))
            setup(nc.vector.tensor_copy(ACC[:, :, :], own[:, :, 0:16]))
            setup(nc.vector.tensor_scalar(env.rounds_f[:, :], env.tile_rounds[:, :], -1.0, 0.0, ALU.add, ALU.max))
            setup(nc.vector.tensor_tensor_scan(env.rounds_f2[:, 1:NT + 1], env.ones_nt[:, :], env.rounds_f[:, :], 0.0, ALU.mult, ALU.add))
            setup(nc.vector.tensor_copy(env.rounds_before[:, 1:NT], env.rounds_f2[:, 1:NT]))
            groups = env.tile_groups[:, :].rearrange("p (i u) -> p u i", u=2)
            for u in range(2):
                setup(nc.vector.tensor_scalar(env.groups_f[:, u, :], groups[:, u, :], float(16 * SLOT_GROUP), None, ALU.mult))
                setup(nc.vector.tensor_tensor_scan(env.groups_sum[:, u, :], env.ones_nt[:, 0:NT // 2], env.groups_f[:, u, :], 0.0, ALU.mult, ALU.add))
            setup(nc.vector.tensor_copy(env.rows_due[:, :, :], env.groups_sum[:, :, :]))
            setup.end()

            def weigh(link, t, u, penalty, slots_sem, slots_count, logits_sem, weights_sem, count):
                g, e, w = G[:, u, :, :], E[:, u, 0:SLOTS, :], W[:, u, 0:SLOTS, :]
                m, den, acc = M[:, bass.ds(t, 1), :], DEN[:, bass.ds(t, 1), :], ACC[:, bass.ds(t, 1), :]
                m, den, acc = (v.rearrange("p o h -> p (o h)") for v in (m, den, acc))
                ad = env.a_dst[:, bass.ds(t, 1), :].to_broadcast([P, SLOTS, HEADS])
                dve.wait_ge(slots_sem, slots_count)
                link(nc.vector.tensor_tensor(e, g[:, :, 16:ROW], ad, ALU.add))
                link(nc.vector.tensor_tensor(e, e, penalty.unsqueeze(2).to_broadcast([P, SLOTS, HEADS]), ALU.add))
                link(nc.vector.scalar_tensor_tensor(e, e, SLOPE, e, ALU.mult, ALU.max))
                link(nc.vector.tensor_reduce(mr[:, :], e.rearrange("p j h -> p h j"), AX.X, ALU.max))
                link(nc.vector.tensor_tensor(mn[:, :], m, mr[:, :], ALU.max))
                link(nc.vector.tensor_tensor(E[:, u, SLOTS, :], m, mn[:, :], ALU.subtract))
                link(nc.vector.tensor_tensor(m, m, mr[:, :], ALU.max))
                nc.vector.tensor_tensor(e, e, mn[:, :].unsqueeze(1).to_broadcast([P, SLOTS, HEADS]), ALU.subtract).then_inc(logits_sem, 1)
                dve.wait_ge(weights_sem, count)
                fade = W[:, u, SLOTS, :]
                link(nc.vector.tensor_reduce(ds_[:, :], w.rearrange("p j h -> p h j"), AX.X, ALU.add))
                link(nc.vector.tensor_tensor(den, den, fade, ALU.mult))
                link(nc.vector.tensor_tensor(den, den, ds_[:, :], ALU.add))
                link(nc.vector.tensor_tensor(PR[:, :, :].rearrange("p j (h x) -> p j h x", x=EXPERTS1),
                                             g[:, :, 0:16].rearrange("p j (h x) -> p j h x", x=EXPERTS1),
                                             w.unsqueeze(3).to_broadcast([P, SLOTS, HEADS, EXPERTS1]), ALU.mult))
                link(nc.vector.tensor_reduce(s16[:, :], PR[:, :, :].rearrange("p j f -> p f j"), AX.X, ALU.add))
                av = acc.rearrange("p (h x) -> p h x", x=EXPERTS1)
                link(nc.vector.tensor_tensor(av, av, fade.unsqueeze(2).to_broadcast([P, HEADS, EXPERTS1]), ALU.mult))
                link(nc.vector.tensor_tensor(acc, acc, s16[:, :], ALU.add))

            dve.wait_ge(cleared, 1)
            for u in range(2):
                nc.vector.nop().then_inc(rows_used[u], 1)
            with dve.Fori(0, NT // 2) as i:
                for u in range(2):
                    t = i * 2 + u
                    link = Chain(dve, step, i * (2 * ROUND_STEPS) + u * ROUND_STEPS, ROUND_STEPS)
                    pen = env.slot_penalty[:, bass.ds(t, 1), :].rearrange("p o s -> p (o s)")
                    due = dve.value_load(env.rows_due[0:1, u, bass.ds(i, 1)], min_val=16 * SLOT_GROUP, max_val=16 * SLOTS * NT // 2)
                    weigh(link, t, u, pen, rows_in[u], due, logits, weights, i * 2 + (u + 1))
                    link(dve.nop())
                    nc.vector.nop().then_inc(rows_used[u], 1)
                    link(dve.nop())
                    link.end()
            with dve.Fori(0, NT) as t:
                n = dve.value_load(env.tile_rounds[0:1, bass.ds(t, 1)], min_val=0, max_val=E_TOTAL // SLOTS)
                before = dve.value_load(env.rounds_before[0:1, bass.ds(t, 1)], min_val=0, max_val=E_TOTAL // SLOTS)
                with dve.If(n > 1):
                    link = Chain(dve, of_step, 0, SLOT_BITS + 2)
                    start = env.start_of[:, bass.ds(t, 1)]
                    for b in range(SLOT_BITS):
                        link(nc.vector.tensor_scalar(of_bits[:, b:b + 1], start, b, 1, ALU.logical_shift_right, ALU.bitwise_and))
                    link(nc.vector.tensor_scalar(of_row[:, 0:1], start, SLOT_BITS, None, ALU.logical_shift_right))
                    link(nc.vector.tensor_scalar(of_row[:, 1:2], of_row[:, 0:1], 1, None, ALU.add))
                    link.end()
                    dve.sem_clear(of_step)
                    with dve.Fori(0, ROUNDS_OUT) as ro:
                      with dve.If(n > ro * ROUNDS_IN + 1):
                       with dve.Fori(0, ROUNDS_IN) as ri:
                        r = ro * ROUNDS_IN + ri + 1
                        with dve.If(n > r):
                            c = before + r
                            link = Chain(dve, of_step, 0, 37 + 0)
                            nc.vector.tensor_scalar(of_row[:, :], of_row[:, :], 1.0, float(E_TOTAL // SLOTS), ALU.add, ALU.min).then_inc(of_index, 1)
                            dve.wait_ge(of_keys_in, c)
                            for b in range(SLOT_BITS - 1, -1, -1):
                                w = SLOTS + (1 << b) - 1
                                link(nc.vector.tensor_copy(of_tmp[:, 0:w], of_keys[:, (1 << b):(1 << b) + w]))
                                link(nc.vector.copy_predicated(of_keys[:, 0:w], of_bits[:, b:b + 1].to_broadcast([P, w]), of_tmp[:, 0:w]))
                            ki = of_keys[:, 0:SLOTS].bitcast(I32)
                            link(nc.vector.tensor_scalar(of_dst[:, :], ki, SRC_BITS, (1 << DST_BITS) - 1, ALU.logical_shift_right, ALU.bitwise_and))
                            link(nc.vector.tensor_scalar(of_slot[:, :], ki, NODES - 1, None, ALU.bitwise_and))
                            link(nc.vector.tensor_tensor(of_pen[:, :], of_dst[:, :], env.node_id[:, bass.ds(t, 1)].to_broadcast([P, SLOTS]), ALU.not_equal))
                            link(nc.vector.scalar_tensor_tensor(of_slot[:, :], of_pen[:, :], float(NODES), of_slot[:, :], ALU.mult, ALU.add))
                            link(nc.vector.tensor_scalar(of_pen[:, :], of_pen[:, :], -BIG, None, ALU.mult))
                            dve.sem_inc(of_slots, 1)
                            weigh(link, t, 0, of_pen[:, :], of_rows_in, c, of_logits, of_weights, c)
                            link.per = link.n
                            link.end()
                            dve.sem_clear(of_step)
            fin = Chain(dve, env.att_fin, 0, 4)
            fin(nc.vector.tensor_scalar(DEN[:, :, :], DEN[:, :, :], 1e-16, None, ALU.add))
            fin(nc.vector.reciprocal(DEN[:, :, :], DEN[:, :, :]))
            a4 = ACC[:, :, :].rearrange("p t (h x) -> p (t h) x", x=EXPERTS1)
            fin(nc.vector.tensor_tensor(a4, a4, DEN[:, :, :].rearrange("p t h -> p (t h)").unsqueeze(2).to_broadcast([P, NT * HEADS, EXPERTS1]), ALU.mult))
            fin(nc.vector.tensor_tensor(ACC[:, :, :], ACC[:, :, :], env.b_gat[:, :].unsqueeze(1).to_broadcast([P, NT, 16]), ALU.add))


class Steps:
    def __init__(self, eng, done, names):
        self.done, self.names, self.next, self.eng = done, list(names), 0, eng
        self.index = {n: k for k, n in enumerate(self.names)}
        assert len(self.index) == len(self.names)
        self.per = len(self.names)

    def begin(self, eng):
        eng.sem_inc(self.done, self.per)

    def did(self, ins, name):
        assert self.names[self.next % self.per] == name, (self.names[self.next % self.per], name)
        self.next += 1
        ins.then_inc(self.done, 1)

    def count(self, name, i):
        return i * self.per + (self.per + self.index[name] + 1)


class Link:
    def __init__(self, eng, sem, i, per):
        self.eng, self.sem, self.base, self.per, self.n = eng, sem, i * per, per, 0

    def __call__(self, ins):
        self.n += 1
        ins.then_inc(self.sem, 1)
        self.eng.wait_ge(self.sem, self.base + self.n)

    def end(self):
        self.eng.sem_inc(self.sem, self.per - self.n)
        self.eng.wait_ge(self.sem, self.base + self.per)


class Norms:
    def __init__(self, nc, env, ready, done, per):
        self.nc, self.env, self.ready, self.done, self.per, self.k, self.i = nc, env, ready, done, per, 0, 0

    def invert(self, dve, ins):
        self.k += 1
        ins.then_inc(self.ready, 1)
        dve.wait_ge(self.done, self.i * self.per + self.k)

    def serve(self, pool, i):
        for k in range(self.per):
            pool.wait_ge(self.ready, i * self.per + (k + 1))
            self.nc.gpsimd.tensor_tensor(self.env.ln_rstd[:, :], self.env.ln_var[:, :], self.env.minus_half[:, 0:GT], ALU.pow).then_inc(self.done, 1)


def bcast(ap, shape, axis):
    return ap.unsqueeze(axis).to_broadcast(shape)


def layer_norm(nc, env, link, x, out, scale_shift=None):
    st, mv = env.ln_stats, env.ln_mv
    for j in range(GT):
        ins = nc.vector.bn_stats(st[:, j, :], x[:, j, :])
    link(ins)
    link.eng.sem_inc(env.pause, 1)
    for j in range(GT):
        ins = nc.vector.bn_aggr(mv[:, j, :], st[:, j, :])
    link(ins)
    env.norms.invert(link.eng, nc.vector.tensor_scalar(env.ln_var[:, :], mv[:, :, 1], LN_EPS, None, ALU.add))
    for j in range(GT):
        ins = nc.vector.tensor_scalar(out[:, j, :], x[:, j, :], mv[:, j, 0:1], env.ln_rstd[:, j:j + 1], ALU.subtract, ALU.mult)
    if scale_shift is not None:
        link(ins)
        link(nc.vector.tensor_tensor(out, out, bcast(scale_shift[0], [P, GT, D], 1), ALU.mult))
        ins = nc.vector.tensor_tensor(out, out, bcast(scale_shift[1], [P, GT, D], 1), ALU.add)
    return ins


def top_two(nc, env, link, scores, n, tiles, tmp):
    shape = [P, tiles, n]
    full = lambda t: t[:, 0:tiles, 0:n]
    one = lambda t: t[:, 0:tiles]

    def mark(vals, top, where):
        link(nc.vector.tensor_reduce(one(top), vals, AX.X, ALU.max))
        link(nc.vector.tensor_tensor(full(tmp.tie), vals, bcast(one(top), shape, 2), ALU.is_equal))
        link(nc.vector.tensor_tensor(full(tmp.tie), full(tmp.tie), bcast(env.earlier[:, 0:n], shape, 1), ALU.mult))
        link(nc.vector.tensor_reduce(one(tmp.best), full(tmp.tie), AX.X, ALU.max))
        link(nc.vector.tensor_tensor(full(where), full(tmp.tie), bcast(one(tmp.best), shape, 2), ALU.is_equal))

    mark(scores, tmp.max1, tmp.first)
    link(nc.vector.scalar_tensor_tensor(full(tmp.rest), full(tmp.first), -BIG, scores, ALU.mult, ALU.add))
    mark(full(tmp.rest), tmp.max2, tmp.second)
    return nc.vector.tensor_tensor(one(tmp.diff), one(tmp.max2), one(tmp.max1), ALU.subtract)


def gate_weights(nc, link, out, n, tiles, tmp):
    shape = [P, tiles, n]
    full = lambda t: t[:, 0:tiles, 0:n]
    one = lambda t: t[:, 0:tiles]
    link(nc.vector.tensor_scalar(one(tmp.w1), one(tmp.diff_exp), 1.0, None, ALU.add))
    link(nc.vector.reciprocal(one(tmp.w1), one(tmp.w1)))
    link(nc.vector.tensor_tensor(one(tmp.w2), one(tmp.diff_exp), one(tmp.w1), ALU.mult))
    link(nc.vector.tensor_tensor(full(tmp.first), full(tmp.first), bcast(one(tmp.w1), shape, 2), ALU.mult))
    link(nc.vector.tensor_tensor(full(tmp.second), full(tmp.second), bcast(one(tmp.w2), shape, 2), ALU.mult))
    return nc.vector.tensor_tensor(out, full(tmp.first), full(tmp.second), ALU.add)


def turn(nc, bank, src, ident, n=P):
    for j in range(GT):
        ins = nc.tensor.transpose(bank[0:n, j * P:(j + 1) * P], src[:, j, 0:n], ident[:, :])
    return ins


def copy(nc, out, in_):
    return nc.vector.tensor_scalar(out, in_, 1.0, None, ALU.mult)


def tiles_of(ap):
    return ap.rearrange("p (j n) -> p j n", j=GT)


def phase_a(nc, env):
    N0 = EXPERTS0
    tensor_names = (["adjT", "l0agg", "l0out", "xt1", "rh", "lg"]
                    + [s for t in range(N0 + 2) for s in ([f"u1_{t}"] if t < N0 else []) + ([f"u2_{t-1}"] if 0 < t <= N0 else []) + ([f"y_{t-2}"] if t >= 2 else [])]
                    + ["gt", "gb", "xt2", "c1", "se", "dist", "sqm", "msg", "c2", "nmp", "ghn", "r", "z", "gin", "ot", "xt3", "hh"])
    scalar_names = (["adjT", "l0agg", "xt1", "rh", "l0exp", "g0exp"]
                    + [s for t in range(N0 + 1) for s in ([f"h1_{t}"] if t < N0 else []) + ([f"h2_{t-1}"] if t > 0 else [])]
                    + ["gt", "xt2", "se", "se2", "sq", "c1", "nsq", "ex", "ms", "nmp", "xc", "r", "z", "nn", "xt3"])
    vector_names = ["xh0", "l0out", "xh1", "lg", "probs_in", "g0diff", "gate"] + [f"comb_{e}" for e in range(N0)] + ["gb", "xh2", "att", "cv", "t1", "o", "ot", "xh3", "rows"]
    LINKS = 128

    with ExitStack() as ctx:
        sb = lambda n, s: ctx.enter_context(nc.sbuf_tensor("a_" + n, s, F32))
        sem = lambda n: ctx.enter_context(nc.semaphore("a_" + n))
        ten, sca, vec = (Steps(None, sem(n), s) for n, s in (("tensor_step", tensor_names), ("scalar_step", scalar_names), ("vector_step", vector_names)))
        link_sem, adj_in, rows_out, margins = sem("vector_link"), sem("adj_loaded"), sem("rows_stored"), sem("margins_cleared")
        X, XH, ADJ, ADJT = (sb(n, [P, GT, D]) for n in ("x", "xh", "adj", "adjt"))
        AG, XT, CV, XC, NMP, R, Z, NN, O, T1 = (sb(n, [P, GT * P]) for n in ("ag", "xt", "cv", "xc", "nmp", "r", "z", "nn", "o", "t1"))
        U, EX, MS = (sb(n, [P, GT, D]) for n in ("u", "ex", "ms"))
        H1 = [sb(f"h1_{k}", [P, GT * P]) for k in range(2)]
        H2 = [sb(f"h2_{k}", [P, GT * P]) for k in range(2)]
        RH = sb("rh", [ROUTER_H, GT * P])
        GTR = sb("gate_rows", [N0, GT * P])
        LG, PB, GATE = (sb(n, [P, GT, N0]) for n in ("lg", "pb", "gate"))
        lsum = sb("lsum", [P, GT])
        H1P = sb("h1p", [P, GT, P + 2 * CONV_PAD])
        SE, SE2, SQ = (sb(n, [3, GT * P]) for n in ("se", "se2", "sq"))
        NSQ = sb("nsq", [P, GT])
        ROWL = sb("rows", [P, GT, ROW])
        ADL, PROD = sb("adl", [P, GT, HEADS]), sb("prod", [P, GT, 16])
        B = env.bank
        U1, U2, Y = (B[1], B[2]), (B[3], B[4]), (B[5], B[6])
        env.norms = norms = Norms(nc, env, sem("var_ready"), sem("rstd_ready"), 4)
        block = ctx.enter_context(nc.Block())
        adj_v = env.adj_dram

        @block.sync
        def _(sp):
            with sp.Fori(0, GROUPS) as i:
                sp.wait_ge(ten.done, ten.count("adjT", i - 1))
                sp.dma_start(ADJ[:, :, :], adj_v[bass.ds(i * GT, GT), :, :].rearrange("g n m -> n g m")).then_inc(adj_in, 16)
                sp.wait_ge(vec.done, vec.count("rows", i))
                sp.dma_start(env.table_dram[bass.ds(i * (GT * P), GT * P), :].rearrange("(t p) f -> p t f", p=P), ROWL[:, :, :]).then_inc(rows_out, 16)
            sp.wait_ge(rows_out, 16 * GROUPS)

        @block.gpsimd
        def _(pool):
            with pool.Fori(0, GROUPS) as i:
                norms.serve(pool, i)

        @block.tensor
        def _(pe):
            ten.begin(pe)
            mm = nc.tensor.matmul
            with pe.Fori(0, GROUPS) as i:
                after = lambda who, name: pe.wait_ge(who.done, who.count(name, i))
                pe.wait_ge(adj_in, i * 16 + 16)
                pe.wait_ge(sca.done, sca.count("xt3", i - 1))
                ten.did(turn(nc, B[0], ADJ, env.ident), "adjT")
                after(vec, "xh0")
                after(sca, "adjT")
                for j in range(GT):
                    ins = mm(B[1][:, j * P:(j + 1) * P], lhsT=XH[:, j, :], rhs=ADJT[:, j, :], start=j == 0, stop=j == GT - 1, skip_group_check=True)
                ten.did(ins, "l0agg")
                after(sca, "l0agg")
                for j in range(GT):
                    o = B[2][:, j * P:(j + 1) * P]
                    mm(o, lhsT=AG[:, j * P:(j + 1) * P], rhs=env.w("l0_w"), start=j == 0, stop=False, skip_group_check=True)
                    ins = mm(o, lhsT=env.ones[0:1, :], rhs=env.row("l0_bias"), start=False, stop=j == GT - 1, skip_group_check=True)
                ten.did(ins, "l0out")
                after(vec, "xh1")
                ten.did(turn(nc, B[0], XH, env.ident), "xt1")
                after(sca, "xt1")
                ten.did(mm(B[7][0:ROUTER_H, :], lhsT=env.w("rw1"), rhs=XT[:, :], start=True, stop=True), "rh")
                after(sca, "rh")
                for j in range(GT):
                    o = B[0][:, j * N0:(j + 1) * N0]
                    mm(o, lhsT=RH[:, j * P:(j + 1) * P], rhs=env.rw2[:, :], start=j == 0, stop=False, skip_group_check=True)
                    ins = mm(o, lhsT=env.ones[0:1, :], rhs=env.row("rb2"), start=False, stop=j == GT - 1, skip_group_check=True)
                ten.did(ins, "lg")
                for t in range(N0 + 2):
                    if t < N0:
                        if t >= 2:
                            after(sca, f"h1_{t-2}")
                        ten.did(mm(U1[t % 2][:, :], lhsT=env.w("ew1", t), rhs=XT[:, :], start=True, stop=True), f"u1_{t}")
                    if 0 < t <= N0:
                        after(sca, f"h1_{t-1}")
                        if t >= 3:
                            after(sca, f"h2_{t-3}")
                        ten.did(mm(U2[(t - 1) % 2][:, :], lhsT=env.w("ew2", t - 1), rhs=H1[(t - 1) % 2][:, :], start=True, stop=True), f"u2_{t-1}")
                    if t >= 2:
                        e = t - 2
                        after(sca, f"h2_{e}")
                        if e >= 2:
                            after(vec, f"comb_{e-2}")
                        for j in range(GT):
                            ins = mm(Y[e % 2][:, j * P:(j + 1) * P], lhsT=H2[e % 2][:, j * P:(j + 1) * P], rhs=env.w("ew3", e), start=j == 0, stop=j == GT - 1, skip_group_check=True)
                        ten.did(ins, f"y_{e}")
                after(vec, "gate")
                ten.did(turn(nc, B[7], GATE, env.ident, N0), "gt")
                after(sca, "gt")
                for j in range(GT):
                    ins = mm(B[0][:, j * P:(j + 1) * P], lhsT=GTR[:, j * P:(j + 1) * P], rhs=env.eb3[:, :], start=j == 0, stop=j == GT - 1, skip_group_check=True)
                ten.did(ins, "gb")
                after(vec, "xh2")
                ten.did(turn(nc, B[0], XH, env.ident), "xt2")
                after(sca, "xt2")
                ten.did(mm(B[1][:, :], lhsT=env.w("conv1"), rhs=XT[:, :], start=True, stop=True), "c1")
                ten.did(mm(B[7][0:3, :], lhsT=env.w("w_se"), rhs=XT[:, :], start=True, stop=True), "se")
                after(sca, "sq")
                for j in range(GT):
                    o, s = B[6][:, j * P:(j + 1) * P], slice(j * P, (j + 1) * P)
                    mm(o, lhsT=SE[:, s], rhs=SE2[:, s], start=j == 0, stop=False, skip_group_check=True)
                    ins = mm(o, lhsT=env.neg_ones[:, :], rhs=SQ[:, s], start=False, stop=j == GT - 1, skip_group_check=True)
                ten.did(ins, "dist")
                for j in range(GT):
                    ins = mm(B[7][:, j:j + 1], lhsT=SQ[:, j * P:(j + 1) * P], rhs=env.neg_ones[:, 0:1], start=j == 0, stop=j == GT - 1, skip_group_check=True)
                ten.did(ins, "sqm")
                for j in range(GT):
                    o = B[5][:, j * P:(j + 1) * P]
                    mm(o, lhsT=XT[:, j * P:(j + 1) * P], rhs=env.w("w_msg"), start=j == 0, stop=False, skip_group_check=True)
                    ins = mm(o, lhsT=env.ones[0:1, :], rhs=env.row("b_msg"), start=False, stop=j == GT - 1, skip_group_check=True)
                ten.did(ins, "msg")
                after(sca, "c1")
                for k in range(CONV_K):
                    ins = mm(tiles_of(B[2][:, :]), lhsT=env.w("conv2", k), rhs=H1P[:, :, k:k + P], start=k == 0, stop=k == CONV_K - 1)
                ten.did(ins, "c2")
                after(sca, "ms")
                after(vec, "att")
                for j in range(GT):
                    ins = mm(B[4][:, j * P:(j + 1) * P], lhsT=MS[:, j, :], rhs=EX[:, j, :], start=j == 0, stop=j == GT - 1, skip_group_check=True)
                ten.did(ins, "nmp")
                ten.did(mm(B[6][:, :], lhsT=env.w("w_hh", 2), rhs=XT[:, :], start=True, stop=True), "ghn")
                after(sca, "nmp")
                after(sca, "xc")
                for gate, bank in ((0, B[3]), (1, B[1]), (2, B[5])):
                    if gate < 2:
                        mm(bank[:, :], lhsT=env.w("w_hh", gate), rhs=XT[:, :], start=True, stop=False)
                    mm(bank[:, :], lhsT=env.w("w_ih", 3 + gate), rhs=NMP[:, :], start=gate == 2, stop=False)
                    ins = mm(bank[:, :], lhsT=env.w("w_ih", gate), rhs=XC[:, :], start=False, stop=True)
                    ten.did(ins, ("r", "z", "gin")[gate])
                after(vec, "o")
                ten.did(turn(nc, B[0], tiles_of(O[:, :]), env.ident), "ot")
                after(vec, "xh3")
                ten.did(turn(nc, B[0], XH, env.ident), "xt3")
                after(sca, "xt3")
                for j in range(GT):
                    ins = mm(B[7][:, j * 16:(j + 1) * 16], lhsT=XT[:, j * P:(j + 1) * P], rhs=env.w("w_gat"), start=j == 0, stop=j == GT - 1, skip_group_check=True)
                ten.did(ins, "hh")

        @block.scalar
        def _(act):
            act.wait_ge(margins, 1)
            sca.begin(act)
            go = nc.scalar.activation
            with act.Fori(0, GROUPS) as i:
                after = lambda who, name: act.wait_ge(who.done, who.count(name, i))
                after(ten, "adjT")
                act.wait_ge(vec.done, vec.count("att", i - 1))
                sca.did(go(ADJT[:, :, :], tiles_of(B[0][:, :]), ACT.Copy), "adjT")
                after(ten, "l0agg")
                sca.did(go(AG[:, :], B[1][:, :], ACT.Copy), "l0agg")
                after(ten, "xt1")
                sca.did(go(XT[:, :], B[0][:, :], ACT.Copy), "xt1")
                after(ten, "rh")
                sca.did(go(RH[:, :], B[7][0:ROUTER_H, :], ACT.Relu, bias=env.col("rb1")[0:ROUTER_H, :]), "rh")
                after(vec, "lg")
                sca.did(go(PB[:, :, :], LG[:, :, :], ACT.Exp), "l0exp")
                after(vec, "g0diff")
                sca.did(go(env.top.diff_exp[:, 0:GT], env.top.diff[:, 0:GT], ACT.Exp), "g0exp")
                for t in range(N0 + 1):
                    if t < N0:
                        after(ten, f"u1_{t}")
                        if t >= 2:
                            after(ten, f"u2_{t-2}")
                        sca.did(go(H1[t % 2][:, :], U1[t % 2][:, :], ACT.Relu, bias=env.col("eb1", t)), f"h1_{t}")
                    if t > 0:
                        after(ten, f"u2_{t-1}")
                        if t >= 3:
                            after(ten, f"y_{t-3}")
                        sca.did(go(H2[(t - 1) % 2][:, :], U2[(t - 1) % 2][:, :], ACT.Relu, bias=env.col("eb2", t - 1)), f"h2_{t-1}")
                after(ten, "gt")
                sca.did(go(GTR[:, :], B[7][0:N0, :], ACT.Copy), "gt")
                after(ten, "xt2")
                sca.did(go(XT[:, :], B[0][:, :], ACT.Copy), "xt2")
                after(ten, "se")
                sca.did(go(SE[:, :], B[7][0:3, :], ACT.Identity, bias=env.col("b_se")[0:3, :]), "se")
                act.wait_ge(sca.done, sca.count("se", i))
                sca.did(go(SE2[:, :], SE[:, :], ACT.Copy, scale=2.0), "se2")
                sca.did(go(SQ[:, :], SE[:, :], ACT.Square), "sq")
                sca.did(go(H1P[:, :, CONV_PAD:CONV_PAD + P], tiles_of(B[1][:, :]), ACT.Relu, bias=env.bn_shift[:, 0:1], scale=env.bn_scale[:, 0:1]), "c1")
                after(ten, "sqm")
                sca.did(go(NSQ[:, :], B[7][:, 0:GT], ACT.Copy), "nsq")
                act.wait_ge(sca.done, sca.count("nsq", i))
                for j in range(GT):
                    ins = go(EX[:, j, :], B[6][:, j * P:(j + 1) * P], ACT.Exp, bias=NSQ[:, j:j + 1])
                sca.did(ins, "ex")
                after(ten, "msg")
                sca.did(go(MS[:, :, :], tiles_of(B[5][:, :]), ACT.Relu), "ms")
                after(ten, "nmp")
                sca.did(go(NMP[:, :], B[4][:, :], ACT.Copy), "nmp")
                after(vec, "cv")
                sca.did(go(XC[:, :], CV[:, :], ACT.Relu, bias=env.bn_shift[:, 1:2]), "xc")
                after(ten, "r")
                sca.did(go(R[:, :], B[3][:, :], ACT.Tanh, bias=env.gru_bias[:, 0:1], scale=0.5), "r")
                after(ten, "z")
                sca.did(go(Z[:, :], B[1][:, :], ACT.Tanh, bias=env.gru_bias[:, 1:2], scale=0.5), "z")
                after(vec, "t1")
                sca.did(go(NN[:, :], T1[:, :], ACT.Tanh, bias=env.col("b_ih", 2)), "nn")
                after(ten, "xt3")
                sca.did(go(XT[:, :], B[0][:, :], ACT.Copy), "xt3")

        @block.vector
        def _(dve):
            v = nc.vector
            v.memset(H1P[:, :, :], 0.0).then_inc(margins, 1)
            dve.wait_ge(margins, 1)
            vec.begin(dve)
            with dve.Fori(0, GROUPS) as i:
                link = Link(dve, link_sem, i, LINKS)
                norms.i = i
                after = lambda who, name: dve.wait_ge(who.done, who.count(name, i))

                def did(ins, name):
                    vec.did(ins, name)
                    dve.wait_ge(vec.done, vec.count(name, i))

                tiles = bass.ds(i * GT, GT)
                link(copy(nc, X[:, :, :], env.x[:, tiles, :]))
                did(layer_norm(nc, env, link, X, XH[:, :, :]), "xh0")
                after(ten, "l0out")
                bank = tiles_of(B[2][:, :])
                link(v.tensor_scalar(U[:, :, :], bank, 0.0, env.prelu[:, :], ALU.min, ALU.mult))
                did(v.scalar_tensor_tensor(U[:, :, :], bank, 0.0, U[:, :, :], ALU.max, ALU.add), "l0out")
                link(v.tensor_tensor(X[:, :, :], X[:, :, :], U[:, :, :], ALU.add))
                did(layer_norm(nc, env, link, X, XH[:, :, :]), "xh1")
                after(ten, "lg")
                lg = B[0][:, 0:GT * N0].rearrange("p (j e) -> p j e", j=GT)
                s4 = [P, GT, N0]
                link(v.tensor_reduce(lsum[:, :], lg, AX.X, ALU.max))
                did(v.tensor_tensor(LG[:, :, :], lg, bcast(lsum[:, :], s4, 2), ALU.subtract), "lg")
                after(sca, "l0exp")
                link(v.tensor_reduce(lsum[:, :], PB[:, :, :], AX.X, ALU.add))
                link(v.reciprocal(lsum[:, :], lsum[:, :]))
                did(v.tensor_tensor(PB[:, :, :], PB[:, :, :], bcast(lsum[:, :], s4, 2), ALU.mult), "probs_in")
                did(top_two(nc, env, link, PB[:, :, :], N0, GT, env.top), "g0diff")
                after(sca, "g0exp")
                did(gate_weights(nc, link, GATE[:, :, :], N0, GT, env.top), "gate")
                for e in range(N0):
                    after(ten, f"y_{e}")
                    for j in range(GT):
                        ins = v.scalar_tensor_tensor(X[:, j, :], Y[e % 2][:, j * P:(j + 1) * P], GATE[:, j, e:e + 1], X[:, j, :], ALU.mult, ALU.add)
                    did(ins, f"comb_{e}")
                after(ten, "gb")
                did(v.tensor_tensor(X[:, :, :], X[:, :, :], tiles_of(B[0][:, :]), ALU.add), "gb")
                did(layer_norm(nc, env, link, X, XH[:, :, :]), "xh2")
                after(sca, "ex")
                did(v.tensor_tensor(EX[:, :, :], EX[:, :, :], ADJT[:, :, :], ALU.mult), "att")
                after(ten, "c2")
                did(v.scalar_tensor_tensor(CV[:, :], B[2][:, :], env.bn_scale[:, 1:2], XT[:, :], ALU.mult, ALU.add), "cv")
                after(sca, "r")
                link(v.tensor_scalar(R[:, :], R[:, :], 0.5, 0.5, ALU.mult, ALU.add))
                link(v.scalar_tensor_tensor(T1[:, :], B[6][:, :], env.col("b_hh", 2), R[:, :], ALU.add, ALU.mult))
                after(ten, "gin")
                did(v.tensor_tensor(T1[:, :], T1[:, :], B[5][:, :], ALU.add), "t1")
                after(sca, "nn")
                link(v.tensor_scalar(Z[:, :], Z[:, :], 0.5, 0.5, ALU.mult, ALU.add))
                link(v.tensor_tensor(O[:, :], XT[:, :], NN[:, :], ALU.subtract))
                link(v.tensor_tensor(O[:, :], O[:, :], Z[:, :], ALU.mult))
                did(v.tensor_tensor(O[:, :], O[:, :], NN[:, :], ALU.add), "o")
                after(ten, "ot")
                did(v.tensor_tensor(X[:, :, :], X[:, :, :], tiles_of(B[0][:, :]), ALU.add), "ot")
                link(copy(nc, env.x[:, tiles, :], X[:, :, :]))
                did(layer_norm(nc, env, link, X, XH[:, :, :]), "xh3")
                after(ten, "hh")
                hh = B[7][:, 0:GT * 16].rearrange("p (j f) -> p j f", j=GT)
                h4 = lambda t: t.rearrange("p j (h x) -> p (j h) x", x=EXPERTS1)
                link(v.tensor_copy(ROWL[:, :, 0:16], hh))
                link(v.tensor_tensor(PROD[:, :, :], ROWL[:, :, 0:16], bcast(env.att_src[:, :], [P, GT, 16], 1), ALU.mult))
                for j in range(GT):
                    ins = v.tensor_reduce(ROWL[:, j, 16:ROW], PROD[:, j, :].rearrange("p (h x) -> p h x", x=EXPERTS1), AX.X, ALU.add)
                link(ins)
                link(v.tensor_tensor(PROD[:, :, :], ROWL[:, :, 0:16], bcast(env.att_dst[:, :], [P, GT, 16], 1), ALU.mult))
                for j in range(GT):
                    ins = v.tensor_reduce(ADL[:, j, :], PROD[:, j, :].rearrange("p (h x) -> p h x", x=EXPERTS1), AX.X, ALU.add)
                link(ins)
                link(copy(nc, env.a_dst[:, tiles, :], ADL[:, :, :]))
                did(copy(nc, env.own_rows[:, tiles, :], ROWL[:, :, :]), "rows")
                dve.wait_ge(rows_out, i * 16 + 16)
                link.end()


class Experts:
    def __init__(self, tag, experts, chunks, w1, w2, b1, b2, func, gates):
        self.tag, self.experts, self.chunks, self.total = tag, experts, chunks, experts * chunks
        self.w1, self.w2, self.b1, self.b2, self.func, self.gates = w1, w2, b1, b2, func, gates

    def tensor_names(self):
        out = []
        for k in range(self.total + 1):
            out += [f"{self.tag}_up_{k}"] if k < self.total else []
            out += [f"{self.tag}_down_{k-1}"] if k > 0 else []
        return out + [f"{self.tag}_gt", f"{self.tag}_gb"]

    def scalar_names(self):
        return [f"{self.tag}_h_{k}" for k in range(self.total)] + [f"{self.tag}_gt"]

    def vector_names(self):
        return [f"{self.tag}_comb_{e}" for e in range(self.experts)] + [f"{self.tag}_gb"]


def phase_c(nc, env):
    f1 = Experts("f1", EXPERTS1, 2, "f1_w1", "f1_w2", "f1_b1", env.f1_b2, ACT.Gelu, "gates1")
    f2 = Experts("f2", EXPERTS2 + 1, 4, "f2_w1", "f2_w2", "f2_b1", env.f2_b2, ACT.Gelu, "gate")
    f3 = Experts("f3", EXPERTS3, 4, "f3_w1", "f3_w2", "f3_b1", env.f3_b2, ACT.Relu, "gate")
    tensor_names = (["f1_xt"] + f1.tensor_names() + ["g2_adjT", "g2_xt", "agg", "conv", "f2_xt", "f2_lg"] + f2.tensor_names()
                    + ["g3_xt", "inter", "sim", "pt", "ov", "f3_xt", "f3_lg"] + f3.tensor_names())
    scalar_names = (["f1_xt"] + f1.scalar_names() + ["g2_adjT", "g2_xt", "agg", "f2_xt", "f2_exp"] + f2.scalar_names()
                    + ["g3_xt", "inter", "soft", "pt", "f3_xt", "f3_exp"] + f3.scalar_names())
    vector_names = (["f1_xh"] + f1.vector_names() + ["g2_xh", "conv", "f2_xh", "f2_diff", "f2_gate"] + f2.vector_names()
                    + ["g3_xh", "masked", "ov", "f3_xh", "f3_diff", "f3_gate"] + f3.vector_names() + ["out"])
    LINKS = 160
    with ExitStack() as ctx:
        sb = lambda n, s, d=F32: ctx.enter_context(nc.sbuf_tensor("c_" + n, s, d))
        sem = lambda n: ctx.enter_context(nc.semaphore("c_" + n))
        ten, sca, vec = (Steps(None, sem(n), s) for n, s in (("tensor_step", tensor_names), ("scalar_step", scalar_names), ("vector_step", vector_names)))
        link_sem, adj_in, mask_in, stored = sem("vector_link"), sem("adj_loaded"), sem("mask_loaded"), sem("out_stored")
        X, XH, ADJ, ADJT, SM, OUT = (sb(n, [P, GT, D]) for n in ("x", "xh", "adj", "adjt", "sim", "out"))
        AG, XT, IT, PT = (sb(n, [P, GT * P]) for n in ("ag", "xt", "it", "pt"))
        H = [sb(f"h_{k}", [P, GT * P]) for k in range(3)]
        GTR = sb("gate_rows", [EMAX, GT * P])
        GATE, LG = sb("gate", [P, GT, EMAX]), sb("lg", [P, GT, EMAX])
        MI, MK, MB = sb("mask_int", [P, GT, P], I32), sb("mask", [P, GT, P]), sb("mask_bias", [P, GT, P])
        mx, nmx, ssum = (sb(n, [P, GT]) for n in ("mx", "nmx", "ssum"))
        B = env.bank
        U, Y = (B[1], B[2], B[3]), (B[4], B[5])
        env.norms = norms = Norms(nc, env, sem("var_ready"), sem("rstd_ready"), 6)
        block = ctx.enter_context(nc.Block())

        @block.gpsimd
        def _(pool):
            with pool.Fori(0, GROUPS) as i:
                norms.serve(pool, i)

        @block.sync
        def _(sp):
            with sp.Fori(0, GROUPS) as i:
                sp.wait_ge(vec.done, vec.count("masked", i - 1))
                sp.dma_start(ADJ[:, :, :], env.adj_dram[bass.ds(i * GT, GT), :, :].rearrange("g n m -> n g m")).then_inc(adj_in, 16)
                sp.dma_start(MI[:, :, :], env.mask_dram[bass.ds(i * GT, GT), :].partition_broadcast(P)).then_inc(mask_in, 16)
                sp.wait_ge(vec.done, vec.count("out", i))
                sp.dma_start(env.out_dram[bass.ds(i * GT, GT), :, :].rearrange("g n d -> n g d"), OUT[:, :, :]).then_inc(stored, 16)
            sp.wait_ge(stored, 16 * GROUPS)

        @block.tensor
        def _(pe):
            ten.begin(pe)
            mm = nc.tensor.matmul
            with pe.Fori(0, GROUPS) as i:
                after = lambda who, name: pe.wait_ge(who.done, who.count(name, i))

                def experts(f):
                    for k in range(f.total + 1):
                        if k < f.total:
                            if k >= 3:
                                after(sca, f"{f.tag}_h_{k-3}")
                            ten.did(mm(U[k % 3][:, :], lhsT=env.w(f.w1, k), rhs=XT[:, :], start=True, stop=True), f"{f.tag}_up_{k}")
                        if k > 0:
                            c = k - 1
                            e, part = divmod(c, f.chunks)
                            after(sca, f"{f.tag}_h_{c}")
                            if part == 0 and e >= 2:
                                after(vec, f"{f.tag}_comb_{e-2}")
                            for j in range(GT):
                                ins = mm(Y[e % 2][:, j * P:(j + 1) * P], lhsT=H[c % 3][:, j * P:(j + 1) * P], rhs=env.w(f.w2, c),
                                         start=j == 0 and part == 0, stop=j == GT - 1 and part == f.chunks - 1, skip_group_check=True)
                            ten.did(ins, f"{f.tag}_down_{c}")
                    if f.tag != "f1":
                        after(vec, f"{f.tag}_gate")
                    ten.did(turn(nc, B[7], GATE, env.ident, f.experts), f"{f.tag}_gt")
                    after(sca, f"{f.tag}_gt")
                    for j in range(GT):
                        ins = mm(B[0][:, j * P:(j + 1) * P], lhsT=GTR[0:f.experts, j * P:(j + 1) * P], rhs=f.b2[:, :], start=j == 0, stop=j == GT - 1, skip_group_check=True)
                    ten.did(ins, f"{f.tag}_gb")

                def turned(name):
                    after(vec, name + "h")
                    ten.did(turn(nc, B[0], XH, env.ident), name + "t")
                    after(sca, name + "t")

                turned("f1_x")
                experts(f1)
                pe.wait_ge(adj_in, i * 16 + 16)
                ten.did(turn(nc, B[6], ADJ, env.ident), "g2_adjT")
                turned("g2_x")
                for j in range(GT):
                    ins = mm(B[2][:, j * P:(j + 1) * P], lhsT=XH[:, j, :], rhs=ADJT[:, j, :], start=j == 0, stop=j == GT - 1, skip_group_check=True)
                ten.did(ins, "agg")
                after(sca, "agg")
                for j in range(GT):
                    o, s = B[4][:, j * P:(j + 1) * P], slice(j * P, (j + 1) * P)
                    mm(o, lhsT=AG[:, s], rhs=env.w("w_rel"), start=j == 0, stop=False, skip_group_check=True)
                    mm(o, lhsT=XT[:, s], rhs=env.w("w_root"), start=False, stop=False, skip_group_check=True)
                    ins = mm(o, lhsT=env.ones[0:1, :], rhs=env.row("b_rel"), start=False, stop=j == GT - 1, skip_group_check=True)
                ten.did(ins, "conv")
                turned("f2_x")
                for j in range(GT):
                    ins = mm(B[7][:, j * EXPERTS2:(j + 1) * EXPERTS2], lhsT=XT[:, j * P:(j + 1) * P], rhs=env.w("f2_wr"), start=j == 0, stop=j == GT - 1, skip_group_check=True)
                ten.did(ins, "f2_lg")
                experts(f2)
                turned("g3_x")
                ten.did(mm(B[1][:, :], lhsT=env.w("g3_w"), rhs=XT[:, :], start=True, stop=True), "inter")
                after(sca, "inter")
                for j in range(GT):
                    s = slice(j * P, (j + 1) * P)
                    ins = mm(B[2][:, s], lhsT=IT[:, s], rhs=XT[:, s], start=j == 0, stop=j == GT - 1, skip_group_check=True)
                ten.did(ins, "sim")
                after(sca, "soft")
                ten.did(turn(nc, B[3], SM, env.ident), "pt")
                after(sca, "pt")
                for j in range(GT):
                    ins = mm(B[4][:, j * P:(j + 1) * P], lhsT=PT[:, j * P:(j + 1) * P], rhs=XH[:, j, :], start=j == 0, stop=j == GT - 1, skip_group_check=True)
                ten.did(ins, "ov")
                turned("f3_x")
                for j in range(GT):
                    o = B[7][:, j * EXPERTS3:(j + 1) * EXPERTS3]
                    mm(o, lhsT=XT[:, j * P:(j + 1) * P], rhs=env.w("f3_wg"), start=j == 0, stop=False, skip_group_check=True)
                    ins = mm(o, lhsT=env.ones[0:1, :], rhs=env.row("f3_bg"), start=False, stop=j == GT - 1, skip_group_check=True)
                ten.did(ins, "f3_lg")
                experts(f3)

        @block.scalar
        def _(act):
            sca.begin(act)
            go = nc.scalar.activation
            with act.Fori(0, GROUPS) as i:
                after = lambda who, name: act.wait_ge(who.done, who.count(name, i))

                def turned(name):
                    after(ten, name)
                    sca.did(go(XT[:, :], B[0][:, :], ACT.Copy), name)

                def experts(f):
                    for k in range(f.total):
                        after(ten, f"{f.tag}_up_{k}")
                        if k >= 3:
                            after(ten, f"{f.tag}_down_{k-3}")
                        sca.did(go(H[k % 3][:, :], U[k % 3][:, :], f.func, bias=env.col(f.b1, k)), f"{f.tag}_h_{k}")
                    after(ten, f"{f.tag}_gt")
                    sca.did(go(GTR[0:f.experts, :], B[7][0:f.experts, :], ACT.Copy), f"{f.tag}_gt")

                def pair(tag):
                    after(vec, f"{tag}_diff")
                    sca.did(go(env.top.diff_exp[:, 0:GT], env.top.diff[:, 0:GT], ACT.Exp), f"{tag}_exp")

                turned("f1_xt")
                experts(f1)
                after(ten, "g2_adjT")
                sca.did(go(ADJT[:, :, :], tiles_of(B[6][:, :]), ACT.Copy), "g2_adjT")
                turned("g2_xt")
                after(ten, "agg")
                sca.did(go(AG[:, :], B[2][:, :], ACT.Copy), "agg")
                turned("f2_xt")
                pair("f2")
                experts(f2)
                turned("g3_xt")
                after(ten, "inter")
                sca.did(go(IT[:, :], B[1][:, :], ACT.Copy), "inter")
                after(vec, "masked")
                for j in range(GT):
                    ins = go(SM[:, j, :], SM[:, j, :], ACT.Exp, bias=nmx[:, j:j + 1], accum_out=ssum[:, j:j + 1])
                sca.did(ins, "soft")
                after(ten, "pt")
                sca.did(go(PT[:, :], B[3][:, :], ACT.Copy), "pt")
                turned("f3_xt")
                pair("f3")
                experts(f3)

        @block.vector
        def _(dve):
            vec.begin(dve)
            v = nc.vector
            with dve.Fori(0, GROUPS) as i:
                link = Link(dve, link_sem, i, LINKS)
                norms.i = i
                after = lambda who, name: dve.wait_ge(who.done, who.count(name, i))

                def did(ins, name):
                    vec.did(ins, name)
                    dve.wait_ge(vec.done, vec.count(name, i))

                def experts(f):
                    for e in range(f.experts):
                        after(ten, f"{f.tag}_down_{(e + 1) * f.chunks - 1}")
                        for j in range(GT):
                            ins = v.scalar_tensor_tensor(X[:, j, :], Y[e % 2][:, j * P:(j + 1) * P], GATE[:, j, e:e + 1], X[:, j, :], ALU.mult, ALU.add)
                        did(ins, f"{f.tag}_comb_{e}")
                    after(ten, f"{f.tag}_gb")
                    did(v.tensor_tensor(X[:, :, :], X[:, :, :], tiles_of(B[0][:, :]), ALU.add), f"{f.tag}_gb")

                def router(f, n, first):
                    after(ten, f"{f.tag}_lg")
                    link(v.tensor_copy(LG[:, :, 0:n], B[7][:, 0:GT * n].rearrange("p (j e) -> p j e", j=GT)))
                    did(top_two(nc, env, link, LG[:, :, 0:n], n, GT, env.top), f"{f.tag}_diff")
                    if first:
                        link(v.memset(GATE[:, :, 0:1], 1.0))
                    after(sca, f"{f.tag}_exp")
                    did(gate_weights(nc, link, GATE[:, :, first:first + n], n, GT, env.top), f"{f.tag}_gate")

                tiles = bass.ds(i * GT, GT)
                link(copy(nc, X[:, :, :], env.x[:, tiles, :]))
                link(copy(nc, GATE[:, :, 0:EXPERTS1], env.gates1[:, tiles, :]))
                did(layer_norm(nc, env, link, X, XH[:, :, :]), "f1_xh")
                experts(f1)
                link(layer_norm(nc, env, link, X, OUT[:, :, :]))
                link(v.tensor_tensor(X[:, :, :], X[:, :, :], OUT[:, :, :], ALU.add))
                did(layer_norm(nc, env, link, OUT, XH[:, :, :], (env.gamma, env.beta)), "g2_xh")
                after(ten, "conv")
                did(v.scalar_tensor_tensor(X[:, :, :], tiles_of(B[4][:, :]), 0.0, X[:, :, :], ALU.max, ALU.add), "conv")
                did(layer_norm(nc, env, link, X, XH[:, :, :]), "f2_xh")
                router(f2, EXPERTS2, 1)
                experts(f2)
                did(layer_norm(nc, env, link, X, XH[:, :, :]), "g3_xh")
                dve.wait_ge(mask_in, i * 16 + 16)
                link(v.tensor_copy(MK[:, :, :], MI[:, :, :]))
                link(v.tensor_scalar(MK[:, :, :], MK[:, :, :], 0.0, None, ALU.not_equal))
                link(v.tensor_scalar(MB[:, :, :], MK[:, :, :], -1.0, BIG, ALU.add, ALU.mult))
                after(ten, "sim")
                link(v.tensor_tensor(SM[:, :, :], tiles_of(B[2][:, :]), ADJ[:, :, :], ALU.mult))
                link(v.tensor_tensor(SM[:, :, :], SM[:, :, :], MK[:, :, :], ALU.mult))
                link(v.tensor_tensor(SM[:, :, :], SM[:, :, :], MB[:, :, :], ALU.add))
                link(v.tensor_reduce(mx[:, :], SM[:, :, :], AX.X, ALU.max))
                did(v.tensor_scalar(nmx[:, :], mx[:, :], -1.0, None, ALU.mult), "masked")
                after(ten, "ov")
                link(v.reciprocal(ssum[:, :], ssum[:, :]))
                for j in range(GT):
                    ins = v.scalar_tensor_tensor(X[:, j, :], B[4][:, j * P:(j + 1) * P], ssum[:, j:j + 1], X[:, j, :], ALU.mult, ALU.add)
                did(ins, "ov")
                did(layer_norm(nc, env, link, X, XH[:, :, :]), "f3_xh")
                router(f3, EXPERTS3, 0)
                experts(f3)
                link.end()
                did(v.tensor_copy(OUT[:, :, :], X[:, :, :]), "out")
                dve.wait_ge(stored, i * 16 + 16)


class Top:
    def __init__(self, sb, tiles, n):
        wide, narrow = [P, tiles, n], [P, tiles]
        self.first, self.second, self.tie, self.rest = sb("top_first", wide), sb("top_second", wide), sb("top_tie", wide), sb("top_rest", wide)
        self.max1, self.max2, self.best = sb("top_max1", narrow), sb("top_max2", narrow), sb("top_best", narrow)
        self.diff, self.diff_exp = sb("top_diff", narrow), sb("top_diff_exp", narrow)
        self.w1, self.w2 = sb("top_w1", narrow), sb("top_w2", narrow)


class Names:
    pass


W_A = [("l0_w", 1, 128), ("rw1", 1, 64), ("ew1", 6, 128), ("ew2", 6, 128), ("ew3", 6, 128), ("conv1", 1, 128), ("conv2", 17, 128),
       ("w_se", 1, 3), ("w_msg", 1, 128), ("w_hh", 3, 128), ("w_ih", 6, 128), ("w_gat", 1, 16)]
W_C = [("f1_w1", 8, 128), ("f1_w2", 8, 128), ("w_rel", 1, 128), ("w_root", 1, 128), ("f2_wr", 1, 8), ("f2_w1", 36, 128), ("f2_w2", 36, 128),
       ("g3_w", 1, 128), ("f3_wg", 1, 8), ("f3_w1", 32, 128), ("f3_w2", 32, 128)]
COLS = [("rb1", 1), ("eb1", 6), ("eb2", 6), ("b_se", 1), ("bn1_g", 1), ("bn1_b", 1), ("bn1_m", 1), ("bn1_v", 1), ("bn2_g", 1), ("bn2_b", 1),
        ("bn2_m", 1), ("bn2_v", 1), ("b_ih", 3), ("b_hh", 3), ("f1_b1", 8), ("f2_b1", 36), ("f3_b1", 32)]
ROWS = [("l0_bias", 128), ("rb2", 6), ("b_msg", 128), ("b_rel", 128), ("f3_bg", 8)]
SPREAD = [("prelu", 1), ("att_src", 16), ("att_dst", 16), ("b_gat", 16), ("gat_gamma", 16), ("gat_beta", 16), ("gamma", 128), ("beta", 128)]


def offsets(table):
    out, at = {}, 0
    for name, *dims in table:
        out[name] = (at, dims[-1])
        at += dims[0] * dims[-1] if len(dims) > 1 else dims[0]
    return out, at


def setup(nc, env, d):
    with ExitStack() as ctx:
        sem = lambda n: ctx.enter_context(nc.semaphore("s_" + n))
        loaded, made, step, var_in, scaled = sem("loaded"), sem("constants_made"), sem("vector_step"), sem("bn_variance_ready"), sem("bn_scale_ready")
        block = ctx.enter_context(nc.Block())

        @block.sync
        def _(sp):
            sp.dma_start(env.cols[:, :], d["cols"]).then_inc(loaded, 16)
            sp.dma_start(env.spread[:, :], d["spread"].partition_broadcast(P)).then_inc(loaded, 16)
            sp.dma_start(env.rows[:, :], d["rows"].rearrange("(o n) -> o n", o=1)).then_inc(loaded, 16)
            for name, t in (("rw2", env.rw2), ("eb3", env.eb3), ("f1_b2", env.f1_b2), ("f2_b2", env.f2_b2), ("f3_b2", env.f3_b2)):
                sp.dma_start(t[:, :], d[name]).then_inc(loaded, 16)
            sp.dma_start(env.x[:, :, :], d["x"].rearrange("g n d -> n g d")).then_inc(loaded, 16)
            sp.wait_ge(loaded, 16 * 9)

        @block.gpsimd
        def _(pool):
            g = nc.gpsimd
            g.memset(env.ident[:, :], 0.0).then_inc(made, 1)
            pool.wait_ge(made, 1)
            g.affine_select(out=env.ident[:, :], in_=env.ident[:, :], compare_op=ALU.not_equal, fill=1.0, base=0,
                            pattern=[[-1, P]], channel_multiplier=1).then_inc(made, 1)
            g.memset(env.minus_half[:, :], -0.5).then_inc(made, 1)
            g.iota(env.earlier_i[:, :], pattern=[[-1, EMAX]], base=EMAX, channel_multiplier=0).then_inc(made, 1)
            pool.wait_ge(var_in, 1)
            g.tensor_tensor(env.bn_scale[:, :], env.bn_scale[:, :], env.minus_half[:, 0:2], ALU.pow).then_inc(scaled, 1)

        @block.vector
        def _(dve):
            v = nc.vector
            n = [0]

            def link(ins):
                n[0] += 1
                ins.then_inc(step, 1)
                dve.wait_ge(step, n[0])

            v.memset(env.ones[:, :], 1.0)
            v.memset(env.neg_ones[:, :], -1.0)
            v.memset(env.rounds_before[:, 0:1], 0)
            link(v.memset(env.ones_nt[:, :], 1.0))
            dve.wait_ge(made, 4)
            link(v.tensor_copy(env.earlier[:, :], env.earlier_i[:, :]))
            dve.wait_ge(loaded, 16 * 9)
            for k, tag in enumerate(("bn1", "bn2")):
                ins = v.tensor_scalar(env.bn_scale[:, k:k + 1], env.col(tag + "_v"), 1e-5, None, ALU.add)
            ins.then_inc(var_in, 1)
            dve.wait_ge(scaled, 1)
            for k, tag in enumerate(("bn1", "bn2")):
                s, h = env.bn_scale[:, k:k + 1], env.bn_shift[:, k:k + 1]
                link(v.tensor_tensor(s, s, env.col(tag + "_g"), ALU.mult))
                link(v.tensor_tensor(h, s, env.col(tag + "_m"), ALU.mult))
                link(v.tensor_tensor(h, env.col(tag + "_b"), h, ALU.subtract))
            for k in range(2):
                link(v.tensor_tensor(env.gru_bias[:, k:k + 1], env.col("b_ih", k), env.col("b_hh", k), ALU.add))
            link(v.tensor_scalar(env.gru_bias[:, :], env.gru_bias[:, :], 0.5, None, ALU.mult))


def gates_l1(nc, env):
    with ExitStack() as ctx:
        sb = lambda n, s: ctx.enter_context(nc.sbuf_tensor("g_" + n, s, F32))
        step, diff, ex, var_in, rstd = (ctx.enter_context(nc.semaphore("g_" + n)) for n in ("vector_step", "diff_ready", "exp_ready", "var_ready", "rstd_ready"))
        T = sb("centered", [P, NT, 16])
        S = sb("squared", [P, NT, 16])
        mean, var = sb("mean", [P, NT]), sb("var", [P, NT])
        top = Top(sb, NT, EXPERTS1)
        score = sb("score", [P, NT, EXPERTS1])
        block = ctx.enter_context(nc.Block())

        @block.gpsimd
        def _(pool):
            pool.wait_ge(var_in, 1)
            nc.gpsimd.tensor_tensor(var[:, :], var[:, :], env.minus_half[:, :], ALU.pow).then_inc(rstd, 1)

        @block.scalar
        def _(act):
            act.wait_ge(diff, 1)
            nc.scalar.activation(top.diff_exp[:, :], top.diff[:, :], ACT.Exp).then_inc(ex, 1)

        @block.vector
        def _(dve):
            v = nc.vector
            n = [0]

            def link(ins):
                n[0] += 1
                ins.then_inc(step, 1)
                dve.wait_ge(step, n[0])

            s16 = [P, NT, 16]
            A = env.att_acc
            link(v.tensor_reduce(mean[:, :], A[:, :, :], AX.X, ALU.add))
            link(v.tensor_scalar(mean[:, :], mean[:, :], 1.0 / 16, None, ALU.mult))
            link(v.tensor_tensor(T[:, :, :], A[:, :, :], bcast(mean[:, :], s16, 2), ALU.subtract))
            link(v.tensor_tensor(S[:, :, :], T[:, :, :], T[:, :, :], ALU.mult))
            link(v.tensor_reduce(var[:, :], S[:, :, :], AX.X, ALU.add))
            v.tensor_scalar(var[:, :], var[:, :], 1.0 / 16, LN_EPS, ALU.mult, ALU.add).then_inc(var_in, 1)
            dve.wait_ge(rstd, 1)
            link(v.tensor_tensor(T[:, :, :], T[:, :, :], bcast(var[:, :], s16, 2), ALU.mult))
            link(v.tensor_tensor(T[:, :, :], T[:, :, :], bcast(env.spread_of("gat_gamma"), s16, 1), ALU.mult))
            link(v.tensor_tensor(T[:, :, :], T[:, :, :], bcast(env.spread_of("gat_beta"), s16, 1), ALU.add))
            link(v.tensor_reduce(score[:, :, :], T[:, :, :].rearrange("p t (h x) -> p t x h", x=EXPERTS1), AX.X, ALU.add))
            link(v.tensor_scalar(score[:, :, :], score[:, :, :], 1.0 / HEADS, None, ALU.mult))
            top_two(nc, env, link, score[:, :, :], EXPERTS1, NT, top).then_inc(diff, 1)
            dve.wait_ge(ex, 1)
            link(gate_weights(nc, link, env.gates1[:, :, :], EXPERTS1, NT, top))


def load_weights(nc, env, tensor, dram):
    with ExitStack() as ctx:
        s = ctx.enter_context(nc.semaphore("weights_" + dram.tensor.name))
        block = ctx.enter_context(nc.Block())

        @block.sync
        def _(sp):
            sp.dma_start(tensor, dram).then_inc(s, 16)
            sp.wait_ge(s, 16)


def program(nc, d):
    env = Names()
    with ExitStack() as ctx:
        sb = lambda n, s, dt=F32: ctx.enter_context(nc.sbuf_tensor(n, s, dt))
        sem = lambda n: ctx.enter_context(nc.semaphore(n))

        cols, ncols = offsets(COLS)
        rows, nrows = offsets(ROWS)
        spread, nspread = offsets(SPREAD)
        env.x = sb("x", [P, NT, D])
        env.cols = sb("cols", [P, ncols])
        env.spread = sb("spread", [P, nspread])
        env.rows = sb("rows", [1, nrows])
        env.rw2 = sb("rw2", [ROUTER_H, EXPERTS0])
        env.eb3 = sb("eb3", [EXPERTS0, D])
        env.f1_b2 = sb("f1_b2", [EXPERTS1, D])
        env.f2_b2 = sb("f2_b2", [EXPERTS2 + 1, D])
        env.f3_b2 = sb("f3_b2", [EXPERTS3, D])
        env.ident = sb("ident", [P, P])
        env.ones = sb("ones", [1, P])
        env.neg_ones = sb("neg_ones", [3, P])
        env.earlier_i = sb("earlier_i", [P, EMAX], I32)
        env.earlier = sb("earlier", [P, EMAX])
        env.bn_scale = sb("bn_scale", [P, 2])
        env.bn_shift = sb("bn_shift", [P, 2])
        env.gru_bias = sb("gru_bias", [P, 2])
        env.ln_stats = sb("ln_stats", [P, GT, 6])
        env.ln_mv = sb("ln_mv", [P, GT, 2])
        env.ln_rstd = sb("ln_rstd", [P, GT])
        env.ln_var = sb("ln_var", [P, GT])
        env.minus_half = sb("minus_half", [P, NT])
        env.own_rows = sb("own_rows", [P, NT, ROW])
        env.a_dst = sb("a_dst", [P, NT, HEADS])
        env.gates1 = sb("gates1", [P, NT, EXPERTS1])
        env.att_acc = sb("att_acc", [P, NT, 16])
        env.start_of = sb("start_of", [P, NT1], I32)
        env.node_id = sb("node_id", [P, NT1], I32)
        env.slot_row = sb("slot_row", [P, NT, SLOTS], I32)
        env.slot_penalty = sb("slot_penalty", [P, NT, SLOTS])
        env.tile_groups = sb("tile_groups", [P, NT], I32)
        env.tile_rounds = sb("tile_rounds", [P, NT], I32)
        env.rounds_before = sb("rounds_before", [P, NT], I32)
        env.ones_nt = sb("ones_nt", [P, NT])
        env.top = Top(sb, GT, EMAX)
        env.spread_of = lambda n: env.spread[:, spread[n][0]:spread[n][0] + spread[n][1]]
        env.col = lambda n, k=0: env.cols[:, cols[n][0] + k:cols[n][0] + k + 1]
        env.row = lambda n: env.rows[0:1, rows[n][0]:rows[n][0] + dict(ROWS)[n]]
        env.prelu, env.gamma, env.beta = env.spread_of("prelu"), env.spread_of("gamma"), env.spread_of("beta")
        env.att_src, env.att_dst, env.b_gat = env.spread_of("att_src"), env.spread_of("att_dst"), env.spread_of("b_gat")
        env.bank = [ctx.enter_context(nc.psum_tensor(f"bank{k}", [P, GT * P], F32)) for k in range(8)]
        dram = lambda n, s, dt: nc.dram_tensor(n, s, dt, kind="Internal").ap()
        env.sorted_dram = dram("sorted_dram", [E_TOTAL + SLOTS], F32)
        env.row_first_dram = dram("row_first_dram", [P], F32)
        env.chunk_first_dram = dram("chunk_first_dram", [P, 32], F32)
        env.start_dram = dram("start_dram", [NT1 * P], I32)
        env.table_dram = dram("table_dram", [NODES, ROW], F32)
        env.adj_dram, env.mask_dram, env.out_dram = d["adj"], d["nodemask"], d["out"]
        env.sign_ready, env.idx_sem, env.att_fin, env.pause = sem("sign_ready"), sem("indices_copied"), sem("aggregate_step"), sem("pause")

        setup(nc, env, d)
        with ExitStack() as part:
            sbp = lambda n, s, dt=F32: part.enter_context(nc.sbuf_tensor(n, s, dt))
            env.keys_a = sbp("keys_a", [P, 4096])
            env.keys_b = sbp("keys_b", [P, 4096])
            env.end_of = sbp("end_of", [P, NT], I32)
            env.part_id = sbp("part_id", [P, 1], I32)
            env.sign_i = sbp("sign_i", [P, 7], I32)
            env.sign = sbp("sign", [P, 7])
            env.tail_i = sbp("tail_i", [P, SLOTS], I32)
            env.tail_keys = sbp("tail_keys", [P, SLOTS])
            env.chunk_first = sbp("chunk_first", [P, 32])
            env.row_first = sbp("row_first", [P, P])
            env.node_key = sbp("node_key", [P, NT1], I32)
            env.search_cmp = sbp("search_cmp", [P, NT1, P])
            env.cnt = sbp("cnt", [P, NT1])
            env.row_f = sbp("row_f", [P, NT1])
            env.row_index = sbp("row_index", [P, NT1], I32)
            env.l2_rows = sbp("l2_rows", [P, NT1, 32])
            env.chunk_index = sbp("chunk_index", [P, NT1], I32)
            env.start_f = sbp("start_f", [P, NT1])
            env.key_row_index = sbp("key_row_index", [P, 2, NT], I32)
            env.key_rows = sbp("key_rows", [P, NT, 2 * SLOTS])
            env.shift_bit = sbp("shift_bit", [P, NT], I32)
            env.degree = sbp("degree", [P, NT])
            env.deg_max = sbp("deg_max", [P, NT])
            env.tile_groups_f = sbp("tile_groups_f", [P, NT])
            with nc.sbuf_tensor("l3_rows", [P, NT1, P], F32) as l3:
                env.l3_rows = l3
                env.shifted = l3[:, :, :].rearrange("p a b -> p (a b)")[:, 0:NT * 2 * SLOTS].rearrange("p (a b) -> p a b", a=NT)
                env.slot_dst = env.search_cmp[:, :, :].rearrange("p a b -> p (a b)")[:, 0:NT * SLOTS].bitcast(I32).rearrange("p (a b) -> p a b", a=NT)
                sort_edges(nc, env, d["edge_index"])

        with ExitStack() as part:
            wa, na = offsets(W_A)
            WA = part.enter_context(nc.sbuf_tensor("weights_a", [P, na], F32))
            env.w = lambda n, k=0: WA[:, wa[n][0] + k * wa[n][1]:wa[n][0] + (k + 1) * wa[n][1]]
            load_weights(nc, env, WA[:, :], d["weights_a"])
            phase_a(nc, env)
        with ExitStack() as part:
            sbp = lambda n, s, dt=F32: part.enter_context(nc.sbuf_tensor(n, s, dt))
            env.att_max = sbp("att_max", [P, NT, 4])
            env.att_den = sbp("att_den", [P, NT, 4])
            env.rounds_f = sbp("rounds_f", [P, NT])
            env.rounds_f2 = sbp("rounds_f2", [P, NT + 1])
            env.groups_f = sbp("groups_f", [P, 2, NT // 2])
            env.groups_sum = sbp("groups_sum", [P, 2, NT // 2])
            env.rows_due = sbp("rows_due", [P, 2, NT // 2], I32)
            env.idx_now = sbp("idx_now", [P, 2, SLOTS], I32)
            attend(nc, env)
            gates_l1(nc, env)
        with ExitStack() as part:
            wc, nw = offsets(W_C)
            WC = part.enter_context(nc.sbuf_tensor("weights_c", [P, nw], F32))
            env.w = lambda n, k=0: WC[:, wc[n][0] + k * wc[n][1]:wc[n][0] + (k + 1) * wc[n][1]]
            load_weights(nc, env, WC[:, :], d["weights_c"])
            phase_c(nc, env)


def kernel(**inputs):
    import numpy as np
    import concourse.bacc as bacc
    from concourse.bass_utils import run_bass_kernel_spmd

    a = {k: np.asarray(v) for k, v in inputs.items()}
    flat = lambda t: np.ascontiguousarray(t).reshape(P, -1)
    stack = lambda t: flat(np.transpose(t, (1, 0, 2)))
    rows_in = lambda t: flat(np.transpose(t.reshape(-1, P, t.shape[-1]), (1, 0, 2)))
    col = lambda t: np.ascontiguousarray(t.reshape(-1, P).T)

    def short_col(t):
        out = np.zeros((P, 1), t.dtype)
        out[:t.size, 0] = t
        return out

    g, f = "L1_gnn_", "L1_ffn_"
    weights_a = np.concatenate([
        a["L0_gnn_W"], a["L0_ffn_router_w1"], stack(a["L0_ffn_expert_w1"]), stack(a["L0_ffn_expert_w2"]), stack(a["L0_ffn_expert_w3"]),
        a[g + "conv1_w"][:, :, 0].T, flat(np.transpose(a[g + "conv2_w"], (1, 2, 0))), a[g + "w_se"].T, a[g + "w_msg"].T,
        a[g + "w_hh"].T, flat(np.concatenate([a[g + "w_ih"][:, :P].T, a[g + "w_ih"][:, P:].T], axis=1)), a[f + "W_gat"]], axis=1)
    weights_c = np.concatenate([
        stack(a[f + "W1"]), rows_in(a[f + "W2"].reshape(-1, P)), a["L2_gnn_W_rel"], a["L2_gnn_W_root"], a["L2_ffn_Wr"],
        a["L2_ffn_W1s"], stack(a["L2_ffn_W1p"]), rows_in(a["L2_ffn_W2s"]), rows_in(a["L2_ffn_W2p"].reshape(-1, P)),
        a["L3_gnn_W"], a["L3_ffn_Wg"].T, flat(np.transpose(a["L3_ffn_W1"], (2, 0, 1))),
        rows_in(np.ascontiguousarray(np.transpose(a["L3_ffn_W2"], (0, 2, 1))).reshape(-1, P))], axis=1)
    cols = np.concatenate([
        short_col(a["L0_ffn_router_b1"]), col(a["L0_ffn_expert_b1"]), col(a["L0_ffn_expert_b2"]), short_col(a[g + "b_se"]),
        *[col(a[g + n]) for n in ("bn1_g", "bn1_b", "bn1_m", "bn1_v", "bn2_g", "bn2_b", "bn2_m", "bn2_v", "b_ih", "b_hh")],
        col(a[f + "b1"]), col(a["L2_ffn_b1s"]), col(a["L2_ffn_b1p"]), col(a["L3_ffn_b1"])], axis=1)
    arrays = {
        "x": a["x"], "adj": a["adj"], "nodemask": a["nodemask"], "edge_index": a["L1_ffn_edge_index"],
        "weights_a": weights_a, "weights_c": weights_c, "cols": cols,
        "rows": np.concatenate([a[n] for n in ("L0_gnn_bias", "L0_ffn_router_b2", g + "b_msg", "L2_gnn_b_rel", "L3_ffn_bg")]),
        "spread": np.concatenate([a["L0_gnn_prelu_a"].reshape(1)] + [a[n].reshape(-1) for n in (
            f + "att_src", f + "att_dst", f + "b_gat", f + "ln_gamma", f + "ln_beta", "L2_gnn_ln_gamma", "L2_gnn_ln_beta")]),
        "rw2": a["L0_ffn_router_w2"], "eb3": a["L0_ffn_expert_b3"], "f1_b2": a[f + "b2"],
        "f2_b2": np.concatenate([a["L2_ffn_b2s"].reshape(1, P), a["L2_ffn_b2p"]], axis=0), "f3_b2": a["L3_ffn_b2"]}
    arrays = {k: np.ascontiguousarray(v) for k, v in arrays.items()}
    nc = bacc.Bacc("TRN2", target_bir_lowering=False, num_devices=1)
    d = {k: nc.dram_tensor(f"in_{k}", v.shape, mybir.dt.from_np(v.dtype), kind="ExternalInput").ap() for k, v in arrays.items()}
    d["out"] = nc.dram_tensor("out", a["x"].shape, F32, kind="ExternalOutput").ap()
    program(nc, d)
    result = run_bass_kernel_spmd(nc, [{f"in_{k}": v for k, v in arrays.items()}], core_ids=[0])
    return result.results[0]["out"]
```

```python
from contextlib import ExitStack

import concourse.bass as bass
from concourse import mybir

F32, I32, U32 = mybir.dt.float32, mybir.dt.int32, mybir.dt.uint32
ALU, ACT, AX = mybir.AluOpType, mybir.ActivationFunctionType, mybir.AxisListType
RMAX = bass.bass_isa.ReduceOp.max

P = 128
D = 128
NODES = 64 * P
NT = NODES // P
NT_BITS, P_BITS = 6, 7
RANK_MAX = 4095.0
NT1 = NT + 1
GT = 4
GROUPS = NT // GT
LN_EPS = 1e-5
BIG = 1e30

EXPERTS0, ROUTER_H = 6, 64
CONV_K, CONV_PAD = 17, 8
HEADS, EXPERTS1 = 4, 4
EXPERTS2, EXPERTS3 = 8, 8
EMAX = 9
ROW = HEADS * EXPERTS1 + 2 * HEADS
SLOPE = 0.2

E_TOTAL = 524288
SRC_BITS, DST_BITS = 13, 14
KEY_BASE = 0x10000000
SLOT_BITS = 5
SLOTS = 1 << SLOT_BITS
GROUP_BITS = 2
SLOT_GROUP = 1 << GROUP_BITS


def sort_edges(nc, env, edge_index):
    KA, KB = env.keys_a, env.keys_b
    start_of = env.start_of
    PER = E_TOTAL // P
    ROWBITS = PER.bit_length() - 1
    ALLBITS = E_TOTAL.bit_length() - 1

    with ExitStack() as ctx:
        sem = lambda n: ctx.enter_context(nc.semaphore(n))
        loaded, iota_done = sem("edges_loaded"), sem("iota_done")
        dve_step, flipped = sem("sort_dve_step"), sem("sort_flipped")
        trans, evac = sem("sort_blocks_transposed"), sem("sort_blocks_copied")
        stage_done = sem("sort_half_done")
        stored, first_loaded = sem("sorted_stored"), sem("row_firsts_loaded")
        want_l2, got_l2, want_l3, got_l3 = sem("l2_rows_ready"), sem("l2_rows_loaded"), sem("l3_rows_ready"), sem("l3_rows_loaded")
        start_ready, start_stored, start_loaded = sem("start_ready"), sem("start_stored"), sem("start_loaded")
        want_keys, got_keys, deg_ready, maxdeg_done = sem("key_rows_ready"), sem("key_rows_loaded"), sem("deg_ready"), sem("maxdeg_done")
        tail_set = sem("tail_keys_set")
        block = ctx.enter_context(nc.Block())

        phases = [("row", [(b, k) for k in range(1, ROWBITS) for b in range(k - 1, -1, -1)], None)]
        phases.append(("flip", None, 0))
        phases.append(("row", [(b, None) for b in range(ROWBITS - 1, -1, -1)], None))
        phases.append(("unflip", None, 0))
        for k in range(ROWBITS + 1, ALLBITS + 1):
            last = k == ALLBITS
            phases.append(("to_column", None, None))
            dirbit = None if last else k - ROWBITS
            phases.append(("column", [(b - ROWBITS, dirbit) for b in range(k - 1, ROWBITS - 1, -1)]
                           + [(b, dirbit) for b in range(ROWBITS - 1, 6, -1)], None))
            phases.append(("to_row", None, dirbit))
            phases.append(("row", [(b, None) for b in range(6, -1, -1)], None))
            if not last:
                phases.append(("unflip", None, dirbit))

        bufs = [KA, KB]
        plan, cur = [], 0
        for kind, steps, bit in phases:
            plan.append((kind, steps, bit, cur))
            cur ^= (len(steps) if steps else 1) & 1
        final = bufs[cur]

        def free_view(buf, a, b):
            hi, lo = max(a, b), min(a, b)
            v = buf[:, :].rearrange("p (h x m y l) -> p h x m y l", x=2, m=1 << (hi - lo - 1), y=2, l=1 << lo)
            if b > a:
                return lambda side, up: v[:, :, 1 - up, :, side, :]
            return lambda side, up: v[:, :, side, :, 1 - up, :]

        NBLK = PER // P
        GRP = 4

        @block.sync
        def _(sp):
            sp.dma_start(KA[:, :].bitcast(I32), edge_index[0, :].rearrange("(p f) -> p f", p=P)).then_inc(loaded, 16)
            sp.dma_start(KB[:, :].bitcast(I32), edge_index[1, :].rearrange("(p f) -> p f", p=P)).then_inc(loaded, 16)
            sp.wait_ge(stage_done, 1)
            sp.dma_start(env.sorted_dram[0:E_TOTAL].rearrange("(p f) -> p f", p=P), final[:, :]).then_inc(stored, 16)
            sp.dma_start(env.row_first_dram.rearrange("(p o) -> p o", o=1), final[:, 0:1]).then_inc(stored, 16)
            sp.dma_start(env.chunk_first_dram, env.chunk_first[:, :]).then_inc(stored, 16)
            sp.wait_ge(tail_set, 1)
            sp.dma_start(env.sorted_dram[E_TOTAL:E_TOTAL + SLOTS].rearrange("(o f) -> o f", o=1), env.tail_keys[0:1, :]).then_inc(stored, 16)
            sp.wait_ge(stored, 64)
            sp.dma_start(env.row_first[:, :], env.row_first_dram.partition_broadcast(P)).then_inc(first_loaded, 16)
            sp.wait_ge(start_ready, 1)
            sp.dma_start(env.start_dram[0:NT1 * P].rearrange("(t p) -> p t", p=P), start_of[:, :], allow_slow_non_contiguous=True).then_inc(start_stored, 16)
            sp.wait_ge(start_stored, 16)
            sp.dma_start(env.end_of[:, :], env.start_dram[1:NT * P + 1].rearrange("(t p) -> p t", p=P), allow_slow_non_contiguous=True).then_inc(start_loaded, 16)

        @block.gpsimd
        def _(pool):
            nc.gpsimd.iota(env.node_id[:, :], pattern=[[P, NT1]], base=0, channel_multiplier=1).then_inc(iota_done, 1)
            nc.gpsimd.iota(env.tile_id_i[:, :], pattern=[[1, NT]], base=0, channel_multiplier=0).then_inc(iota_done, 1)
            nc.gpsimd.iota(env.part_id[:, :], pattern=[[0, 1]], base=0, channel_multiplier=1).then_inc(iota_done, 1)
            pool.wait_ge(want_l2, 1)
            pool.wait_ge(stored, 64)
            for t in range(NT1):
                pool.indirect_dma_start(out=env.l2_rows[:, t, :], out_offset=None, in_=env.chunk_first_dram,
                                        in_offset=bass.IndirectOffsetOnAxis(ap=env.row_index[:, t:t + 1].bitcast(U32), axis=0),
                                        bounds_check=P - 1, oob_is_err=False).then_inc(got_l2, 16)
            pool.wait_ge(want_l3, 1)
            for t in range(NT1):
                pool.indirect_dma_start(out=env.l3_rows[:, t, :], out_offset=None,
                                        in_=env.sorted_dram[0:E_TOTAL].rearrange("(c f) -> c f", f=P),
                                        in_offset=bass.IndirectOffsetOnAxis(ap=env.chunk_index[:, t:t + 1].bitcast(U32), axis=0),
                                        bounds_check=E_TOTAL // P - 1, oob_is_err=False).then_inc(got_l3, 16)
            pool.wait_ge(want_keys, 1)
            for t in range(NT):
                for side in range(2):
                    pool.indirect_dma_start(out=env.key_rows[:, t, side * SLOTS:(side + 1) * SLOTS], out_offset=None,
                                            in_=env.sorted_dram.rearrange("(c f) -> c f", f=SLOTS),
                                            in_offset=bass.IndirectOffsetOnAxis(ap=env.key_row_index[:, side, t:t + 1].bitcast(U32), axis=0),
                                            bounds_check=E_TOTAL // SLOTS, oob_is_err=False).then_inc(got_keys, 16)
            pool.wait_ge(deg_ready, 1)
            nc.gpsimd.partition_all_reduce(env.deg_max[:, :], env.degree[:, :], P, RMAX).then_inc(maxdeg_done, 1)

        @block.tensor
        def _(pe):
            n = 0
            turns = 0
            for kind, steps, bit, at in plan:
                if kind not in ("to_column", "to_row"):
                    continue
                pe.wait_ge(flipped, turns + 1)
                turns += 1
                for g in range(NBLK // GRP):
                    if n >= 4:
                        pe.wait_ge(evac, n - 3)
                    for b in range(GRP):
                        c = g * GRP + b
                        ins = nc.tensor.transpose(env.bank[n % 4][:, b * P:(b + 1) * P], bufs[at][:, c * P:(c + 1) * P], env.ident[:, :])
                    ins.then_inc(trans, 1)
                    n += 1

        @block.scalar
        def _(act):
            n = 0
            act.wait_ge(sign_ready := env.sign_ready, 1)
            for kind, steps, bit, at in plan:
                if kind not in ("to_column", "to_row"):
                    continue
                for g in range(NBLK // GRP):
                    act.wait_ge(trans, n + 1)
                    dst = bufs[at ^ 1][:, g * GRP * P:(g + 1) * GRP * P]
                    if kind == "to_row" and bit is not None:
                        nc.scalar.activation(dst, env.bank[n % 4][:, :], ACT.Copy, scale=env.sign[:, bit:bit + 1]).then_inc(evac, 1)
                    else:
                        nc.scalar.activation(dst, env.bank[n % 4][:, :], ACT.Copy).then_inc(evac, 1)
                    n += 1

        @block.vector
        def _(dve):
            done = [0]

            def link(ins, count=1):
                done[0] += count
                ins.then_inc(dve_step, count)
                dve.wait_ge(dve_step, done[0])

            dve.wait_ge(iota_done, 3)
            link(nc.vector.tensor_copy(env.tile_id[:, :], env.tile_id_i[:, :]))
            for b in range(7):
                nc.vector.tensor_scalar(env.sign_i[:, b:b + 1], env.part_id[:, :], b, 1, ALU.logical_shift_right, ALU.bitwise_and).then_inc(dve_step, 1)
                done[0] += 1
            dve.wait_ge(dve_step, done[0])
            nc.vector.tensor_scalar(env.sign[:, :], env.sign_i[:, :], -2.0, 1.0, ALU.mult, ALU.add).then_inc(env.sign_ready, 1)
            nc.vector.memset(env.tail_i[:, :], (NODES << SRC_BITS) | KEY_BASE)
            dve.wait_ge(env.sign_ready, 1)
            ai, bi = KA[:, :].bitcast(I32), KB[:, :].bitcast(I32)
            dve.wait_ge(loaded, 32)
            link(nc.vector.tensor_scalar(ai, ai, NODES - 1, None, ALU.min))
            link(nc.vector.tensor_scalar(bi, bi, NODES, None, ALU.min))
            link(nc.vector.tensor_scalar(bi, bi, SRC_BITS, KEY_BASE, ALU.logical_shift_left, ALU.bitwise_or))
            link(nc.vector.tensor_tensor(ai, ai, bi, ALU.bitwise_or))
            turns = 0
            for kind, steps, bit, at in plan:
                if kind in ("row", "column"):
                    for a, b in steps:
                        src, dst = bufs[at], bufs[at ^ 1]
                        if b is None:
                            s = src[:, :].rearrange("p (h x l) -> p h x l", x=2, l=1 << a)
                            d = dst[:, :].rearrange("p (h x l) -> p h x l", x=2, l=1 << a)
                            nc.vector.tensor_tensor(d[:, :, 0, :], s[:, :, 0, :], s[:, :, 1, :], ALU.min).then_inc(dve_step, 1)
                            nc.vector.tensor_tensor(d[:, :, 1, :], s[:, :, 0, :], s[:, :, 1, :], ALU.max).then_inc(dve_step, 1)
                            done[0] += 2
                        else:
                            s, d = free_view(src, a, b), free_view(dst, a, b)
                            for up in (1, 0):
                                nc.vector.tensor_tensor(d(0, up), s(0, up), s(1, up), ALU.min if up else ALU.max).then_inc(dve_step, 1)
                                nc.vector.tensor_tensor(d(1, up), s(0, up), s(1, up), ALU.max if up else ALU.min).then_inc(dve_step, 1)
                            done[0] += 4
                        dve.wait_ge(dve_step, done[0])
                        at ^= 1
                elif kind in ("flip", "unflip"):
                    link(nc.vector.tensor_scalar(bufs[at ^ 1][:, :], bufs[at][:, :], env.sign[:, bit:bit + 1], None, ALU.mult))
                else:
                    dve.nop().then_inc(flipped, 1)
                    turns += 1
                    dve.wait_ge(evac, turns * NBLK // GRP)
            nc.vector.tensor_copy(env.chunk_first[:, :], final[:, ::P]).then_inc(stage_done, 1)
            dve.wait_ge(stage_done, 1)
            nc.vector.tensor_copy(env.tail_keys[:, :].bitcast(I32), env.tail_i[:, :]).then_inc(tail_set, 1)

            link(nc.vector.tensor_scalar(env.node_key[:, :], env.node_id[:, :], SRC_BITS, KEY_BASE, ALU.logical_shift_left, ALU.bitwise_or))
            key = env.node_key[:, :].bitcast(F32)

            def below(rows, width, count):
                cmp = env.search_cmp[:, :, 0:width]
                link(nc.vector.tensor_tensor(cmp, rows, key.unsqueeze(2).to_broadcast([P, NT1, width]), ALU.is_lt))
                link(nc.vector.tensor_reduce(count, cmp, AX.X, ALU.add))

            dve.wait_ge(first_loaded, 16)
            below(env.row_first[:, :].unsqueeze(1).to_broadcast([P, NT1, P]), P, env.cnt[:, :])
            link(nc.vector.tensor_scalar(env.row_f[:, :], env.cnt[:, :], -1.0, 0.0, ALU.add, ALU.max))
            nc.vector.tensor_copy(env.row_index[:, :], env.row_f[:, :]).then_inc(want_l2, 1)
            dve.wait_ge(got_l2, 16 * NT1)
            below(env.l2_rows[:, :, :], NBLK, env.cnt[:, :])
            link(nc.vector.tensor_scalar(env.cnt[:, :], env.cnt[:, :], -1.0, 0.0, ALU.add, ALU.max))
            link(nc.vector.scalar_tensor_tensor(env.row_f[:, :], env.row_f[:, :], float(NBLK), env.cnt[:, :], ALU.mult, ALU.add))
            nc.vector.tensor_copy(env.chunk_index[:, :], env.row_f[:, :]).then_inc(want_l3, 1)
            dve.wait_ge(got_l3, 16 * NT1)
            below(env.l3_rows[:, :, :], P, env.cnt[:, :])
            link(nc.vector.scalar_tensor_tensor(env.start_f[:, :], env.row_f[:, :], float(P), env.cnt[:, :], ALU.mult, ALU.add))
            link(nc.vector.tensor_copy(start_of[:, :], env.start_f[:, :]))
            dve.nop().then_inc(start_ready, 1)

            dve.wait_ge(start_loaded, 16)
            link(nc.vector.tensor_tensor(env.degree_in[:, :], env.end_of[:, :], start_of[:, 0:NT], ALU.subtract))
            rank = [env.rank_a, env.rank_b]
            link(nc.vector.tensor_scalar(rank[1][:, :], env.degree_in[:, :], RANK_MAX, float(NT), ALU.min, ALU.mult))
            link(nc.vector.tensor_tensor(rank[0][:, :], rank[1][:, :], env.tile_id[:, :], ALU.add))
            at = 0
            for k in range(1, NT_BITS + 1):
                for a in range(k - 1, -1, -1):
                    s_, d_ = rank[at], rank[at ^ 1]
                    if k == NT_BITS:
                        sv, dv = (t[:, :].rearrange("p (h x l) -> p h x l", x=2, l=1 << a) for t in (s_, d_))
                        nc.vector.tensor_tensor(dv[:, :, 0, :], sv[:, :, 0, :], sv[:, :, 1, :], ALU.min)
                        ins = nc.vector.tensor_tensor(dv[:, :, 1, :], sv[:, :, 0, :], sv[:, :, 1, :], ALU.max)
                    else:
                        sv, dv = free_view(s_, a, k), free_view(d_, a, k)
                        for up in (1, 0):
                            nc.vector.tensor_tensor(dv(0, up), sv(0, up), sv(1, up), ALU.min if up else ALU.max)
                            ins = nc.vector.tensor_tensor(dv(1, up), sv(0, up), sv(1, up), ALU.max if up else ALU.min)
                    link(ins)
                    at ^= 1
            link(nc.vector.tensor_copy(env.rank_i[:, :], rank[at][:, :]))
            link(nc.vector.tensor_scalar(env.rank_i[:, :], env.rank_i[:, :], NT - 1, None, ALU.bitwise_and))
            cube = [P, NT, NT]
            pick = env.pick
            link(nc.vector.tensor_copy(env.place_tile[:, :], env.rank_i[:, :]))
            link(nc.vector.tensor_tensor(pick, env.place_tile[:, :].unsqueeze(2).to_broadcast(cube), env.tile_id[:, :].unsqueeze(1).to_broadcast(cube), ALU.is_equal))
            for vals, out in ((start_of[:, 0:NT], env.start_f[:, 0:NT]), (env.degree_in[:, :], env.degree[:, :])):
                link(nc.vector.tensor_tensor(env.picked, pick, vals.unsqueeze(1).to_broadcast(cube), ALU.mult))
                link(nc.vector.tensor_reduce(out, env.picked, AX.X, ALU.add))
            link(nc.vector.tensor_copy(start_of[:, 0:NT], env.start_f[:, 0:NT]))
            link(nc.vector.tensor_scalar(env.node_id[:, 0:NT], env.rank_i[:, :], P_BITS, None, ALU.logical_shift_left))
            link(nc.vector.tensor_tensor(env.node_id[:, 0:NT], env.node_id[:, 0:NT], env.part_id[:, :].to_broadcast([P, NT]), ALU.bitwise_or))
            link(nc.vector.tensor_scalar(env.key_row_index[:, 0, :], start_of[:, 0:NT], SLOT_BITS, None, ALU.logical_shift_right))
            nc.vector.tensor_scalar(env.key_row_index[:, 1, :], env.key_row_index[:, 0, :], 1, None, ALU.add).then_inc(want_keys, 1)
            dve.wait_ge(got_keys, 16 * 2 * NT)
            rows, shift_bit = env.key_rows, env.shift_bit
            for b in range(SLOT_BITS - 1, -1, -1):
                link(nc.vector.tensor_scalar(shift_bit[:, :], start_of[:, 0:NT], b, 1, ALU.logical_shift_right, ALU.bitwise_and))
                w = SLOTS + (1 << b) - 1
                link(nc.vector.tensor_copy(env.shifted[:, :, 0:w], rows[:, :, (1 << b):(1 << b) + w]))
                link(nc.vector.copy_predicated(rows[:, :, 0:w], shift_bit[:, :].unsqueeze(2).to_broadcast([P, NT, w]), env.shifted[:, :, 0:w]))
            keyi = rows[:, :, 0:SLOTS].bitcast(I32)
            dst_i, src_i = env.slot_dst, env.slot_row
            link(nc.vector.tensor_scalar(dst_i[:, :, :], keyi, SRC_BITS, (1 << DST_BITS) - 1, ALU.logical_shift_right, ALU.bitwise_and))
            link(nc.vector.tensor_scalar(src_i[:, :, :], keyi, NODES - 1, None, ALU.bitwise_and))
            link(nc.vector.tensor_tensor(env.slot_penalty[:, :, :], dst_i[:, :, :], env.node_id[:, 0:NT].unsqueeze(2).to_broadcast([P, NT, SLOTS]), ALU.not_equal))
            link(nc.vector.scalar_tensor_tensor(src_i[:, :, :], env.slot_penalty[:, :, :], float(NODES), src_i[:, :, :], ALU.mult, ALU.add))
            link(nc.vector.tensor_scalar(env.slot_penalty[:, :, :], env.slot_penalty[:, :, :], -BIG, None, ALU.mult))
            dve.nop().then_inc(deg_ready, 1)
            dve.wait_ge(maxdeg_done, 1)
            link(nc.vector.tensor_scalar(env.tile_groups_f[:, :], env.deg_max[:, :], float(SLOTS), 1.0, ALU.min, ALU.max))
            link(nc.vector.tensor_scalar(env.tile_groups_f[:, :], env.tile_groups_f[:, :], float(SLOT_GROUP - 1), None, ALU.add))
            link(nc.vector.tensor_copy(env.tile_groups[:, :], env.tile_groups_f[:, :]))
            link(nc.vector.tensor_scalar(env.tile_groups[:, :], env.tile_groups[:, :], GROUP_BITS, None, ALU.logical_shift_right))
            link(nc.vector.tensor_scalar(env.tile_groups_f[:, :], env.deg_max[:, :], float(SLOTS - 1), None, ALU.add))
            link(nc.vector.tensor_copy(env.tile_rounds[:, :], env.tile_groups_f[:, :]))
            link(nc.vector.tensor_scalar(env.tile_rounds[:, :], env.tile_rounds[:, :], SLOT_BITS, None, ALU.logical_shift_right))


class Chain:
    def __init__(self, eng, sem, base, per):
        self.eng, self.sem, self.base, self.per, self.n = eng, sem, base, per, 0

    def __call__(self, ins):
        self.n += 1
        ins.then_inc(self.sem, 1)
        self.eng.wait_ge(self.sem, self.base + self.n)

    def end(self):
        assert self.n == self.per, (self.n, self.per)


ROUND_STEPS = 16
ROUNDS_IN = 128
ROUNDS_OUT = E_TOTAL // SLOTS // ROUNDS_IN


def attend(nc, env):
    with ExitStack() as ctx:
        sb = lambda n, s, d: ctx.enter_context(nc.sbuf_tensor(n, s, d))
        sem = lambda n: ctx.enter_context(nc.semaphore(n))
        G = sb("gathered", [P, 2, SLOTS, ROW], F32)
        E = sb("edge_logits", [P, 2, SLOTS + 1, HEADS], F32)
        W = sb("edge_weights", [P, 2, SLOTS + 1, HEADS], F32)
        PR = sb("weighted_rows", [P, SLOTS, HEADS * EXPERTS1], F32)
        mr, mn, ds_, s16 = (sb(n, [P, w], F32) for n, w in (("round_max", HEADS), ("new_max", HEADS), ("round_den", HEADS), ("round_sum", 16)))
        of_row = sb("of_row", [P, 2], I32)
        of_bits = sb("of_bits", [P, SLOT_BITS], I32)
        of_keys = sb("of_keys", [P, 2 * SLOTS], F32)
        of_tmp = sb("of_shifted", [P, 2 * SLOTS], F32)
        of_slot, of_pen = sb("of_slot_row", [P, SLOTS], I32), sb("of_penalty", [P, SLOTS], F32)
        of_dst = sb("of_dst", [P, SLOTS], I32)
        rows_in = [sem("rows_in_0"), sem("rows_in_1")]
        rows_used = [sem("rows_used_0"), sem("rows_used_1")]
        own_in = sem("own_rows_in")
        turn = sem("pool_turn")
        cleared, began, step, logits, weights = sem("gathered_cleared"), sem("state_ready"), sem("attend_step"), sem("logits_ready"), sem("weights_ready")
        of_index, of_keys_in, of_slots, of_rows_in = sem("of_index_ready"), sem("of_keys_in"), sem("of_slots_ready"), sem("of_rows_in")
        of_dma, of_step, of_logits, of_weights, of_done = sem("of_dma"), sem("of_step"), sem("of_logits_ready"), sem("of_weights_ready"), sem("of_round_done")
        block = ctx.enter_context(nc.Block())
        M, DEN, ACC = env.att_max, env.att_den, env.att_acc

        def gather(pool, dst, index, s):
            pool.indirect_dma_start(out=dst, out_offset=None, in_=env.table_dram,
                                    in_offset=bass.IndirectOffsetOnAxis(ap=index, axis=0),
                                    bounds_check=NODES - 1, oob_is_err=False).then_inc(s, 16)

        def further_rounds(eng, first, more):
            with eng.Fori(0, NT) as t:
                n = eng.value_load(env.tile_rounds[0:1, bass.ds(t, 1)], min_val=0, max_val=E_TOTAL // SLOTS)
                before = eng.value_load(env.rounds_before[0:1, bass.ds(t, 1)], min_val=0, max_val=E_TOTAL // SLOTS)
                with eng.If(n > 1):
                    first(t)
                    more(t, before + 1)
                    with eng.If(n > 2):
                        with eng.Fori(0, ROUNDS_OUT) as ro:
                            with eng.If(n > ro * ROUNDS_IN + 2):
                                with eng.Fori(0, ROUNDS_IN) as ri:
                                    r = ro * ROUNDS_IN + ri + 2
                                    with eng.If(n > r):
                                        more(t, before + r)

        @block.gpsimd
        def _(pool):
            nc.gpsimd.memset(G[:, :, :, :], 0.0).then_inc(cleared, 1)
            for t in range(NT):
                pool.indirect_dma_start(out=env.own_rows[:, t, :], out_offset=None, in_=env.table_dram,
                                        in_offset=bass.IndirectOffsetOnAxis(ap=env.node_id[:, t:t + 1].bitcast(U32), axis=0),
                                        bounds_check=NODES - 1, oob_is_err=False).then_inc(own_in, 16)
            pool.wait_ge(cleared, 1)
            with pool.Fori(0, NT // 2) as i:
                for u in range(2):
                    t = i * 2 + u
                    pool.wait_ge(rows_used[u], i + 1)
                    pool.sem_inc(turn, 1)
                    n = pool.value_load(env.tile_groups[0:1, bass.ds(t, 1)], min_val=0, max_val=SLOTS // SLOT_GROUP)
                    nc.gpsimd.tensor_copy(env.idx_now[:, u, :], env.slot_row[:, bass.ds(t, 1), :].rearrange("p o s -> p (o s)")).then_inc(env.idx_sem, 1)
                    pool.wait_ge(env.idx_sem, i * 2 + (u + 1))
                    pool.sem_inc(turn, 1)
                    for q in range(SLOTS // SLOT_GROUP):
                        with pool.If(n > q):
                            for j in range(q * SLOT_GROUP, (q + 1) * SLOT_GROUP):
                                gather(pool, G[:, u, j, :], env.idx_now[:, u, j:j + 1].bitcast(U32), rows_in[u])
            def more(c):
                pool.wait_ge(of_index, c)
                pool.sem_inc(turn, 1)
                for side in range(2):
                    pool.indirect_dma_start(out=of_keys[:, side * SLOTS:(side + 1) * SLOTS], out_offset=None,
                                            in_=env.sorted_dram.rearrange("(c f) -> c f", f=SLOTS),
                                            in_offset=bass.IndirectOffsetOnAxis(ap=of_row[:, side:side + 1].bitcast(U32), axis=0),
                                            bounds_check=E_TOTAL // SLOTS, oob_is_err=False).then_inc(of_dma, 16)
                pool.wait_ge(of_dma, 32)
                pool.dma_reset(range(of_dma.num, of_dma.num + 1))
                pool.sem_clear(of_dma)
                pool.sem_inc(of_keys_in, 1)
                pool.wait_ge(of_slots, c)
                pool.sem_inc(turn, 1)
                for j in range(SLOTS):
                    gather(pool, G[:, 0, j, :], of_slot[:, j:j + 1].bitcast(U32), of_dma)
                pool.wait_ge(of_dma, 16 * SLOTS)
                pool.dma_reset(range(of_dma.num, of_dma.num + 1))
                pool.sem_clear(of_dma)
                pool.sem_inc(of_rows_in, 1)

            further_rounds(pool, lambda t: None, lambda t, c: more(c))

        @block.scalar
        def _(act):
            with act.Fori(0, NT // 2) as i:
                for u in range(2):
                    act.wait_ge(logits, i * 2 + (u + 1))
                    nc.scalar.activation(W[:, u, :, :], E[:, u, :, :], ACT.Exp).then_inc(weights, 1)
            def more(t, c):
                act.wait_ge(of_logits, c)
                nc.scalar.activation(W[:, 0, :, :], E[:, 0, :, :], ACT.Exp).then_inc(of_weights, 1)

            further_rounds(act, lambda t: None, more)

        @block.vector
        def _(dve):
            setup = Chain(dve, began, 0, 12)
            own = env.own_rows
            dve.wait_ge(own_in, 16 * NT)
            setup(nc.vector.tensor_tensor(M[:, :, :], own[:, :, 16:20], own[:, :, 20:ROW], ALU.add))
            setup(nc.vector.scalar_tensor_tensor(M[:, :, :], M[:, :, :], SLOPE, M[:, :, :], ALU.mult, ALU.max))
            setup(nc.vector.memset(DEN[:, :, :], 1.0))
            setup(nc.vector.tensor_copy(ACC[:, :, :], own[:, :, 0:16]))
            setup(nc.vector.tensor_scalar(env.rounds_f[:, :], env.tile_rounds[:, :], -1.0, 0.0, ALU.add, ALU.max))
            setup(nc.vector.tensor_tensor_scan(env.rounds_f2[:, 1:NT + 1], env.ones_nt[:, :], env.rounds_f[:, :], 0.0, ALU.mult, ALU.add))
            setup(nc.vector.tensor_copy(env.rounds_before[:, 1:NT], env.rounds_f2[:, 1:NT]))
            groups = env.tile_groups[:, :].rearrange("p (i u) -> p u i", u=2)
            for u in range(2):
                setup(nc.vector.tensor_scalar(env.groups_f[:, u, :], groups[:, u, :], float(16 * SLOT_GROUP), None, ALU.mult))
                setup(nc.vector.tensor_tensor_scan(env.groups_sum[:, u, :], env.ones_nt[:, 0:NT // 2], env.groups_f[:, u, :], 0.0, ALU.mult, ALU.add))
            setup(nc.vector.tensor_copy(env.rows_due[:, :, :], env.groups_sum[:, :, :]))
            setup.end()

            def weigh(link, t, u, penalty, slots_sem, slots_count, logits_sem, weights_sem, count):
                g, e, w = G[:, u, :, :], E[:, u, 0:SLOTS, :], W[:, u, 0:SLOTS, :]
                m, den, acc = M[:, bass.ds(t, 1), :], DEN[:, bass.ds(t, 1), :], ACC[:, bass.ds(t, 1), :]
                m, den, acc = (v.rearrange("p o h -> p (o h)") for v in (m, den, acc))
                ad = env.own_rows[:, bass.ds(t, 1), 20:ROW].to_broadcast([P, SLOTS, HEADS])
                dve.wait_ge(slots_sem, slots_count)
                link(nc.vector.tensor_tensor(e, g[:, :, 16:20], ad, ALU.add))
                link(nc.vector.tensor_tensor(e, e, penalty.unsqueeze(2).to_broadcast([P, SLOTS, HEADS]), ALU.add))
                link(nc.vector.scalar_tensor_tensor(e, e, SLOPE, e, ALU.mult, ALU.max))
                link(nc.vector.tensor_reduce(mr[:, :], e.rearrange("p j h -> p h j"), AX.X, ALU.max))
                link(nc.vector.tensor_tensor(mn[:, :], m, mr[:, :], ALU.max))
                link(nc.vector.tensor_tensor(E[:, u, SLOTS, :], m, mn[:, :], ALU.subtract))
                link(nc.vector.tensor_tensor(m, m, mr[:, :], ALU.max))
                nc.vector.tensor_tensor(e, e, mn[:, :].unsqueeze(1).to_broadcast([P, SLOTS, HEADS]), ALU.subtract).then_inc(logits_sem, 1)
                dve.wait_ge(weights_sem, count)
                fade = W[:, u, SLOTS, :]
                link(nc.vector.tensor_reduce(ds_[:, :], w.rearrange("p j h -> p h j"), AX.X, ALU.add))
                link(nc.vector.tensor_tensor(den, den, fade, ALU.mult))
                link(nc.vector.tensor_tensor(den, den, ds_[:, :], ALU.add))
                link(nc.vector.tensor_tensor(PR[:, :, :].rearrange("p j (h x) -> p j h x", x=EXPERTS1),
                                             g[:, :, 0:16].rearrange("p j (h x) -> p j h x", x=EXPERTS1),
                                             w.unsqueeze(3).to_broadcast([P, SLOTS, HEADS, EXPERTS1]), ALU.mult))
                link(nc.vector.tensor_reduce(s16[:, :], PR[:, :, :].rearrange("p j f -> p f j"), AX.X, ALU.add))
                av = acc.rearrange("p (h x) -> p h x", x=EXPERTS1)
                link(nc.vector.tensor_tensor(av, av, fade.unsqueeze(2).to_broadcast([P, HEADS, EXPERTS1]), ALU.mult))
                link(nc.vector.tensor_tensor(acc, acc, s16[:, :], ALU.add))

            dve.wait_ge(cleared, 1)
            for u in range(2):
                nc.vector.nop().then_inc(rows_used[u], 1)
            with dve.Fori(0, NT // 2) as i:
                for u in range(2):
                    t = i * 2 + u
                    link = Chain(dve, step, i * (2 * ROUND_STEPS) + u * ROUND_STEPS, ROUND_STEPS)
                    pen = env.slot_penalty[:, bass.ds(t, 1), :].rearrange("p o s -> p (o s)")
                    due = dve.value_load(env.rows_due[0:1, u, bass.ds(i, 1)], min_val=16 * SLOT_GROUP, max_val=16 * SLOTS * NT // 2)
                    weigh(link, t, u, pen, rows_in[u], due, logits, weights, i * 2 + (u + 1))
                    link(dve.nop())
                    nc.vector.nop().then_inc(rows_used[u], 1)
                    link(dve.nop())
                    link.end()
            def first(t):
                link = Chain(dve, of_step, 0, SLOT_BITS + 2)
                start = env.start_of[:, bass.ds(t, 1)]
                for b in range(SLOT_BITS):
                    link(nc.vector.tensor_scalar(of_bits[:, b:b + 1], start, b, 1, ALU.logical_shift_right, ALU.bitwise_and))
                link(nc.vector.tensor_scalar(of_row[:, 0:1], start, SLOT_BITS, None, ALU.logical_shift_right))
                link(nc.vector.tensor_scalar(of_row[:, 1:2], of_row[:, 0:1], 1, None, ALU.add))
                link.end()
                dve.sem_clear(of_step)

            def more(t, c):
                link = Chain(dve, of_step, 0, 2 * SLOT_BITS + 5 + 14)
                nc.vector.tensor_scalar(of_row[:, :], of_row[:, :], 1.0, float(E_TOTAL // SLOTS), ALU.add, ALU.min).then_inc(of_index, 1)
                dve.wait_ge(of_keys_in, c)
                for b in range(SLOT_BITS - 1, -1, -1):
                    w = SLOTS + (1 << b) - 1
                    link(nc.vector.tensor_copy(of_tmp[:, 0:w], of_keys[:, (1 << b):(1 << b) + w]))
                    link(nc.vector.copy_predicated(of_keys[:, 0:w], of_bits[:, b:b + 1].to_broadcast([P, w]), of_tmp[:, 0:w]))
                ki = of_keys[:, 0:SLOTS].bitcast(I32)
                link(nc.vector.tensor_scalar(of_dst[:, :], ki, SRC_BITS, (1 << DST_BITS) - 1, ALU.logical_shift_right, ALU.bitwise_and))
                link(nc.vector.tensor_scalar(of_slot[:, :], ki, NODES - 1, None, ALU.bitwise_and))
                link(nc.vector.tensor_tensor(of_pen[:, :], of_dst[:, :], env.node_id[:, bass.ds(t, 1)].to_broadcast([P, SLOTS]), ALU.not_equal))
                link(nc.vector.scalar_tensor_tensor(of_slot[:, :], of_pen[:, :], float(NODES), of_slot[:, :], ALU.mult, ALU.add))
                link(nc.vector.tensor_scalar(of_pen[:, :], of_pen[:, :], -BIG, None, ALU.mult))
                dve.sem_inc(of_slots, 1)
                weigh(link, t, 0, of_pen[:, :], of_rows_in, c, of_logits, of_weights, c)
                link.end()
                dve.sem_clear(of_step)

            further_rounds(dve, first, more)
            fin = Chain(dve, env.att_fin, 0, 4)
            fin(nc.vector.tensor_scalar(DEN[:, :, :], DEN[:, :, :], 1e-16, None, ALU.add))
            fin(nc.vector.reciprocal(DEN[:, :, :], DEN[:, :, :]))
            a4 = ACC[:, :, :].rearrange("p t (h x) -> p (t h) x", x=EXPERTS1)
            fin(nc.vector.tensor_tensor(a4, a4, DEN[:, :, :].rearrange("p t h -> p (t h)").unsqueeze(2).to_broadcast([P, NT * HEADS, EXPERTS1]), ALU.mult))
            fin(nc.vector.tensor_tensor(ACC[:, :, :], ACC[:, :, :], env.b_gat[:, :].unsqueeze(1).to_broadcast([P, NT, 16]), ALU.add))


class Steps:
    def __init__(self, eng, done, names):
        self.done, self.names, self.next, self.eng = done, list(names), 0, eng
        self.index = {n: k for k, n in enumerate(self.names)}
        assert len(self.index) == len(self.names)
        self.per = len(self.names)

    def begin(self, eng):
        eng.sem_inc(self.done, self.per)

    def did(self, ins, name):
        assert self.names[self.next % self.per] == name, (self.names[self.next % self.per], name)
        self.next += 1
        ins.then_inc(self.done, 1)

    def count(self, name, i):
        return i * self.per + (self.per + self.index[name] + 1)


class Link:
    def __init__(self, eng, sem, i, per):
        self.eng, self.sem, self.base, self.per, self.n = eng, sem, i * per, per, 0

    def __call__(self, ins):
        self.n += 1
        ins.then_inc(self.sem, 1)
        self.eng.wait_ge(self.sem, self.base + self.n)

    def end(self):
        self.eng.sem_inc(self.sem, self.per - self.n)
        self.eng.wait_ge(self.sem, self.base + self.per)


class Norms:
    def __init__(self, nc, env, ready, done, per):
        self.nc, self.env, self.ready, self.done, self.per, self.k, self.i = nc, env, ready, done, per, 0, 0

    def invert(self, dve, ins):
        self.k += 1
        ins.then_inc(self.ready, 1)
        dve.wait_ge(self.done, self.i * self.per + self.k)

    def serve(self, pool, i):
        for k in range(self.per):
            pool.wait_ge(self.ready, i * self.per + (k + 1))
            self.nc.gpsimd.tensor_tensor(self.env.ln_rstd[:, :], self.env.ln_var[:, :], self.env.minus_half[:, 0:GT], ALU.pow).then_inc(self.done, 1)


def bcast(ap, shape, axis):
    return ap.unsqueeze(axis).to_broadcast(shape)


def layer_norm(nc, env, link, x, out, scale_shift=None):
    st, mv = env.ln_stats, env.ln_mv
    for j in range(GT):
        ins = nc.vector.bn_stats(st[:, j, :], x[:, j, :])
    link(ins)
    link.eng.sem_inc(env.pause, 1)
    for j in range(GT):
        ins = nc.vector.bn_aggr(mv[:, j, :], st[:, j, :])
    link(ins)
    env.norms.invert(link.eng, nc.vector.tensor_scalar(env.ln_var[:, :], mv[:, :, 1], LN_EPS, None, ALU.add))
    for j in range(GT):
        ins = nc.vector.tensor_scalar(out[:, j, :], x[:, j, :], mv[:, j, 0:1], env.ln_rstd[:, j:j + 1], ALU.subtract, ALU.mult)
    if scale_shift is not None:
        link(ins)
        link(nc.vector.tensor_tensor(out, out, bcast(scale_shift[0], [P, GT, D], 1), ALU.mult))
        ins = nc.vector.tensor_tensor(out, out, bcast(scale_shift[1], [P, GT, D], 1), ALU.add)
    return ins


def top_two(nc, env, link, scores, n, tiles, tmp):
    shape = [P, tiles, n]
    full = lambda t: t[:, 0:tiles, 0:n]
    one = lambda t: t[:, 0:tiles]

    def mark(vals, top, where):
        link(nc.vector.tensor_reduce(one(top), vals, AX.X, ALU.max))
        link(nc.vector.tensor_tensor(full(tmp.tie), vals, bcast(one(top), shape, 2), ALU.is_equal))
        link(nc.vector.tensor_tensor(full(tmp.tie), full(tmp.tie), bcast(env.earlier[:, 0:n], shape, 1), ALU.mult))
        link(nc.vector.tensor_reduce(one(tmp.best), full(tmp.tie), AX.X, ALU.max))
        link(nc.vector.tensor_tensor(full(where), full(tmp.tie), bcast(one(tmp.best), shape, 2), ALU.is_equal))

    mark(scores, tmp.max1, tmp.first)
    link(nc.vector.scalar_tensor_tensor(full(tmp.rest), full(tmp.first), -BIG, scores, ALU.mult, ALU.add))
    mark(full(tmp.rest), tmp.max2, tmp.second)
    return nc.vector.tensor_tensor(one(tmp.diff), one(tmp.max2), one(tmp.max1), ALU.subtract)


def gate_weights(nc, link, out, n, tiles, tmp):
    shape = [P, tiles, n]
    full = lambda t: t[:, 0:tiles, 0:n]
    one = lambda t: t[:, 0:tiles]
    link(nc.vector.tensor_scalar(one(tmp.w1), one(tmp.diff_exp), 1.0, None, ALU.add))
    link(nc.vector.reciprocal(one(tmp.w1), one(tmp.w1)))
    link(nc.vector.tensor_tensor(one(tmp.w2), one(tmp.diff_exp), one(tmp.w1), ALU.mult))
    link(nc.vector.tensor_tensor(full(tmp.first), full(tmp.first), bcast(one(tmp.w1), shape, 2), ALU.mult))
    link(nc.vector.tensor_tensor(full(tmp.second), full(tmp.second), bcast(one(tmp.w2), shape, 2), ALU.mult))
    return nc.vector.tensor_tensor(out, full(tmp.first), full(tmp.second), ALU.add)


def turn(nc, bank, src, ident, n=P):
    for j in range(GT):
        ins = nc.tensor.transpose(bank[0:n, j * P:(j + 1) * P], src[:, j, 0:n], ident[:, :])
    return ins


def copy(nc, out, in_):
    return nc.vector.tensor_scalar(out, in_, 1.0, None, ALU.mult)


def tiles_of(ap):
    return ap.rearrange("p (j n) -> p j n", j=GT)


def phase_a(nc, env):
    N0 = EXPERTS0
    tensor_names = (["adjT", "l0agg", "l0out", "xt1", "rh", "lg"]
                    + [s for t in range(N0 + 2) for s in ([f"u1_{t}"] if t < N0 else []) + ([f"u2_{t-1}"] if 0 < t <= N0 else []) + ([f"y_{t-2}"] if t >= 2 else [])]
                    + ["gt", "gb", "xt2", "c1", "se", "dist", "sqm", "msg", "c2", "nmp", "ghn", "r", "z", "gin", "ot", "xt3", "hh"])
    scalar_names = (["adjT", "l0agg", "xt1", "rh", "l0exp", "g0exp"]
                    + [s for t in range(N0 + 1) for s in ([f"h1_{t}"] if t < N0 else []) + ([f"h2_{t-1}"] if t > 0 else [])]
                    + ["gt", "xt2", "se", "se2", "sq", "c1", "nsq", "ex", "ms", "nmp", "xc", "r", "z", "nn", "xt3"])
    vector_names = ["xh0", "l0out", "xh1", "lg", "probs_in", "g0diff", "gate"] + [f"comb_{e}" for e in range(N0)] + ["gb", "xh2", "att", "cv", "t1", "o", "ot", "xh3", "rows"]
    LINKS = 128

    with ExitStack() as ctx:
        sb = lambda n, s: ctx.enter_context(nc.sbuf_tensor("a_" + n, s, F32))
        sem = lambda n: ctx.enter_context(nc.semaphore("a_" + n))
        ten, sca, vec = (Steps(None, sem(n), s) for n, s in (("tensor_step", tensor_names), ("scalar_step", scalar_names), ("vector_step", vector_names)))
        link_sem, adj_in, rows_out, margins = sem("vector_link"), sem("adj_loaded"), sem("rows_stored"), sem("margins_cleared")
        X, XH, ADJ, ADJT = (sb(n, [P, GT, D]) for n in ("x", "xh", "adj", "adjt"))
        AG, XT, CV, XC, NMP, R, Z, NN, O, T1 = (sb(n, [P, GT * P]) for n in ("ag", "xt", "cv", "xc", "nmp", "r", "z", "nn", "o", "t1"))
        U, EX, MS = (sb(n, [P, GT, D]) for n in ("u", "ex", "ms"))
        H1 = [sb(f"h1_{k}", [P, GT * P]) for k in range(2)]
        H2 = [sb(f"h2_{k}", [P, GT * P]) for k in range(2)]
        RH = sb("rh", [ROUTER_H, GT * P])
        GTR = sb("gate_rows", [N0, GT * P])
        LG, PB, GATE = (sb(n, [P, GT, N0]) for n in ("lg", "pb", "gate"))
        lsum = sb("lsum", [P, GT])
        H1P = sb("h1p", [P, GT, P + 2 * CONV_PAD])
        SE, SE2, SQ = (sb(n, [3, GT * P]) for n in ("se", "se2", "sq"))
        NSQ = sb("nsq", [P, GT])
        ROWL = sb("rows", [P, GT, ROW])
        PROD = sb("prod", [P, GT, 16])
        B = env.bank
        U1, U2, Y = (B[1], B[2]), (B[3], B[4]), (B[5], B[6])
        env.norms = norms = Norms(nc, env, sem("var_ready"), sem("rstd_ready"), 4)
        block = ctx.enter_context(nc.Block())
        adj_v = env.adj_dram

        @block.sync
        def _(sp):
            with sp.Fori(0, GROUPS) as i:
                sp.wait_ge(ten.done, ten.count("adjT", i - 1))
                sp.dma_start(ADJ[:, :, :], adj_v[bass.ds(i * GT, GT), :, :].rearrange("g n m -> n g m")).then_inc(adj_in, 16)
                sp.wait_ge(vec.done, vec.count("rows", i))
                sp.dma_start(env.table_dram[bass.ds(i * (GT * P), GT * P), :].rearrange("(t p) f -> p t f", p=P), ROWL[:, :, :]).then_inc(rows_out, 16)
            sp.wait_ge(rows_out, 16 * GROUPS)

        @block.gpsimd
        def _(pool):
            with pool.Fori(0, GROUPS) as i:
                norms.serve(pool, i)

        @block.tensor
        def _(pe):
            ten.begin(pe)
            mm = nc.tensor.matmul
            with pe.Fori(0, GROUPS) as i:
                after = lambda who, name: pe.wait_ge(who.done, who.count(name, i))
                pe.wait_ge(adj_in, i * 16 + 16)
                pe.wait_ge(sca.done, sca.count("xt3", i - 1))
                ten.did(turn(nc, B[0], ADJ, env.ident), "adjT")
                after(vec, "xh0")
                after(sca, "adjT")
                for j in range(GT):
                    ins = mm(B[1][:, j * P:(j + 1) * P], lhsT=XH[:, j, :], rhs=ADJT[:, j, :], start=j == 0, stop=j == GT - 1, skip_group_check=True)
                ten.did(ins, "l0agg")
                after(sca, "l0agg")
                for j in range(GT):
                    o = B[2][:, j * P:(j + 1) * P]
                    mm(o, lhsT=AG[:, j * P:(j + 1) * P], rhs=env.w("l0_w"), start=j == 0, stop=False, skip_group_check=True)
                    ins = mm(o, lhsT=env.ones[0:1, :], rhs=env.row("l0_bias"), start=False, stop=j == GT - 1, skip_group_check=True)
                ten.did(ins, "l0out")
                after(vec, "xh1")
                ten.did(turn(nc, B[0], XH, env.ident), "xt1")
                after(sca, "xt1")
                ten.did(mm(B[7][0:ROUTER_H, :], lhsT=env.w("rw1"), rhs=XT[:, :], start=True, stop=True), "rh")
                after(sca, "rh")
                for j in range(GT):
                    o = B[0][:, j * N0:(j + 1) * N0]
                    mm(o, lhsT=RH[:, j * P:(j + 1) * P], rhs=env.rw2[:, :], start=j == 0, stop=False, skip_group_check=True)
                    ins = mm(o, lhsT=env.ones[0:1, :], rhs=env.row("rb2"), start=False, stop=j == GT - 1, skip_group_check=True)
                ten.did(ins, "lg")
                for t in range(N0 + 2):
                    if t < N0:
                        if t >= 2:
                            after(sca, f"h1_{t-2}")
                        ten.did(mm(U1[t % 2][:, :], lhsT=env.w("ew1", t), rhs=XT[:, :], start=True, stop=True), f"u1_{t}")
                    if 0 < t <= N0:
                        after(sca, f"h1_{t-1}")
                        if t >= 3:
                            after(sca, f"h2_{t-3}")
                        ten.did(mm(U2[(t - 1) % 2][:, :], lhsT=env.w("ew2", t - 1), rhs=H1[(t - 1) % 2][:, :], start=True, stop=True), f"u2_{t-1}")
                    if t >= 2:
                        e = t - 2
                        after(sca, f"h2_{e}")
                        if e >= 2:
                            after(vec, f"comb_{e-2}")
                        for j in range(GT):
                            ins = mm(Y[e % 2][:, j * P:(j + 1) * P], lhsT=H2[e % 2][:, j * P:(j + 1) * P], rhs=env.w("ew3", e), start=j == 0, stop=j == GT - 1, skip_group_check=True)
                        ten.did(ins, f"y_{e}")
                after(vec, "gate")
                ten.did(turn(nc, B[7], GATE, env.ident, N0), "gt")
                after(sca, "gt")
                for j in range(GT):
                    ins = mm(B[0][:, j * P:(j + 1) * P], lhsT=GTR[:, j * P:(j + 1) * P], rhs=env.eb3[:, :], start=j == 0, stop=j == GT - 1, skip_group_check=True)
                ten.did(ins, "gb")
                after(vec, "xh2")
                ten.did(turn(nc, B[0], XH, env.ident), "xt2")
                after(sca, "xt2")
                ten.did(mm(B[1][:, :], lhsT=env.w("conv1"), rhs=XT[:, :], start=True, stop=True), "c1")
                ten.did(mm(B[7][0:3, :], lhsT=env.w("w_se"), rhs=XT[:, :], start=True, stop=True), "se")
                after(sca, "sq")
                for j in range(GT):
                    o, s = B[6][:, j * P:(j + 1) * P], slice(j * P, (j + 1) * P)
                    mm(o, lhsT=SE[:, s], rhs=SE2[:, s], start=j == 0, stop=False, skip_group_check=True)
                    ins = mm(o, lhsT=env.neg_ones[:, :], rhs=SQ[:, s], start=False, stop=j == GT - 1, skip_group_check=True)
                ten.did(ins, "dist")
                for j in range(GT):
                    ins = mm(B[7][:, j:j + 1], lhsT=SQ[:, j * P:(j + 1) * P], rhs=env.neg_ones[:, 0:1], start=j == 0, stop=j == GT - 1, skip_group_check=True)
                ten.did(ins, "sqm")
                for j in range(GT):
                    o = B[5][:, j * P:(j + 1) * P]
                    mm(o, lhsT=XT[:, j * P:(j + 1) * P], rhs=env.w("w_msg"), start=j == 0, stop=False, skip_group_check=True)
                    ins = mm(o, lhsT=env.ones[0:1, :], rhs=env.row("b_msg"), start=False, stop=j == GT - 1, skip_group_check=True)
                ten.did(ins, "msg")
                after(sca, "c1")
                for k in range(CONV_K):
                    ins = mm(tiles_of(B[2][:, :]), lhsT=env.w("conv2", k), rhs=H1P[:, :, k:k + P], start=k == 0, stop=k == CONV_K - 1)
                ten.did(ins, "c2")
                after(sca, "ms")
                after(vec, "att")
                for j in range(GT):
                    ins = mm(B[4][:, j * P:(j + 1) * P], lhsT=MS[:, j, :], rhs=EX[:, j, :], start=j == 0, stop=j == GT - 1, skip_group_check=True)
                ten.did(ins, "nmp")
                ten.did(mm(B[6][:, :], lhsT=env.w("w_hh", 2), rhs=XT[:, :], start=True, stop=True), "ghn")
                after(sca, "nmp")
                after(sca, "xc")
                for gate, bank in ((0, B[3]), (1, B[1]), (2, B[5])):
                    if gate < 2:
                        mm(bank[:, :], lhsT=env.w("w_hh", gate), rhs=XT[:, :], start=True, stop=False)
                    mm(bank[:, :], lhsT=env.w("w_ih", 3 + gate), rhs=NMP[:, :], start=gate == 2, stop=False)
                    ins = mm(bank[:, :], lhsT=env.w("w_ih", gate), rhs=XC[:, :], start=False, stop=True)
                    ten.did(ins, ("r", "z", "gin")[gate])
                after(vec, "o")
                ten.did(turn(nc, B[0], tiles_of(O[:, :]), env.ident), "ot")
                after(vec, "xh3")
                ten.did(turn(nc, B[0], XH, env.ident), "xt3")
                after(sca, "xt3")
                for j in range(GT):
                    ins = mm(B[7][:, j * 16:(j + 1) * 16], lhsT=XT[:, j * P:(j + 1) * P], rhs=env.w("w_gat"), start=j == 0, stop=j == GT - 1, skip_group_check=True)
                ten.did(ins, "hh")

        @block.scalar
        def _(act):
            act.wait_ge(margins, 1)
            sca.begin(act)
            go = nc.scalar.activation
            with act.Fori(0, GROUPS) as i:
                after = lambda who, name: act.wait_ge(who.done, who.count(name, i))
                after(ten, "adjT")
                act.wait_ge(vec.done, vec.count("att", i - 1))
                sca.did(go(ADJT[:, :, :], tiles_of(B[0][:, :]), ACT.Copy), "adjT")
                after(ten, "l0agg")
                sca.did(go(AG[:, :], B[1][:, :], ACT.Copy), "l0agg")
                after(ten, "xt1")
                sca.did(go(XT[:, :], B[0][:, :], ACT.Copy), "xt1")
                after(ten, "rh")
                sca.did(go(RH[:, :], B[7][0:ROUTER_H, :], ACT.Relu, bias=env.col("rb1")[0:ROUTER_H, :]), "rh")
                after(vec, "lg")
                sca.did(go(PB[:, :, :], LG[:, :, :], ACT.Exp), "l0exp")
                after(vec, "g0diff")
                sca.did(go(env.top.diff_exp[:, 0:GT], env.top.diff[:, 0:GT], ACT.Exp), "g0exp")
                for t in range(N0 + 1):
                    if t < N0:
                        after(ten, f"u1_{t}")
                        if t >= 2:
                            after(ten, f"u2_{t-2}")
                        sca.did(go(H1[t % 2][:, :], U1[t % 2][:, :], ACT.Relu, bias=env.col("eb1", t)), f"h1_{t}")
                    if t > 0:
                        after(ten, f"u2_{t-1}")
                        if t >= 3:
                            after(ten, f"y_{t-3}")
                        sca.did(go(H2[(t - 1) % 2][:, :], U2[(t - 1) % 2][:, :], ACT.Relu, bias=env.col("eb2", t - 1)), f"h2_{t-1}")
                after(ten, "gt")
                sca.did(go(GTR[:, :], B[7][0:N0, :], ACT.Copy), "gt")
                after(ten, "xt2")
                sca.did(go(XT[:, :], B[0][:, :], ACT.Copy), "xt2")
                after(ten, "se")
                sca.did(go(SE[:, :], B[7][0:3, :], ACT.Identity, bias=env.col("b_se")[0:3, :]), "se")
                act.wait_ge(sca.done, sca.count("se", i))
                sca.did(go(SE2[:, :], SE[:, :], ACT.Copy, scale=2.0), "se2")
                sca.did(go(SQ[:, :], SE[:, :], ACT.Square), "sq")
                sca.did(go(H1P[:, :, CONV_PAD:CONV_PAD + P], tiles_of(B[1][:, :]), ACT.Relu, bias=env.bn_shift[:, 0:1], scale=env.bn_scale[:, 0:1]), "c1")
                after(ten, "sqm")
                sca.did(go(NSQ[:, :], B[7][:, 0:GT], ACT.Copy), "nsq")
                act.wait_ge(sca.done, sca.count("nsq", i))
                for j in range(GT):
                    ins = go(EX[:, j, :], B[6][:, j * P:(j + 1) * P], ACT.Exp, bias=NSQ[:, j:j + 1])
                sca.did(ins, "ex")
                after(ten, "msg")
                sca.did(go(MS[:, :, :], tiles_of(B[5][:, :]), ACT.Relu), "ms")
                after(ten, "nmp")
                sca.did(go(NMP[:, :], B[4][:, :], ACT.Copy), "nmp")
                after(vec, "cv")
                sca.did(go(XC[:, :], CV[:, :], ACT.Relu, bias=env.bn_shift[:, 1:2]), "xc")
                after(ten, "r")
                sca.did(go(R[:, :], B[3][:, :], ACT.Tanh, bias=env.gru_bias[:, 0:1], scale=0.5), "r")
                after(ten, "z")
                sca.did(go(Z[:, :], B[1][:, :], ACT.Tanh, bias=env.gru_bias[:, 1:2], scale=0.5), "z")
                after(vec, "t1")
                sca.did(go(NN[:, :], T1[:, :], ACT.Tanh, bias=env.col("b_ih", 2)), "nn")
                after(ten, "xt3")
                sca.did(go(XT[:, :], B[0][:, :], ACT.Copy), "xt3")

        @block.vector
        def _(dve):
            v = nc.vector
            v.memset(H1P[:, :, :], 0.0).then_inc(margins, 1)
            dve.wait_ge(margins, 1)
            vec.begin(dve)
            with dve.Fori(0, GROUPS) as i:
                link = Link(dve, link_sem, i, LINKS)
                norms.i = i
                after = lambda who, name: dve.wait_ge(who.done, who.count(name, i))

                def did(ins, name):
                    vec.did(ins, name)
                    dve.wait_ge(vec.done, vec.count(name, i))

                tiles = bass.ds(i * GT, GT)
                link(copy(nc, X[:, :, :], env.x[:, tiles, :]))
                did(layer_norm(nc, env, link, X, XH[:, :, :]), "xh0")
                after(ten, "l0out")
                bank = tiles_of(B[2][:, :])
                link(v.tensor_scalar(U[:, :, :], bank, 0.0, env.prelu[:, :], ALU.min, ALU.mult))
                did(v.scalar_tensor_tensor(U[:, :, :], bank, 0.0, U[:, :, :], ALU.max, ALU.add), "l0out")
                link(v.tensor_tensor(X[:, :, :], X[:, :, :], U[:, :, :], ALU.add))
                did(layer_norm(nc, env, link, X, XH[:, :, :]), "xh1")
                after(ten, "lg")
                lg = B[0][:, 0:GT * N0].rearrange("p (j e) -> p j e", j=GT)
                s4 = [P, GT, N0]
                link(v.tensor_reduce(lsum[:, :], lg, AX.X, ALU.max))
                did(v.tensor_tensor(LG[:, :, :], lg, bcast(lsum[:, :], s4, 2), ALU.subtract), "lg")
                after(sca, "l0exp")
                link(v.tensor_reduce(lsum[:, :], PB[:, :, :], AX.X, ALU.add))
                link(v.reciprocal(lsum[:, :], lsum[:, :]))
                did(v.tensor_tensor(PB[:, :, :], PB[:, :, :], bcast(lsum[:, :], s4, 2), ALU.mult), "probs_in")
                did(top_two(nc, env, link, PB[:, :, :], N0, GT, env.top), "g0diff")
                after(sca, "g0exp")
                did(gate_weights(nc, link, GATE[:, :, :], N0, GT, env.top), "gate")
                for e in range(N0):
                    after(ten, f"y_{e}")
                    for j in range(GT):
                        ins = v.scalar_tensor_tensor(X[:, j, :], Y[e % 2][:, j * P:(j + 1) * P], GATE[:, j, e:e + 1], X[:, j, :], ALU.mult, ALU.add)
                    did(ins, f"comb_{e}")
                after(ten, "gb")
                did(v.tensor_tensor(X[:, :, :], X[:, :, :], tiles_of(B[0][:, :]), ALU.add), "gb")
                did(layer_norm(nc, env, link, X, XH[:, :, :]), "xh2")
                after(sca, "ex")
                did(v.tensor_tensor(EX[:, :, :], EX[:, :, :], ADJT[:, :, :], ALU.mult), "att")
                after(ten, "c2")
                did(v.scalar_tensor_tensor(CV[:, :], B[2][:, :], env.bn_scale[:, 1:2], XT[:, :], ALU.mult, ALU.add), "cv")
                after(sca, "r")
                link(v.tensor_scalar(R[:, :], R[:, :], 0.5, 0.5, ALU.mult, ALU.add))
                link(v.scalar_tensor_tensor(T1[:, :], B[6][:, :], env.col("b_hh", 2), R[:, :], ALU.add, ALU.mult))
                after(ten, "gin")
                did(v.tensor_tensor(T1[:, :], T1[:, :], B[5][:, :], ALU.add), "t1")
                after(sca, "nn")
                link(v.tensor_scalar(Z[:, :], Z[:, :], 0.5, 0.5, ALU.mult, ALU.add))
                link(v.tensor_tensor(O[:, :], XT[:, :], NN[:, :], ALU.subtract))
                link(v.tensor_tensor(O[:, :], O[:, :], Z[:, :], ALU.mult))
                did(v.tensor_tensor(O[:, :], O[:, :], NN[:, :], ALU.add), "o")
                after(ten, "ot")
                did(v.tensor_tensor(X[:, :, :], X[:, :, :], tiles_of(B[0][:, :]), ALU.add), "ot")
                link(copy(nc, env.x[:, tiles, :], X[:, :, :]))
                did(layer_norm(nc, env, link, X, XH[:, :, :]), "xh3")
                after(ten, "hh")
                hh = B[7][:, 0:GT * 16].rearrange("p (j f) -> p j f", j=GT)
                h4 = lambda t: t.rearrange("p j (h x) -> p (j h) x", x=EXPERTS1)
                link(v.tensor_copy(ROWL[:, :, 0:16], hh))
                link(v.tensor_tensor(PROD[:, :, :], ROWL[:, :, 0:16], bcast(env.att_src[:, :], [P, GT, 16], 1), ALU.mult))
                for j in range(GT):
                    ins = v.tensor_reduce(ROWL[:, j, 16:20], PROD[:, j, :].rearrange("p (h x) -> p h x", x=EXPERTS1), AX.X, ALU.add)
                link(ins)
                link(v.tensor_tensor(PROD[:, :, :], ROWL[:, :, 0:16], bcast(env.att_dst[:, :], [P, GT, 16], 1), ALU.mult))
                for j in range(GT):
                    ins = v.tensor_reduce(ROWL[:, j, 20:ROW], PROD[:, j, :].rearrange("p (h x) -> p h x", x=EXPERTS1), AX.X, ALU.add)
                did(ins, "rows")
                dve.wait_ge(rows_out, i * 16 + 16)
                link.end()


class Experts:
    def __init__(self, tag, experts, chunks, w1, w2, b1, b2, func):
        self.tag, self.experts, self.chunks, self.total = tag, experts, chunks, experts * chunks
        self.w1, self.w2, self.b1, self.b2, self.func = w1, w2, b1, b2, func

    def tensor_names(self):
        out = []
        for k in range(self.total + 1):
            out += [f"{self.tag}_up_{k}"] if k < self.total else []
            out += [f"{self.tag}_down_{k-1}"] if k > 0 else []
        return out + [f"{self.tag}_gt", f"{self.tag}_gb"]

    def scalar_names(self):
        return [f"{self.tag}_h_{k}" for k in range(self.total)] + [f"{self.tag}_gt"]

    def vector_names(self):
        return [f"{self.tag}_comb_{e}" for e in range(self.experts)] + [f"{self.tag}_gb"]


STREAMS = 2
TURNS = GROUPS // STREAMS


def by_stage(stages):
    return [f"{n}@{s}" for names in stages for s in range(STREAMS) for n in names]


class Stream:
    def __init__(self, sb, s, bank):
        w = lambda n: sb(f"{n}_{s}", [P, GT, D])
        self.s, self.turned = s, bank
        self.X, self.XH, self.ADJ, self.ADJT, self.SM, self.OUT, self.XT, self.AG = (w(n) for n in ("x", "xh", "adj", "adjt", "sim", "out", "xt", "ag"))
        self.GTR, self.GATE = sb(f"gate_rows_{s}", [EMAX, GT * P]), sb(f"gate_{s}", [P, GT, EMAX])
        self.nmx, self.ssum = sb(f"nmx_{s}", [P, GT]), sb(f"ssum_{s}", [P, GT])


def phase_c(nc, env):
    f1 = Experts("f1", EXPERTS1, 2, "f1_w1", "f1_w2", "f1_b1", env.f1_b2, ACT.Gelu)
    f2 = Experts("f2", EXPERTS2 + 1, 4, "f2_w1", "f2_w2", "f2_b1", env.f2_b2, ACT.Gelu)
    f3 = Experts("f3", EXPERTS3, 4, "f3_w1", "f3_w2", "f3_b1", env.f3_b2, ACT.Relu)
    tensor_names = by_stage([["f1_xt"] + f1.tensor_names(), ["g2_adjT", "g2_xt", "agg", "conv"], ["f2_xt", "f2_lg"] + f2.tensor_names(),
                             ["g3_xt", "inter", "sim"], ["pt", "ov"], ["f3_xt", "f3_lg"] + f3.tensor_names()])
    scalar_names = by_stage([["f1_xt"] + f1.scalar_names(), ["g2_adjT", "g2_xt", "agg"], ["f2_xt", "f2_exp"] + f2.scalar_names(),
                             ["g3_xt", "inter"], ["soft", "pt"], ["f3_xt", "f3_exp"] + f3.scalar_names()])
    vector_names = by_stage([["f1_xh"], f1.vector_names() + ["g2_xh"], ["conv", "f2_xh"], ["f2_diff", "f2_gate"] + f2.vector_names() + ["g3_xh"],
                             ["masked"], ["ov", "f3_xh"], ["f3_diff", "f3_gate"] + f3.vector_names() + ["out"]])
    LINKS = 300
    with ExitStack() as ctx:
        sb = lambda n, s, d=F32: ctx.enter_context(nc.sbuf_tensor("c_" + n, s, d))
        sem = lambda n: ctx.enter_context(nc.semaphore("c_" + n))
        ten, sca, vec = (Steps(None, sem(n), s) for n, s in (("tensor_step", tensor_names), ("scalar_step", scalar_names), ("vector_step", vector_names)))
        link_sem = sem("vector_link")
        adj_in, mask_in, stored = ([sem(f"{n}_{s}") for s in range(STREAMS)] for n in ("adj_loaded", "mask_loaded", "out_stored"))
        B = env.bank
        U, Y = (B[1], B[2], B[3]), (B[4], B[5])
        streams = [Stream(sb, s, (B[0], B[6])[s]) for s in range(STREAMS)]
        H = [sb(f"h_{k}", [P, GT * P]) for k in range(3)]
        LG, mx = sb("lg", [P, GT, EMAX]), sb("mx", [P, GT])
        MI = [sb(f"mask_int_{s}", [P, GT, P], I32) for s in range(STREAMS)]
        MK, MB = sb("mask", [P, GT, P]), sb("mask_bias", [P, GT, P])
        env.norms = norms = Norms(nc, env, sem("var_ready"), sem("rstd_ready"), 6 * STREAMS)
        flat = lambda t: t[:, :, :].rearrange("p j n -> p (j n)")
        block = ctx.enter_context(nc.Block())

        @block.gpsimd
        def _(pool):
            with pool.Fori(0, TURNS) as i:
                norms.serve(pool, i)

        @block.sync
        def _(sp):
            with sp.Fori(0, TURNS) as i:
                for st in streams:
                    s = st.s
                    graphs = bass.ds(i * (STREAMS * GT) + s * GT, GT)
                    sp.wait_ge(vec.done, vec.count(f"masked@{s}", i - 1))
                    sp.dma_start(st.ADJ[:, :, :], env.adj_dram[graphs, :, :].rearrange("g n m -> n g m")).then_inc(adj_in[s], 16)
                    sp.dma_start(MI[s][:, :, :], env.mask_dram[graphs, :].partition_broadcast(P)).then_inc(mask_in[s], 16)
                for st in streams:
                    s = st.s
                    graphs = bass.ds(i * (STREAMS * GT) + s * GT, GT)
                    sp.wait_ge(vec.done, vec.count(f"out@{s}", i))
                    sp.dma_start(env.out_dram[graphs, :, :].rearrange("g n d -> n g d"), st.OUT[:, :, :]).then_inc(stored[s], 16)
            for s in range(STREAMS):
                sp.wait_ge(stored[s], 16 * TURNS)

        @block.tensor
        def _(pe):
            ten.begin(pe)
            mm = nc.tensor.matmul
            with pe.Fori(0, TURNS) as i:
                after = lambda who, name, at=0: pe.wait_ge(who.done, who.count(name, i + at))

                def turned(st, name):
                    after(vec, f"{name}h@{st.s}")
                    ten.did(turn(nc, st.turned, st.XH, env.ident), f"{name}t@{st.s}")
                    after(sca, f"{name}t@{st.s}")

                def experts(st, f, out_free):
                    s, XT = st.s, flat(st.XT)
                    for k in range(f.total + 1):
                        if k < f.total:
                            if k >= 3:
                                after(sca, f"{f.tag}_h_{k-3}@{s}")
                            ten.did(mm(U[k % 3][:, :], lhsT=env.w(f.w1, k), rhs=XT, start=True, stop=True), f"{f.tag}_up_{k}@{s}")
                        if k > 0:
                            c = k - 1
                            e, part = divmod(c, f.chunks)
                            after(sca, f"{f.tag}_h_{c}@{s}")
                            if c == 0:
                                after(vec, *out_free)
                            if part == 0 and e >= 2:
                                after(vec, f"{f.tag}_comb_{e-2}@{s}")
                            for j in range(GT):
                                ins = mm(Y[e % 2][:, j * P:(j + 1) * P], lhsT=H[c % 3][:, j * P:(j + 1) * P], rhs=env.w(f.w2, c),
                                         start=j == 0 and part == 0, stop=j == GT - 1 and part == f.chunks - 1, skip_group_check=True)
                            ten.did(ins, f"{f.tag}_down_{c}@{s}")
                    if f.tag != "f1":
                        after(vec, f"{f.tag}_gate@{s}")
                    ten.did(turn(nc, B[7], st.GATE, env.ident, f.experts), f"{f.tag}_gt@{s}")
                    after(sca, f"{f.tag}_gt@{s}")
                    for j in range(GT):
                        ins = mm(st.turned[:, j * P:(j + 1) * P], lhsT=st.GTR[0:f.experts, j * P:(j + 1) * P], rhs=f.b2[:, :], start=j == 0, stop=j == GT - 1, skip_group_check=True)
                    ten.did(ins, f"{f.tag}_gb@{s}")

                def free_after(st, f, name, before=0):
                    return (f"{name}@1", before) if st.s == 0 else (f"{f.tag}_comb_{f.experts - 1}@0",)

                def router(st, f, n, w, bias):
                    XT = flat(st.XT)
                    for j in range(GT):
                        o = B[7][:, j * n:(j + 1) * n]
                        ins = mm(o, lhsT=XT[:, j * P:(j + 1) * P], rhs=env.w(w), start=j == 0, stop=bias is None and j == GT - 1, skip_group_check=True)
                        if bias is not None:
                            ins = mm(o, lhsT=env.ones[0:1, :], rhs=env.row(bias), start=False, stop=j == GT - 1, skip_group_check=True)
                    ten.did(ins, f"{f.tag}_lg@{st.s}")

                for st in streams:
                    turned(st, "f1_x")
                    experts(st, f1, free_after(st, f1, f"f3_comb_{EXPERTS3 - 1}", -1))
                for st in streams:
                    s, AG, XT = st.s, flat(st.AG), flat(st.XT)
                    pe.wait_ge(adj_in[s], i * 16 + 16)
                    after(vec, f"g2_xh@{s}")
                    ten.did(turn(nc, st.turned, st.ADJ, env.ident), f"g2_adjT@{s}")
                    after(sca, f"g2_adjT@{s}")
                    turned(st, "g2_x")
                    for j in range(GT):
                        ins = mm(U[s][:, j * P:(j + 1) * P], lhsT=st.XH[:, j, :], rhs=st.ADJT[:, j, :], start=j == 0, stop=j == GT - 1, skip_group_check=True)
                    ten.did(ins, f"agg@{s}")
                    after(sca, f"agg@{s}")
                    after(vec, f"f1_comb_{EXPERTS1 - 1}@1")
                    for j in range(GT):
                        o, c = Y[s][:, j * P:(j + 1) * P], slice(j * P, (j + 1) * P)
                        mm(o, lhsT=AG[:, c], rhs=env.w("w_rel"), start=j == 0, stop=False, skip_group_check=True)
                        mm(o, lhsT=XT[:, c], rhs=env.w("w_root"), start=False, stop=False, skip_group_check=True)
                        ins = mm(o, lhsT=env.ones[0:1, :], rhs=env.row("b_rel"), start=False, stop=j == GT - 1, skip_group_check=True)
                    ten.did(ins, f"conv@{s}")
                for st in streams:
                    turned(st, "f2_x")
                    router(st, f2, EXPERTS2, "f2_wr", None)
                    experts(st, f2, free_after(st, f2, "conv"))
                for st in streams:
                    s, XT = st.s, flat(st.XT)
                    turned(st, "g3_x")
                    ten.did(mm(B[3][:, :], lhsT=env.w("g3_w"), rhs=XT, start=True, stop=True), f"inter@{s}")
                    after(sca, f"inter@{s}")
                    for j in range(GT):
                        c = slice(j * P, (j + 1) * P)
                        ins = mm(U[s][:, c], lhsT=flat(st.AG)[:, c], rhs=XT[:, c], start=j == 0, stop=j == GT - 1, skip_group_check=True)
                    ten.did(ins, f"sim@{s}")
                for st in streams:
                    s = st.s
                    after(sca, f"soft@{s}")
                    ten.did(turn(nc, B[3], st.SM, env.ident), f"pt@{s}")
                    after(sca, f"pt@{s}")
                    after(vec, f"f2_comb_{EXPERTS2}@1")
                    for j in range(GT):
                        ins = mm(Y[s][:, j * P:(j + 1) * P], lhsT=st.AG[:, j, :], rhs=st.XH[:, j, :], start=j == 0, stop=j == GT - 1, skip_group_check=True)
                    ten.did(ins, f"ov@{s}")
                for st in streams:
                    turned(st, "f3_x")
                    router(st, f3, EXPERTS3, "f3_wg", "f3_bg")
                    experts(st, f3, free_after(st, f3, "ov"))

        @block.scalar
        def _(act):
            sca.begin(act)
            go = nc.scalar.activation
            with act.Fori(0, TURNS) as i:
                after = lambda who, name: act.wait_ge(who.done, who.count(name, i))

                def turned(st, name):
                    after(ten, f"{name}@{st.s}")
                    sca.did(go(st.XT[:, :, :], tiles_of(st.turned[:, :]), ACT.Copy), f"{name}@{st.s}")

                def experts(st, f):
                    s = st.s
                    for k in range(f.total):
                        after(ten, f"{f.tag}_up_{k}@{s}")
                        if k >= 3:
                            after(ten, f"{f.tag}_down_{k-3}@{s}")
                        sca.did(go(H[k % 3][:, :], U[k % 3][:, :], f.func, bias=env.col(f.b1, k)), f"{f.tag}_h_{k}@{s}")
                    after(ten, f"{f.tag}_gt@{s}")
                    sca.did(go(st.GTR[0:f.experts, :], B[7][0:f.experts, :], ACT.Copy), f"{f.tag}_gt@{s}")

                def pair(st, tag):
                    after(vec, f"{tag}_diff@{st.s}")
                    sca.did(go(env.top.diff_exp[:, 0:GT], env.top.diff[:, 0:GT], ACT.Exp), f"{tag}_exp@{st.s}")

                for st in streams:
                    turned(st, "f1_xt")
                    experts(st, f1)
                for st in streams:
                    after(ten, f"g2_adjT@{st.s}")
                    sca.did(go(st.ADJT[:, :, :], tiles_of(st.turned[:, :]), ACT.Copy), f"g2_adjT@{st.s}")
                    turned(st, "g2_xt")
                    after(ten, f"agg@{st.s}")
                    sca.did(go(flat(st.AG), U[st.s][:, :], ACT.Copy), f"agg@{st.s}")
                for st in streams:
                    turned(st, "f2_xt")
                    pair(st, "f2")
                    experts(st, f2)
                for st in streams:
                    turned(st, "g3_xt")
                    after(ten, f"inter@{st.s}")
                    sca.did(go(flat(st.AG), B[3][:, :], ACT.Copy), f"inter@{st.s}")
                for st in streams:
                    s = st.s
                    after(vec, f"masked@{s}")
                    for j in range(GT):
                        ins = go(st.SM[:, j, :], st.SM[:, j, :], ACT.Exp, bias=st.nmx[:, j:j + 1], accum_out=st.ssum[:, j:j + 1])
                    sca.did(ins, f"soft@{s}")
                    after(ten, f"pt@{s}")
                    sca.did(go(flat(st.AG), B[3][:, :], ACT.Copy), f"pt@{s}")
                for st in streams:
                    turned(st, "f3_xt")
                    pair(st, "f3")
                    experts(st, f3)

        @block.vector
        def _(dve):
            vec.begin(dve)
            v = nc.vector
            with dve.Fori(0, TURNS) as i:
                link = Link(dve, link_sem, i, LINKS)
                norms.i = i
                after = lambda who, name: dve.wait_ge(who.done, who.count(name, i))

                def did(ins, name):
                    vec.did(ins, name)
                    dve.wait_ge(vec.done, vec.count(name, i))

                def experts(st, f):
                    X = st.X
                    for e in range(f.experts):
                        after(ten, f"{f.tag}_down_{(e + 1) * f.chunks - 1}@{st.s}")
                        for j in range(GT):
                            ins = v.scalar_tensor_tensor(X[:, j, :], Y[e % 2][:, j * P:(j + 1) * P], st.GATE[:, j, e:e + 1], X[:, j, :], ALU.mult, ALU.add)
                        did(ins, f"{f.tag}_comb_{e}@{st.s}")
                    after(ten, f"{f.tag}_gb@{st.s}")
                    did(v.tensor_tensor(X[:, :, :], X[:, :, :], tiles_of(st.turned[:, :]), ALU.add), f"{f.tag}_gb@{st.s}")

                def router(st, f, n, first):
                    after(ten, f"{f.tag}_lg@{st.s}")
                    link(v.tensor_copy(LG[:, :, 0:n], B[7][:, 0:GT * n].rearrange("p (j e) -> p j e", j=GT)))
                    did(top_two(nc, env, link, LG[:, :, 0:n], n, GT, env.top), f"{f.tag}_diff@{st.s}")
                    if first:
                        link(v.memset(st.GATE[:, :, 0:1], 1.0))
                    after(sca, f"{f.tag}_exp@{st.s}")
                    did(gate_weights(nc, link, st.GATE[:, :, first:first + n], n, GT, env.top), f"{f.tag}_gate@{st.s}")

                norm = lambda st, *more: layer_norm(nc, env, link, st.X, st.XH[:, :, :], *more)
                for st in streams:
                    tiles = bass.ds(i * (STREAMS * GT) + st.s * GT, GT)
                    link(copy(nc, st.X[:, :, :], env.x[:, tiles, :]))
                    link(copy(nc, st.GATE[:, :, 0:EXPERTS1], env.gates1[:, tiles, :]))
                    did(norm(st), f"f1_xh@{st.s}")
                for st in streams:
                    experts(st, f1)
                    link(layer_norm(nc, env, link, st.X, st.OUT[:, :, :]))
                    link(v.tensor_tensor(st.X[:, :, :], st.X[:, :, :], st.OUT[:, :, :], ALU.add))
                    did(layer_norm(nc, env, link, st.OUT, st.XH[:, :, :], (env.gamma, env.beta)), f"g2_xh@{st.s}")
                for st in streams:
                    after(ten, f"conv@{st.s}")
                    did(v.scalar_tensor_tensor(st.X[:, :, :], tiles_of(Y[st.s][:, :]), 0.0, st.X[:, :, :], ALU.max, ALU.add), f"conv@{st.s}")
                    did(norm(st), f"f2_xh@{st.s}")
                for st in streams:
                    router(st, f2, EXPERTS2, 1)
                    experts(st, f2)
                    did(norm(st), f"g3_xh@{st.s}")
                for st in streams:
                    SM = st.SM
                    dve.wait_ge(mask_in[st.s], i * 16 + 16)
                    link(v.tensor_copy(MK[:, :, :], MI[st.s][:, :, :]))
                    link(v.tensor_scalar(MK[:, :, :], MK[:, :, :], 0.0, None, ALU.not_equal))
                    link(v.tensor_scalar(MB[:, :, :], MK[:, :, :], -1.0, BIG, ALU.add, ALU.mult))
                    after(ten, f"sim@{st.s}")
                    link(v.tensor_tensor(SM[:, :, :], tiles_of(U[st.s][:, :]), st.ADJ[:, :, :], ALU.mult))
                    link(v.tensor_tensor(SM[:, :, :], SM[:, :, :], MK[:, :, :], ALU.mult))
                    link(v.tensor_tensor(SM[:, :, :], SM[:, :, :], MB[:, :, :], ALU.add))
                    link(v.tensor_reduce(mx[:, :], SM[:, :, :], AX.X, ALU.max))
                    did(v.tensor_scalar(st.nmx[:, :], mx[:, :], -1.0, None, ALU.mult), f"masked@{st.s}")
                for st in streams:
                    after(ten, f"ov@{st.s}")
                    link(v.reciprocal(st.ssum[:, :], st.ssum[:, :]))
                    for j in range(GT):
                        ins = v.scalar_tensor_tensor(st.X[:, j, :], Y[st.s][:, j * P:(j + 1) * P], st.ssum[:, j:j + 1], st.X[:, j, :], ALU.mult, ALU.add)
                    did(ins, f"ov@{st.s}")
                    did(norm(st), f"f3_xh@{st.s}")
                for st in streams:
                    router(st, f3, EXPERTS3, 0)
                    experts(st, f3)
                    did(v.tensor_copy(st.OUT[:, :, :], st.X[:, :, :]), f"out@{st.s}")
                link.end()
                for s in range(STREAMS):
                    dve.wait_ge(stored[s], i * 16 + 16)


class Top:
    def __init__(self, sb, tiles, n):
        wide, narrow = [P, tiles, n], [P, tiles]
        self.first, self.second, self.tie, self.rest = sb("top_first", wide), sb("top_second", wide), sb("top_tie", wide), sb("top_rest", wide)
        self.max1, self.max2, self.best = sb("top_max1", narrow), sb("top_max2", narrow), sb("top_best", narrow)
        self.diff, self.diff_exp = sb("top_diff", narrow), sb("top_diff_exp", narrow)
        self.w1, self.w2 = sb("top_w1", narrow), sb("top_w2", narrow)


class Names:
    pass


W_A = [("l0_w", 1, 128), ("rw1", 1, 64), ("ew1", 6, 128), ("ew2", 6, 128), ("ew3", 6, 128), ("conv1", 1, 128), ("conv2", 17, 128),
       ("w_se", 1, 3), ("w_msg", 1, 128), ("w_hh", 3, 128), ("w_ih", 6, 128), ("w_gat", 1, 16)]
W_C = [("f1_w1", 8, 128), ("f1_w2", 8, 128), ("w_rel", 1, 128), ("w_root", 1, 128), ("f2_wr", 1, 8), ("f2_w1", 36, 128), ("f2_w2", 36, 128),
       ("g3_w", 1, 128), ("f3_wg", 1, 8), ("f3_w1", 32, 128), ("f3_w2", 32, 128)]
COLS = [("rb1", 1), ("eb1", 6), ("eb2", 6), ("b_se", 1), ("bn1_g", 1), ("bn1_b", 1), ("bn1_m", 1), ("bn1_v", 1), ("bn2_g", 1), ("bn2_b", 1),
        ("bn2_m", 1), ("bn2_v", 1), ("b_ih", 3), ("b_hh", 3), ("f1_b1", 8), ("f2_b1", 36), ("f3_b1", 32)]
ROWS = [("l0_bias", 128), ("rb2", 6), ("b_msg", 128), ("b_rel", 128), ("f3_bg", 8)]
SPREAD = [("prelu", 1), ("att_src", 16), ("att_dst", 16), ("b_gat", 16), ("gat_gamma", 16), ("gat_beta", 16), ("gamma", 128), ("beta", 128)]


def offsets(table):
    out, at = {}, 0
    for name, *dims in table:
        out[name] = (at, dims[-1])
        at += dims[0] * dims[-1] if len(dims) > 1 else dims[0]
    return out, at


def setup(nc, env, d):
    with ExitStack() as ctx:
        sem = lambda n: ctx.enter_context(nc.semaphore("s_" + n))
        loaded, made, step, var_in, scaled = sem("loaded"), sem("constants_made"), sem("vector_step"), sem("bn_variance_ready"), sem("bn_scale_ready")
        block = ctx.enter_context(nc.Block())

        @block.sync
        def _(sp):
            sp.dma_start(env.cols[:, :], d["cols"]).then_inc(loaded, 16)
            sp.dma_start(env.spread[:, :], d["spread"].partition_broadcast(P)).then_inc(loaded, 16)
            sp.dma_start(env.rows[:, :], d["rows"].rearrange("(o n) -> o n", o=1)).then_inc(loaded, 16)
            for name, t in (("rw2", env.rw2), ("eb3", env.eb3), ("f1_b2", env.f1_b2), ("f2_b2", env.f2_b2), ("f3_b2", env.f3_b2)):
                sp.dma_start(t[:, :], d[name]).then_inc(loaded, 16)
            sp.dma_start(env.x[:, :, :], d["x"].rearrange("g n d -> n g d")).then_inc(loaded, 16)
            sp.wait_ge(loaded, 16 * 9)

        @block.gpsimd
        def _(pool):
            g = nc.gpsimd
            g.memset(env.ident[:, :], 0.0).then_inc(made, 1)
            pool.wait_ge(made, 1)
            g.affine_select(out=env.ident[:, :], in_=env.ident[:, :], compare_op=ALU.not_equal, fill=1.0, base=0,
                            pattern=[[-1, P]], channel_multiplier=1).then_inc(made, 1)
            g.memset(env.minus_half[:, :], -0.5).then_inc(made, 1)
            g.iota(env.earlier_i[:, :], pattern=[[-1, EMAX]], base=EMAX, channel_multiplier=0).then_inc(made, 1)
            pool.wait_ge(var_in, 1)
            g.tensor_tensor(env.bn_scale[:, :], env.bn_scale[:, :], env.minus_half[:, 0:2], ALU.pow).then_inc(scaled, 1)

        @block.vector
        def _(dve):
            v = nc.vector
            n = [0]

            def link(ins):
                n[0] += 1
                ins.then_inc(step, 1)
                dve.wait_ge(step, n[0])

            v.memset(env.ones[:, :], 1.0)
            v.memset(env.neg_ones[:, :], -1.0)
            v.memset(env.rounds_before[:, 0:1], 0)
            link(v.memset(env.ones_nt[:, :], 1.0))
            dve.wait_ge(made, 4)
            link(v.tensor_copy(env.earlier[:, :], env.earlier_i[:, :]))
            dve.wait_ge(loaded, 16 * 9)
            for k, tag in enumerate(("bn1", "bn2")):
                ins = v.tensor_scalar(env.bn_scale[:, k:k + 1], env.col(tag + "_v"), 1e-5, None, ALU.add)
            ins.then_inc(var_in, 1)
            dve.wait_ge(scaled, 1)
            for k, tag in enumerate(("bn1", "bn2")):
                s, h = env.bn_scale[:, k:k + 1], env.bn_shift[:, k:k + 1]
                link(v.tensor_tensor(s, s, env.col(tag + "_g"), ALU.mult))
                link(v.tensor_tensor(h, s, env.col(tag + "_m"), ALU.mult))
                link(v.tensor_tensor(h, env.col(tag + "_b"), h, ALU.subtract))
            for k in range(2):
                link(v.tensor_tensor(env.gru_bias[:, k:k + 1], env.col("b_ih", k), env.col("b_hh", k), ALU.add))
            link(v.tensor_scalar(env.gru_bias[:, :], env.gru_bias[:, :], 0.5, None, ALU.mult))


def gates_l1(nc, env):
    with ExitStack() as ctx:
        sb = lambda n, s: ctx.enter_context(nc.sbuf_tensor("g_" + n, s, F32))
        step, diff, ex, var_in, rstd = (ctx.enter_context(nc.semaphore("g_" + n)) for n in ("vector_step", "diff_ready", "exp_ready", "var_ready", "rstd_ready"))
        T = sb("centered", [P, NT, 16])
        S = sb("squared", [P, NT, 16])
        mean, var = sb("mean", [P, NT]), sb("var", [P, NT])
        top = Top(sb, NT, EXPERTS1)
        score = sb("score", [P, NT, EXPERTS1])
        PICK, PICKED = sb("pick", [P, NT, NT]), sb("picked", [P, NT, NT])
        block = ctx.enter_context(nc.Block())

        @block.gpsimd
        def _(pool):
            pool.wait_ge(var_in, 1)
            nc.gpsimd.tensor_tensor(var[:, :], var[:, :], env.minus_half[:, :], ALU.pow).then_inc(rstd, 1)

        @block.scalar
        def _(act):
            act.wait_ge(diff, 1)
            nc.scalar.activation(top.diff_exp[:, :], top.diff[:, :], ACT.Exp).then_inc(ex, 1)

        @block.vector
        def _(dve):
            v = nc.vector
            n = [0]

            def link(ins):
                n[0] += 1
                ins.then_inc(step, 1)
                dve.wait_ge(step, n[0])

            s16 = [P, NT, 16]
            A = env.att_acc
            link(v.tensor_reduce(mean[:, :], A[:, :, :], AX.X, ALU.add))
            link(v.tensor_scalar(mean[:, :], mean[:, :], 1.0 / 16, None, ALU.mult))
            link(v.tensor_tensor(T[:, :, :], A[:, :, :], bcast(mean[:, :], s16, 2), ALU.subtract))
            link(v.tensor_tensor(S[:, :, :], T[:, :, :], T[:, :, :], ALU.mult))
            link(v.tensor_reduce(var[:, :], S[:, :, :], AX.X, ALU.add))
            v.tensor_scalar(var[:, :], var[:, :], 1.0 / 16, LN_EPS, ALU.mult, ALU.add).then_inc(var_in, 1)
            dve.wait_ge(rstd, 1)
            link(v.tensor_tensor(T[:, :, :], T[:, :, :], bcast(var[:, :], s16, 2), ALU.mult))
            link(v.tensor_tensor(T[:, :, :], T[:, :, :], bcast(env.spread_of("gat_gamma"), s16, 1), ALU.mult))
            link(v.tensor_tensor(T[:, :, :], T[:, :, :], bcast(env.spread_of("gat_beta"), s16, 1), ALU.add))
            link(v.tensor_reduce(score[:, :, :], T[:, :, :].rearrange("p t (h x) -> p t x h", x=EXPERTS1), AX.X, ALU.add))
            link(v.tensor_scalar(score[:, :, :], score[:, :, :], 1.0 / HEADS, None, ALU.mult))
            top_two(nc, env, link, score[:, :, :], EXPERTS1, NT, top).then_inc(diff, 1)
            dve.wait_ge(ex, 1)
            link(gate_weights(nc, link, score[:, :, :], EXPERTS1, NT, top))
            cube = [P, NT, NT]
            link(v.tensor_tensor(PICK[:, :, :], env.tile_id[:, :].unsqueeze(2).to_broadcast(cube), env.place_tile[:, :].unsqueeze(1).to_broadcast(cube), ALU.is_equal))
            for e in range(EXPERTS1):
                link(v.tensor_tensor(PICKED[:, :, :], PICK[:, :, :], score[:, :, e].unsqueeze(1).to_broadcast(cube), ALU.mult))
                link(v.tensor_reduce(env.gates1[:, :, e], PICKED[:, :, :], AX.X, ALU.add))


def load_weights(nc, env, tensor, dram):
    with ExitStack() as ctx:
        s = ctx.enter_context(nc.semaphore("weights_" + dram.tensor.name))
        block = ctx.enter_context(nc.Block())

        @block.sync
        def _(sp):
            sp.dma_start(tensor, dram).then_inc(s, 16)
            sp.wait_ge(s, 16)


def program(nc, d):
    env = Names()
    with ExitStack() as ctx:
        sb = lambda n, s, dt=F32: ctx.enter_context(nc.sbuf_tensor(n, s, dt))
        sem = lambda n: ctx.enter_context(nc.semaphore(n))

        cols, ncols = offsets(COLS)
        rows, nrows = offsets(ROWS)
        spread, nspread = offsets(SPREAD)
        env.x = sb("x", [P, NT, D])
        env.cols = sb("cols", [P, ncols])
        env.spread = sb("spread", [P, nspread])
        env.rows = sb("rows", [1, nrows])
        env.rw2 = sb("rw2", [ROUTER_H, EXPERTS0])
        env.eb3 = sb("eb3", [EXPERTS0, D])
        env.f1_b2 = sb("f1_b2", [EXPERTS1, D])
        env.f2_b2 = sb("f2_b2", [EXPERTS2 + 1, D])
        env.f3_b2 = sb("f3_b2", [EXPERTS3, D])
        env.ident = sb("ident", [P, P])
        env.ones = sb("ones", [1, P])
        env.neg_ones = sb("neg_ones", [3, P])
        env.earlier_i = sb("earlier_i", [P, EMAX], I32)
        env.earlier = sb("earlier", [P, EMAX])
        env.bn_scale = sb("bn_scale", [P, 2])
        env.bn_shift = sb("bn_shift", [P, 2])
        env.gru_bias = sb("gru_bias", [P, 2])
        env.ln_stats = sb("ln_stats", [P, GT, 6])
        env.ln_mv = sb("ln_mv", [P, GT, 2])
        env.ln_rstd = sb("ln_rstd", [P, GT])
        env.ln_var = sb("ln_var", [P, GT])
        env.minus_half = sb("minus_half", [P, NT])
        env.own_rows = sb("own_rows", [P, NT, ROW])
        env.tile_id = sb("tile_id", [P, NT])
        env.place_tile = sb("place_tile", [P, NT])
        env.gates1 = sb("gates1", [P, NT, EXPERTS1])
        env.att_acc = sb("att_acc", [P, NT, 16])
        env.start_of = sb("start_of", [P, NT1], I32)
        env.node_id = sb("node_id", [P, NT1], I32)
        env.slot_row = sb("slot_row", [P, NT, SLOTS], I32)
        env.slot_penalty = sb("slot_penalty", [P, NT, SLOTS])
        env.tile_groups = sb("tile_groups", [P, NT], I32)
        env.tile_rounds = sb("tile_rounds", [P, NT], I32)
        env.rounds_before = sb("rounds_before", [P, NT], I32)
        env.ones_nt = sb("ones_nt", [P, NT])
        env.top = Top(sb, GT, EMAX)
        env.spread_of = lambda n: env.spread[:, spread[n][0]:spread[n][0] + spread[n][1]]
        env.col = lambda n, k=0: env.cols[:, cols[n][0] + k:cols[n][0] + k + 1]
        env.row = lambda n: env.rows[0:1, rows[n][0]:rows[n][0] + dict(ROWS)[n]]
        env.prelu, env.gamma, env.beta = env.spread_of("prelu"), env.spread_of("gamma"), env.spread_of("beta")
        env.att_src, env.att_dst, env.b_gat = env.spread_of("att_src"), env.spread_of("att_dst"), env.spread_of("b_gat")
        env.bank = [ctx.enter_context(nc.psum_tensor(f"bank{k}", [P, GT * P], F32)) for k in range(8)]
        dram = lambda n, s, dt: nc.dram_tensor(n, s, dt, kind="Internal").ap()
        env.sorted_dram = dram("sorted_dram", [E_TOTAL + SLOTS], F32)
        env.row_first_dram = dram("row_first_dram", [P], F32)
        env.chunk_first_dram = dram("chunk_first_dram", [P, 32], F32)
        env.start_dram = dram("start_dram", [NT1 * P], I32)
        env.table_dram = dram("table_dram", [NODES, ROW], F32)
        env.adj_dram, env.mask_dram, env.out_dram = d["adj"], d["nodemask"], d["out"]
        env.sign_ready, env.idx_sem, env.att_fin, env.pause = sem("sign_ready"), sem("indices_copied"), sem("aggregate_step"), sem("pause")

        setup(nc, env, d)
        with ExitStack() as part:
            sbp = lambda n, s, dt=F32: part.enter_context(nc.sbuf_tensor(n, s, dt))
            env.keys_a = sbp("keys_a", [P, 4096])
            env.keys_b = sbp("keys_b", [P, 4096])
            env.end_of = sbp("end_of", [P, NT], I32)
            env.part_id = sbp("part_id", [P, 1], I32)
            env.sign_i = sbp("sign_i", [P, 7], I32)
            env.sign = sbp("sign", [P, 7])
            env.tail_i = sbp("tail_i", [P, SLOTS], I32)
            env.tail_keys = sbp("tail_keys", [P, SLOTS])
            env.chunk_first = sbp("chunk_first", [P, 32])
            env.row_first = sbp("row_first", [P, P])
            env.node_key = sbp("node_key", [P, NT1], I32)
            env.search_cmp = sbp("search_cmp", [P, NT1, P])
            env.cnt = sbp("cnt", [P, NT1])
            env.row_f = sbp("row_f", [P, NT1])
            env.row_index = sbp("row_index", [P, NT1], I32)
            env.l2_rows = sbp("l2_rows", [P, NT1, 32])
            env.chunk_index = sbp("chunk_index", [P, NT1], I32)
            env.start_f = sbp("start_f", [P, NT1])
            env.key_row_index = sbp("key_row_index", [P, 2, NT], I32)
            env.key_rows = sbp("key_rows", [P, NT, 2 * SLOTS])
            env.shift_bit = sbp("shift_bit", [P, NT], I32)
            env.degree_in = sbp("degree_in", [P, NT])
            env.rank_a = sbp("rank_a", [P, NT])
            env.rank_b = sbp("rank_b", [P, NT])
            env.rank_i = sbp("rank_i", [P, NT], I32)
            env.tile_id_i = sbp("tile_id_i", [P, NT], I32)
            env.degree = sbp("degree", [P, NT])
            env.deg_max = sbp("deg_max", [P, NT])
            env.tile_groups_f = sbp("tile_groups_f", [P, NT])
            with nc.sbuf_tensor("l3_rows", [P, NT1, P], F32) as l3:
                env.l3_rows = l3
                env.shifted = l3[:, :, :].rearrange("p a b -> p (a b)")[:, 0:NT * 2 * SLOTS].rearrange("p (a b) -> p a b", a=NT)
                env.pick = l3[:, :, :].rearrange("p a b -> p (a b)")[:, 0:NT * NT].rearrange("p (a b) -> p a b", a=NT)
                env.picked = env.search_cmp[:, :, :].rearrange("p a b -> p (a b)")[:, 0:NT * NT].rearrange("p (a b) -> p a b", a=NT)
                env.slot_dst = env.search_cmp[:, :, :].rearrange("p a b -> p (a b)")[:, 0:NT * SLOTS].bitcast(I32).rearrange("p (a b) -> p a b", a=NT)
                sort_edges(nc, env, d["edge_index"])

        with ExitStack() as part:
            wa, na = offsets(W_A)
            WA = part.enter_context(nc.sbuf_tensor("weights_a", [P, na], F32))
            env.w = lambda n, k=0: WA[:, wa[n][0] + k * wa[n][1]:wa[n][0] + (k + 1) * wa[n][1]]
            load_weights(nc, env, WA[:, :], d["weights_a"])
            phase_a(nc, env)
        with ExitStack() as part:
            sbp = lambda n, s, dt=F32: part.enter_context(nc.sbuf_tensor(n, s, dt))
            env.att_max = sbp("att_max", [P, NT, 4])
            env.att_den = sbp("att_den", [P, NT, 4])
            env.rounds_f = sbp("rounds_f", [P, NT])
            env.rounds_f2 = sbp("rounds_f2", [P, NT + 1])
            env.groups_f = sbp("groups_f", [P, 2, NT // 2])
            env.groups_sum = sbp("groups_sum", [P, 2, NT // 2])
            env.rows_due = sbp("rows_due", [P, 2, NT // 2], I32)
            env.idx_now = sbp("idx_now", [P, 2, SLOTS], I32)
            attend(nc, env)
            gates_l1(nc, env)
        with ExitStack() as part:
            wc, nw = offsets(W_C)
            WC = part.enter_context(nc.sbuf_tensor("weights_c", [P, nw], F32))
            env.w = lambda n, k=0: WC[:, wc[n][0] + k * wc[n][1]:wc[n][0] + (k + 1) * wc[n][1]]
            load_weights(nc, env, WC[:, :], d["weights_c"])
            phase_c(nc, env)


def kernel(**inputs):
    import numpy as np
    import concourse.bacc as bacc
    from concourse.bass_utils import run_bass_kernel_spmd

    a = {k: np.asarray(v) for k, v in inputs.items()}
    flat = lambda t: np.ascontiguousarray(t).reshape(P, -1)
    stack = lambda t: flat(np.transpose(t, (1, 0, 2)))
    rows_in = lambda t: flat(np.transpose(t.reshape(-1, P, t.shape[-1]), (1, 0, 2)))
    col = lambda t: np.ascontiguousarray(t.reshape(-1, P).T)

    def short_col(t):
        out = np.zeros((P, 1), t.dtype)
        out[:t.size, 0] = t
        return out

    g, f = "L1_gnn_", "L1_ffn_"
    weights_a = np.concatenate([
        a["L0_gnn_W"], a["L0_ffn_router_w1"], stack(a["L0_ffn_expert_w1"]), stack(a["L0_ffn_expert_w2"]), stack(a["L0_ffn_expert_w3"]),
        a[g + "conv1_w"][:, :, 0].T, flat(np.transpose(a[g + "conv2_w"], (1, 2, 0))), a[g + "w_se"].T, a[g + "w_msg"].T,
        a[g + "w_hh"].T, flat(np.concatenate([a[g + "w_ih"][:, :P].T, a[g + "w_ih"][:, P:].T], axis=1)), a[f + "W_gat"]], axis=1)
    weights_c = np.concatenate([
        stack(a[f + "W1"]), rows_in(a[f + "W2"].reshape(-1, P)), a["L2_gnn_W_rel"], a["L2_gnn_W_root"], a["L2_ffn_Wr"],
        a["L2_ffn_W1s"], stack(a["L2_ffn_W1p"]), rows_in(a["L2_ffn_W2s"]), rows_in(a["L2_ffn_W2p"].reshape(-1, P)),
        a["L3_gnn_W"], a["L3_ffn_Wg"].T, flat(np.transpose(a["L3_ffn_W1"], (2, 0, 1))),
        rows_in(np.ascontiguousarray(np.transpose(a["L3_ffn_W2"], (0, 2, 1))).reshape(-1, P))], axis=1)
    cols = np.concatenate([
        short_col(a["L0_ffn_router_b1"]), col(a["L0_ffn_expert_b1"]), col(a["L0_ffn_expert_b2"]), short_col(a[g + "b_se"]),
        *[col(a[g + n]) for n in ("bn1_g", "bn1_b", "bn1_m", "bn1_v", "bn2_g", "bn2_b", "bn2_m", "bn2_v", "b_ih", "b_hh")],
        col(a[f + "b1"]), col(a["L2_ffn_b1s"]), col(a["L2_ffn_b1p"]), col(a["L3_ffn_b1"])], axis=1)
    arrays = {
        "x": a["x"], "adj": a["adj"], "nodemask": a["nodemask"], "edge_index": a["L1_ffn_edge_index"],
        "weights_a": weights_a, "weights_c": weights_c, "cols": cols,
        "rows": np.concatenate([a[n] for n in ("L0_gnn_bias", "L0_ffn_router_b2", g + "b_msg", "L2_gnn_b_rel", "L3_ffn_bg")]),
        "spread": np.concatenate([a["L0_gnn_prelu_a"].reshape(1)] + [a[n].reshape(-1) for n in (
            f + "att_src", f + "att_dst", f + "b_gat", f + "ln_gamma", f + "ln_beta", "L2_gnn_ln_gamma", "L2_gnn_ln_beta")]),
        "rw2": a["L0_ffn_router_w2"], "eb3": a["L0_ffn_expert_b3"], "f1_b2": a[f + "b2"],
        "f2_b2": np.concatenate([a["L2_ffn_b2s"].reshape(1, P), a["L2_ffn_b2p"]], axis=0), "f3_b2": a["L3_ffn_b2"]}
    arrays = {k: np.ascontiguousarray(v) for k, v in arrays.items()}
    nc = bacc.Bacc("TRN2", target_bir_lowering=False, num_devices=1)
    d = {k: nc.dram_tensor(f"in_{k}", v.shape, mybir.dt.from_np(v.dtype), kind="ExternalInput").ap() for k, v in arrays.items()}
    d["out"] = nc.dram_tensor("out", a["x"].shape, F32, kind="ExternalOutput").ap()
    program(nc, d)
    result = run_bass_kernel_spmd(nc, [{f"in_{k}": v for k, v in arrays.items()}], core_ids=[0])
    return result.results[0]["out"]
```

```python
from contextlib import ExitStack

import concourse.bass as bass
from concourse import mybir

F32, BF16, I32, U32 = mybir.dt.float32, mybir.dt.bfloat16, mybir.dt.int32, mybir.dt.uint32
ALU, ACT, AX = mybir.AluOpType, mybir.ActivationFunctionType, mybir.AxisListType
RMAX = bass.bass_isa.ReduceOp.max

P = 128
D = 128
NODES = 64 * P
NT = NODES // P
NT_BITS, P_BITS = 6, 7
RANK_MAX = 4095.0
NT1 = NT + 1
GT = 4
GROUPS = NT // GT
LN_EPS = 1e-5
BIG = 1e30

EXPERTS0, ROUTER_H = 6, 64
CONV_K, CONV_PAD = 17, 8
HEADS, EXPERTS1 = 4, 4
EXPERTS2, EXPERTS3 = 8, 8
EMAX = 9
ROW = HEADS * EXPERTS1 + 2 * HEADS
SLOPE = 0.2

E_TOTAL = 524288
SRC_BITS, DST_BITS = 13, 14
KEY_BASE = 0x10000000
SLOT_BITS = 5
SLOTS = 1 << SLOT_BITS
KEY_ROWS = E_TOTAL // SLOTS
GROUP_BITS = 1
SLOT_GROUP = 1 << GROUP_BITS


def sort_edges(nc, env, edge_index, loads):
    KA, KB = env.keys_a, env.keys_b
    start_of = env.start_of
    PER = E_TOTAL // P
    ROWBITS = PER.bit_length() - 1
    ALLBITS = E_TOTAL.bit_length() - 1

    with ExitStack() as ctx:
        sem = lambda n: ctx.enter_context(nc.semaphore(n))
        loaded, iota_done = sem("edges_loaded"), sem("iota_done")
        dve_step, flipped = sem("sort_dve_step"), sem("sort_flipped")
        trans, evac = sem("sort_blocks_transposed"), sem("sort_blocks_copied")
        stage_done = sem("sort_half_done")
        stored, weights_in = sem("sorted_stored"), sem("weights_loaded")
        one_hots, counted, sums_in, summed = sem("one_hots_ready"), sem("firsts_counted"), sem("counts_copied"), sem("firsts_summed")
        want_rows, got_rows = sem("first_rows_ready"), sem("first_rows_loaded")
        start_ready, start_stored, start_loaded = sem("start_ready"), sem("start_stored"), sem("start_loaded")
        want_keys, got_keys, deg_ready, maxdeg_done = sem("key_rows_ready"), sem("key_rows_loaded"), sem("deg_ready"), sem("maxdeg_done")
        tail_set = sem("tail_keys_set")
        block = ctx.enter_context(nc.Block())

        phases = [("row", [(b, k) for k in range(1, ROWBITS) for b in range(k - 1, -1, -1)], None)]
        phases.append(("flip", None, 0))
        phases.append(("row", [(b, None) for b in range(ROWBITS - 1, -1, -1)], None))
        phases.append(("unflip", None, 0))
        for k in range(ROWBITS + 1, ALLBITS + 1):
            last = k == ALLBITS
            phases.append(("to_column", None, None))
            dirbit = None if last else k - ROWBITS
            phases.append(("column", [(b - ROWBITS, dirbit) for b in range(k - 1, ROWBITS - 1, -1)]
                           + [(b, dirbit) for b in range(ROWBITS - 1, 6, -1)], None))
            phases.append(("to_row", None, dirbit))
            phases.append(("row", [(b, None) for b in range(6, -1, -1)], None))
            if not last:
                phases.append(("unflip", None, dirbit))

        bufs = [KA, KB]
        plan, cur = [], 0
        for kind, steps, bit in phases:
            plan.append((kind, steps, bit, cur))
            cur ^= (len(steps) if steps else 1) & 1
        final = bufs[cur]

        def free_view(keys, a, b):
            hi, lo = max(a, b), min(a, b)
            v = keys.rearrange("p (h x m y l) -> p h x m y l", x=2, m=1 << (hi - lo - 1), y=2, l=1 << lo)
            if b > a:
                return lambda side, up: v[:, :, 1 - up, :, side, :]
            return lambda side, up: v[:, :, side, :, 1 - up, :]

        NBLK = PER // P
        GRP = 4
        PARTS = 4
        whole = slice(0, PER)
        parts = [slice(k * PER // PARTS, (k + 1) * PER // PARTS) for k in range(PARTS)]
        GROUPS_PART = NBLK // GRP // PARTS
        FIRST_COLS = 32

        @block.sync
        def _(sp):
            sp.dma_start(KA[:, :].bitcast(I32), edge_index[0, :].rearrange("(p f) -> p f", p=P)).then_inc(loaded, 16)
            sp.dma_start(KB[:, :].bitcast(I32), edge_index[1, :].rearrange("(p f) -> p f", p=P)).then_inc(loaded, 16)
            for to, dram in loads:
                sp.dma_start(to, dram).then_inc(weights_in, 16)
            pairs = env.sorted_pairs
            keys = final[:, :].rearrange("p (r f) -> p r f", f=SLOTS)
            sp.wait_ge(stage_done, 1)
            sp.dma_start(pairs[1:KEY_ROWS + 1, 0:SLOTS].rearrange("(p r) f -> p r f", p=P), keys).then_inc(stored, 16)
            sp.dma_start(pairs[0:KEY_ROWS, SLOTS:2 * SLOTS].rearrange("(p r) f -> p r f", p=P), keys).then_inc(stored, 16)
            sp.wait_ge(tail_set, 1)
            sp.dma_start(pairs[KEY_ROWS:KEY_ROWS + 1, SLOTS:2 * SLOTS], env.tail_keys[0:1, 0:SLOTS]).then_inc(stored, 16)
            sp.dma_start(pairs[0:1, 0:SLOTS], env.tail_keys[0:1, 0:SLOTS]).then_inc(stored, 16)
            sp.dma_start(pairs[KEY_ROWS + 1:KEY_ROWS + 2, :], env.tail_keys[0:1, :]).then_inc(stored, 16)
            sp.wait_ge(weights_in, 16 * len(loads))
            sp.wait_ge(start_ready, 1)
            sp.dma_start(env.start_dram[0:NT1 * P].rearrange("(t p) -> p t", p=P), start_of[:, :], allow_slow_non_contiguous=True).then_inc(start_stored, 16)
            sp.wait_ge(start_stored, 16)
            sp.dma_start(env.end_of[:, :], env.start_dram[1:NT * P + 1].rearrange("(t p) -> p t", p=P), allow_slow_non_contiguous=True).then_inc(start_loaded, 16)

        @block.gpsimd
        def _(pool):
            nc.gpsimd.iota(env.node_id[:, :], pattern=[[P, NT1]], base=0, channel_multiplier=1).then_inc(iota_done, 1)
            nc.gpsimd.iota(env.tile_id_i[:, :], pattern=[[1, NT]], base=0, channel_multiplier=0).then_inc(iota_done, 1)
            nc.gpsimd.iota(env.part_id[:, :], pattern=[[0, 1]], base=0, channel_multiplier=1).then_inc(iota_done, 1)
            nc.gpsimd.iota(env.lane_id_i[:, :], pattern=[[1, P]], base=0, channel_multiplier=0).then_inc(iota_done, 1)
            pool.wait_ge(want_rows, 1)
            pool.wait_ge(stored, 80)
            for t in range(NT1):
                pool.indirect_dma_start(out=env.first_rows[:, t, :], out_offset=None, in_=env.sorted_pairs,
                                        in_offset=bass.IndirectOffsetOnAxis(ap=env.row_index[:, t:t + 1].bitcast(U32), axis=0),
                                        bounds_check=KEY_ROWS + 1, oob_is_err=False).then_inc(got_rows, 16)
            pool.wait_ge(want_keys, 1)
            for t in range(NT):
                pool.indirect_dma_start(out=env.key_rows[:, t, :], out_offset=None, in_=env.sorted_pairs,
                                        in_offset=bass.IndirectOffsetOnAxis(ap=env.key_row_index[:, t:t + 1].bitcast(U32), axis=0),
                                        bounds_check=KEY_ROWS + 1, oob_is_err=False).then_inc(got_keys, 16)
            pool.wait_ge(deg_ready, 1)
            nc.gpsimd.partition_all_reduce(env.deg_max[:, :], env.degree[:, :], P, RMAX).then_inc(maxdeg_done, 1)

        @block.tensor
        def _(pe):
            n = 0
            turns = 0
            for kind, steps, bit, at in plan:
                if kind not in ("to_column", "to_row"):
                    continue
                for g in range(NBLK // GRP):
                    if g % GROUPS_PART == 0:
                        turns += 1
                        pe.wait_ge(flipped, turns)
                    if n >= 4:
                        pe.wait_ge(evac, n - 3)
                    for b in range(GRP):
                        c = g * GRP + b
                        ins = nc.tensor.transpose(env.bank[n % 4][:, b * P:(b + 1) * P], bufs[at][:, c * P:(c + 1) * P], env.ident[:, :])
                    ins.then_inc(trans, 1)
                    n += 1
            for q in range(P // FIRST_COLS):
                pe.wait_ge(one_hots, q + 1)
                for c in range(q * FIRST_COLS, (q + 1) * FIRST_COLS):
                    ins = nc.tensor.matmul(env.bank[0][:, 0:NT], lhsT=env.lane_hot[:, c, :], rhs=env.tile_hot[:, c, :], start=c == 0, stop=c == P - 1)
            ins.then_inc(counted, 1)
            pe.wait_ge(sums_in, 1)
            nc.tensor.matmul(env.bank[1][:, 0:NT1], lhsT=env.later_lane[:, :], rhs=env.counts[:, :], start=True, stop=False)
            nc.tensor.matmul(env.bank[1][:, 0:NT1], lhsT=env.all_lanes[:, :], rhs=env.tiles_before[:, :], start=False, stop=True).then_inc(summed, 1)

        @block.scalar
        def _(act):
            n = 0
            act.wait_ge(sign_ready := env.sign_ready, 1)
            for kind, steps, bit, at in plan:
                if kind not in ("to_column", "to_row"):
                    continue
                for g in range(NBLK // GRP):
                    act.wait_ge(trans, n + 1)
                    dst = bufs[at ^ 1][:, g * GRP * P:(g + 1) * GRP * P]
                    if kind == "to_row" and bit is not None:
                        nc.scalar.activation(dst, env.bank[n % 4][:, :], ACT.Copy, scale=env.sign[:, bit:bit + 1]).then_inc(evac, 1)
                    else:
                        nc.scalar.activation(dst, env.bank[n % 4][:, :], ACT.Copy).then_inc(evac, 1)
                    n += 1

        @block.vector
        def _(dve):
            done = [0]

            def link(ins, count=1):
                done[0] += count
                ins.then_inc(dve_step, count)
                dve.wait_ge(dve_step, done[0])

            dve.wait_ge(iota_done, 4)
            link(nc.vector.tensor_copy(env.tile_id[:, :], env.tile_id_i[:, :]))
            link(nc.vector.tensor_copy(env.lane_id[:, :], env.lane_id_i[:, :]))
            link(nc.vector.tensor_copy(env.part_id_f[:, :], env.part_id[:, :]))
            link(nc.vector.tensor_scalar(env.later_lane[:, :], env.lane_id[:, :], env.part_id_f[:, :], None, ALU.is_gt))
            link(nc.vector.memset(env.all_lanes[:, :], 1.0))
            link(nc.vector.memset(env.counts[:, :], 0.0))
            link(nc.vector.memset(env.tiles_before[:, :], 0.0))
            for b in range(7):
                nc.vector.tensor_scalar(env.sign_i[:, b:b + 1], env.part_id[:, :], b, 1, ALU.logical_shift_right, ALU.bitwise_and).then_inc(dve_step, 1)
                done[0] += 1
            dve.wait_ge(dve_step, done[0])
            nc.vector.tensor_scalar(env.sign[:, :], env.sign_i[:, :], -2.0, 1.0, ALU.mult, ALU.add).then_inc(env.sign_ready, 1)
            nc.vector.memset(env.tail_i[:, :], (NODES << SRC_BITS) | KEY_BASE)
            dve.wait_ge(env.sign_ready, 1)
            ai, bi = KA[:, :].bitcast(I32), KB[:, :].bitcast(I32)
            dve.wait_ge(loaded, 32)
            link(nc.vector.tensor_scalar(ai, ai, NODES - 1, None, ALU.min))
            link(nc.vector.tensor_scalar(bi, bi, NODES, None, ALU.min))
            link(nc.vector.tensor_scalar(bi, bi, SRC_BITS, KEY_BASE, ALU.logical_shift_left, ALU.bitwise_or))
            link(nc.vector.tensor_tensor(ai, ai, bi, ALU.bitwise_or))

            def compare(src, dst, a, b, cols):
                s, d = src[:, cols], dst[:, cols]
                if b is None:
                    s, d = (t.rearrange("p (h x l) -> p h x l", x=2, l=1 << a) for t in (s, d))
                    return [nc.vector.tensor_tensor(d[:, :, side, :], s[:, :, 0, :], s[:, :, 1, :], op) for side, op in ((0, ALU.min), (1, ALU.max))]
                s, d = free_view(s, a, b), free_view(d, a, b)
                return [nc.vector.tensor_tensor(d(side, up), s(0, up), s(1, up), ALU.min if side != up else ALU.max) for up in (1, 0) for side in (0, 1)]

            def operation(kind, step, bit, at, cols):
                src, dst = bufs[at], bufs[at ^ 1]
                if kind in ("flip", "unflip"):
                    return [nc.vector.tensor_scalar(dst[:, cols], src[:, cols], env.sign[:, bit:bit + 1], None, ALU.mult)]
                return compare(src, dst, step[0], step[1], cols)

            todo = []
            for kind, steps, bit, at in plan:
                if kind in ("to_column", "to_row"):
                    todo.append(None)
                else:
                    for step in steps or [None]:
                        todo.append((kind, step, bit, at))
                        at ^= 1
            turns = 0
            for n, op in enumerate(todo):
                if op is None:
                    continue
                after_turn, before_turn = n > 0 and todo[n - 1] is None, n + 1 < len(todo) and todo[n + 1] is None
                for k, cols in enumerate(parts if after_turn or before_turn else [whole]):
                    if after_turn:
                        dve.wait_ge(evac, turns * NBLK // GRP + (k + 1) * GROUPS_PART)
                    instructions = operation(*op, cols)
                    for ins in instructions:
                        ins.then_inc(dve_step, 1)
                    done[0] += len(instructions)
                    if before_turn:
                        dve.wait_ge(dve_step, done[0])
                        dve.nop().then_inc(flipped, 1)
                turns += after_turn
                if not before_turn:
                    dve.wait_ge(dve_step, done[0])
            first = env.first_keys
            nc.vector.tensor_copy(first[:, :], final[:, ::SLOTS].bitcast(I32)).then_inc(stage_done, 1)
            dve.wait_ge(stage_done, 1)
            nc.vector.tensor_copy(env.tail_keys[:, :].bitcast(I32), env.tail_i[:, :]).then_inc(tail_set, 1)
            for field, shift, bits in ((env.first_tile, SRC_BITS + P_BITS, DST_BITS - P_BITS), (env.first_lane, SRC_BITS, P_BITS)):
                link(nc.vector.tensor_scalar(env.field[:, :], first[:, :], shift, (1 << bits) - 1, ALU.logical_shift_right, ALU.bitwise_and))
                link(nc.vector.tensor_copy(field[:, :], env.field[:, :]))
            for q in range(P // FIRST_COLS):
                c = slice(q * FIRST_COLS, (q + 1) * FIRST_COLS)
                tiles, lanes = [P, FIRST_COLS, NT], [P, FIRST_COLS, P]
                link(nc.vector.tensor_tensor(env.tile_hot[:, c, :], env.first_tile[:, c].unsqueeze(2).to_broadcast(tiles), env.tile_id[:, :].unsqueeze(1).to_broadcast(tiles), ALU.is_equal))
                nc.vector.tensor_tensor(env.lane_hot[:, c, :], env.first_lane[:, c].unsqueeze(2).to_broadcast(lanes), env.lane_id[:, :].unsqueeze(1).to_broadcast(lanes), ALU.is_equal).then_inc(one_hots, 1)
            link(nc.vector.tensor_scalar(env.node_key[:, :], env.node_id[:, :], SRC_BITS, KEY_BASE, ALU.logical_shift_left, ALU.bitwise_or))
            dve.wait_ge(counted, 1)
            link(nc.vector.tensor_copy(env.counts[:, 0:NT], env.bank[0][:, 0:NT]))
            nc.vector.tensor_tensor_scan(env.tiles_before[:, 1:NT1], env.ones_nt[:, :], env.counts[:, 0:NT], 0.0, ALU.mult, ALU.add).then_inc(sums_in, 1)
            dve.wait_ge(summed, 1)
            link(nc.vector.tensor_scalar(env.row_f[:, :], env.bank[1][:, 0:NT1], 1.0, None, ALU.max))
            nc.vector.tensor_copy(env.row_index[:, :], env.row_f[:, :]).then_inc(want_rows, 1)
            dve.wait_ge(got_rows, 16 * NT1)
            key = env.node_key[:, :].bitcast(F32)
            link(nc.vector.tensor_tensor(env.is_below[:, :, :], env.first_rows[:, :, 0:SLOTS], key.unsqueeze(2).to_broadcast([P, NT1, SLOTS]), ALU.is_lt))
            link(nc.vector.tensor_reduce(env.cnt[:, :], env.is_below[:, :, :], AX.X, ALU.add))
            link(nc.vector.tensor_scalar(env.row_f[:, :], env.row_f[:, :], -1.0, float(SLOTS), ALU.add, ALU.mult))
            link(nc.vector.tensor_tensor(env.start_f[:, :], env.row_f[:, :], env.cnt[:, :], ALU.add))
            link(nc.vector.tensor_copy(start_of[:, :], env.start_f[:, :]))
            dve.nop().then_inc(start_ready, 1)

            dve.wait_ge(start_loaded, 16)
            link(nc.vector.tensor_tensor(env.degree_in[:, :], env.end_of[:, :], start_of[:, 0:NT], ALU.subtract))
            rank = [env.rank_a, env.rank_b]
            link(nc.vector.tensor_scalar(rank[1][:, :], env.degree_in[:, :], RANK_MAX, float(NT), ALU.min, ALU.mult))
            link(nc.vector.tensor_tensor(rank[0][:, :], rank[1][:, :], env.tile_id[:, :], ALU.add))
            at = 0
            for k in range(1, NT_BITS + 1):
                for a in range(k - 1, -1, -1):
                    s_, d_ = rank[at], rank[at ^ 1]
                    if k == NT_BITS:
                        sv, dv = (t[:, :].rearrange("p (h x l) -> p h x l", x=2, l=1 << a) for t in (s_, d_))
                        nc.vector.tensor_tensor(dv[:, :, 0, :], sv[:, :, 0, :], sv[:, :, 1, :], ALU.min)
                        ins = nc.vector.tensor_tensor(dv[:, :, 1, :], sv[:, :, 0, :], sv[:, :, 1, :], ALU.max)
                    else:
                        sv, dv = free_view(s_[:, :], a, k), free_view(d_[:, :], a, k)
                        for up in (1, 0):
                            nc.vector.tensor_tensor(dv(0, up), sv(0, up), sv(1, up), ALU.min if up else ALU.max)
                            ins = nc.vector.tensor_tensor(dv(1, up), sv(0, up), sv(1, up), ALU.max if up else ALU.min)
                    link(ins)
                    at ^= 1
            link(nc.vector.tensor_copy(env.rank_i[:, :], rank[at][:, :]))
            link(nc.vector.tensor_scalar(env.rank_i[:, :], env.rank_i[:, :], NT - 1, None, ALU.bitwise_and))
            cube = [P, NT, NT]
            pick = env.pick
            link(nc.vector.tensor_copy(env.place_tile[:, :], env.rank_i[:, :]))
            link(nc.vector.tensor_tensor(pick, env.place_tile[:, :].unsqueeze(2).to_broadcast(cube), env.tile_id[:, :].unsqueeze(1).to_broadcast(cube), ALU.is_equal))
            for vals, out in ((start_of[:, 0:NT], env.start_f[:, 0:NT]), (env.degree_in[:, :], env.degree[:, :])):
                link(nc.vector.tensor_tensor(env.picked, pick, vals.unsqueeze(1).to_broadcast(cube), ALU.mult))
                link(nc.vector.tensor_reduce(out, env.picked, AX.X, ALU.add))
            link(nc.vector.tensor_copy(start_of[:, 0:NT], env.start_f[:, 0:NT]))
            link(nc.vector.tensor_scalar(env.node_id[:, 0:NT], env.rank_i[:, :], P_BITS, None, ALU.logical_shift_left))
            link(nc.vector.tensor_tensor(env.node_id[:, 0:NT], env.node_id[:, 0:NT], env.part_id[:, :].to_broadcast([P, NT]), ALU.bitwise_or))
            link(nc.vector.tensor_scalar(env.key_row_index[:, :], start_of[:, 0:NT], SLOT_BITS, None, ALU.logical_shift_right))
            nc.vector.tensor_scalar(env.key_row_index[:, :], env.key_row_index[:, :], 1, None, ALU.add).then_inc(want_keys, 1)
            dve.wait_ge(got_keys, 16 * NT)
            rows, shift_bit = env.key_rows, env.shift_bit
            for b in range(SLOT_BITS - 1, -1, -1):
                link(nc.vector.tensor_scalar(shift_bit[:, :], start_of[:, 0:NT], b, 1, ALU.logical_shift_right, ALU.bitwise_and))
                w = SLOTS + (1 << b) - 1
                link(nc.vector.tensor_copy(env.shifted[:, :, 0:w], rows[:, :, (1 << b):(1 << b) + w]))
                link(nc.vector.copy_predicated(rows[:, :, 0:w], shift_bit[:, :].unsqueeze(2).to_broadcast([P, NT, w]), env.shifted[:, :, 0:w]))
            keyi = rows[:, :, 0:SLOTS].bitcast(I32)
            dst_i, src_i = env.slot_dst, env.slot_row
            link(nc.vector.tensor_scalar(dst_i[:, :, :], keyi, SRC_BITS, (1 << DST_BITS) - 1, ALU.logical_shift_right, ALU.bitwise_and))
            link(nc.vector.tensor_scalar(src_i[:, :, :], keyi, NODES - 1, None, ALU.bitwise_and))
            link(nc.vector.tensor_tensor(env.slot_penalty[:, :, :], dst_i[:, :, :], env.node_id[:, 0:NT].unsqueeze(2).to_broadcast([P, NT, SLOTS]), ALU.not_equal))
            link(nc.vector.scalar_tensor_tensor(src_i[:, :, :], env.slot_penalty[:, :, :], float(NODES), src_i[:, :, :], ALU.mult, ALU.add))
            link(nc.vector.tensor_scalar(env.slot_penalty[:, :, :], env.slot_penalty[:, :, :], -BIG, None, ALU.mult))
            dve.nop().then_inc(deg_ready, 1)
            dve.wait_ge(maxdeg_done, 1)
            link(nc.vector.tensor_scalar(env.tile_groups_f[:, :], env.deg_max[:, :], float(SLOTS), 1.0, ALU.min, ALU.max))
            link(nc.vector.tensor_scalar(env.tile_groups_f[:, :], env.tile_groups_f[:, :], float(SLOT_GROUP - 1), None, ALU.add))
            link(nc.vector.tensor_copy(env.tile_groups[:, :], env.tile_groups_f[:, :]))
            link(nc.vector.tensor_scalar(env.tile_groups[:, :], env.tile_groups[:, :], GROUP_BITS, None, ALU.logical_shift_right))
            link(nc.vector.tensor_scalar(env.tile_groups_f[:, :], env.deg_max[:, :], float(SLOTS - 1), None, ALU.add))
            link(nc.vector.tensor_copy(env.tile_rounds[:, :], env.tile_groups_f[:, :]))
            link(nc.vector.tensor_scalar(env.tile_rounds[:, :], env.tile_rounds[:, :], SLOT_BITS, None, ALU.logical_shift_right))


class Chain:
    def __init__(self, eng, sem, base, per):
        self.eng, self.sem, self.base, self.per, self.n = eng, sem, base, per, 0

    def __call__(self, ins):
        self.n += 1
        ins.then_inc(self.sem, 1)
        self.eng.wait_ge(self.sem, self.base + self.n)

    def end(self):
        assert self.n == self.per, (self.n, self.per)


ROUND_STEPS = 16
ROUNDS_IN = 128
ROUNDS_OUT = E_TOTAL // SLOTS // ROUNDS_IN


def attend(nc, env, load):
    with ExitStack() as ctx:
        sb = lambda n, s, d: ctx.enter_context(nc.sbuf_tensor(n, s, d))
        sem = lambda n: ctx.enter_context(nc.semaphore(n))
        G = sb("gathered", [P, 2, SLOTS, ROW], F32)
        E = sb("edge_logits", [P, 2, SLOTS + 1, HEADS], F32)
        W = sb("edge_weights", [P, 2, SLOTS + 1, HEADS], F32)
        PR = sb("weighted_rows", [P, SLOTS, HEADS * EXPERTS1], F32)
        mr, mn, ds_, s16 = (sb(n, [P, w], F32) for n, w in (("round_max", HEADS), ("new_max", HEADS), ("round_den", HEADS), ("round_sum", 16)))
        of_row = sb("of_row", [P, 1], I32)
        of_bits = sb("of_bits", [P, SLOT_BITS], I32)
        of_keys = sb("of_keys", [P, 2 * SLOTS], F32)
        of_tmp = sb("of_shifted", [P, 2 * SLOTS], F32)
        of_slot, of_pen = sb("of_slot_row", [P, SLOTS], I32), sb("of_penalty", [P, SLOTS], F32)
        of_dst = sb("of_dst", [P, SLOTS], I32)
        rows_in = [sem("rows_in_0"), sem("rows_in_1")]
        rows_used = [sem("rows_used_0"), sem("rows_used_1")]
        own_in = sem("own_rows_in")
        turn = sem("pool_turn")
        cleared, began, step, logits, weights = sem("gathered_cleared"), sem("state_ready"), sem("attend_step"), sem("logits_ready"), sem("weights_ready")
        of_index, of_keys_in, of_slots, of_rows_in = sem("of_index_ready"), sem("of_keys_in"), sem("of_slots_ready"), sem("of_rows_in")
        of_dma, of_step, of_logits, of_weights = sem("of_dma"), sem("of_step"), sem("of_logits_ready"), sem("of_weights_ready")
        CHUNKS, WIDE = 2 * EXPERTS1, 2 * P
        hidden = sb("expert_hidden", [P, CHUNKS, WIDE], F32)
        results = sb("expert_results", [P, EXPERTS1, 2, D], F32)
        raised, activated, lowered = sem("hidden_products"), sem("hidden_activated"), sem("expert_products")
        weights_in = sem("weights_c_loaded")
        results_ready, results_stored = sem("expert_results_ready"), sem("expert_results_stored")
        up_bank = lambda k: env.bank[k // 2][:, (k % 2) * WIDE:(k % 2 + 1) * WIDE]
        block = ctx.enter_context(nc.Block())
        M, DEN, ACC = env.att_max, env.att_den, env.att_acc

        def gather(pool, dst, index, s):
            pool.indirect_dma_start(out=dst, out_offset=None, in_=env.table_dram,
                                    in_offset=bass.IndirectOffsetOnAxis(ap=index, axis=0),
                                    bounds_check=NODES - 1, oob_is_err=False).then_inc(s, 16)

        def further_rounds(eng, first, more):
            with eng.Fori(0, NT // 8) as t8:
                most = eng.value_load(env.tile_rounds[0:1, bass.ds(t8 * 8 + 7, 1)], min_val=0, max_val=E_TOTAL // SLOTS)
                with eng.If(most > 1):
                    with eng.Fori(0, 8) as t_in:
                        t = t8 * 8 + t_in
                        n = eng.value_load(env.tile_rounds[0:1, bass.ds(t, 1)], min_val=0, max_val=E_TOTAL // SLOTS)
                        before = eng.value_load(env.rounds_before[0:1, bass.ds(t, 1)], min_val=0, max_val=E_TOTAL // SLOTS)
                        with eng.If(n > 1):
                            first(t)
                            more(t, before + 1)
                            with eng.If(n > 2):
                                with eng.Fori(0, ROUNDS_OUT) as ro:
                                    with eng.If(n > ro * ROUNDS_IN + 2):
                                        with eng.Fori(0, ROUNDS_IN) as ri:
                                            r = ro * ROUNDS_IN + ri + 2
                                            with eng.If(n > r):
                                                more(t, before + r)

        @block.gpsimd
        def _(pool):
            nc.gpsimd.memset(G[:, :, :, :], 0.0).then_inc(cleared, 1)
            for t in range(NT):
                pool.indirect_dma_start(out=env.own_rows[:, t, :], out_offset=None, in_=env.table_dram,
                                        in_offset=bass.IndirectOffsetOnAxis(ap=env.node_id[:, t:t + 1].bitcast(U32), axis=0),
                                        bounds_check=NODES - 1, oob_is_err=False).then_inc(own_in, 16)
            pool.wait_ge(cleared, 1)
            with pool.Fori(0, NT // 2) as i:
                for u in range(2):
                    t = i * 2 + u
                    pool.wait_ge(rows_used[u], i + 1)
                    pool.sem_inc(turn, 1)
                    n = pool.value_load(env.tile_groups[0:1, bass.ds(t, 1)], min_val=0, max_val=SLOTS // SLOT_GROUP)
                    nc.gpsimd.tensor_copy(env.idx_now[:, u, :], env.slot_row[:, bass.ds(t, 1), :].rearrange("p o s -> p (o s)")).then_inc(env.idx_sem, 1)
                    pool.wait_ge(env.idx_sem, i * 2 + (u + 1))
                    pool.sem_inc(turn, 1)
                    for q in range(SLOTS // SLOT_GROUP):
                        with pool.If(n > q):
                            for j in range(q * SLOT_GROUP, (q + 1) * SLOT_GROUP):
                                gather(pool, G[:, u, j, :], env.idx_now[:, u, j:j + 1].bitcast(U32), rows_in[u])
            def more(c):
                pool.wait_ge(of_index, c)
                pool.sem_inc(turn, 1)
                pool.indirect_dma_start(out=of_keys[:, :], out_offset=None, in_=env.sorted_pairs,
                                        in_offset=bass.IndirectOffsetOnAxis(ap=of_row[:, :].bitcast(U32), axis=0),
                                        bounds_check=KEY_ROWS + 1, oob_is_err=False).then_inc(of_dma, 16)
                pool.wait_ge(of_dma, 16)
                pool.dma_reset(range(of_dma.num, of_dma.num + 1))
                pool.sem_clear(of_dma)
                pool.sem_inc(of_keys_in, 1)
                pool.wait_ge(of_slots, c)
                pool.sem_inc(turn, 1)
                for j in range(SLOTS):
                    gather(pool, G[:, 0, j, :], of_slot[:, j:j + 1].bitcast(U32), of_dma)
                pool.wait_ge(of_dma, 16 * SLOTS)
                pool.dma_reset(range(of_dma.num, of_dma.num + 1))
                pool.sem_clear(of_dma)
                pool.sem_inc(of_rows_in, 1)

            further_rounds(pool, lambda t: None, lambda t, c: more(c))

        @block.sync
        def _(sp):
            sp.dma_start(*load).then_inc(weights_in, 16)
            with sp.Fori(0, NT // 2) as i:
                sp.wait_ge(results_ready, i * 2 + 2)
                sp.dma_start(env.results_dram[bass.ds(i, 1), :, :, :, :].rearrange("o p e j d -> p (o e j d)"), results[:, :, :, :].rearrange("p e j d -> p (e j d)")).then_inc(results_stored, 16)
            sp.wait_ge(results_stored, 16 * (NT // 2))
            sp.wait_ge(weights_in, 16)

        @block.tensor
        def _(pe):
            with pe.Fori(0, NT // 2) as i:
                inputs = env.xt_all[:, bass.ds(i * 2, 2), :].rearrange("p j n -> p (j n)")
                for k in range(CHUNKS):
                    ins = nc.tensor.matmul(up_bank(k), lhsT=env.w("f1_w1", k), rhs=inputs, start=k % 2 == 0, stop=k % 2 == 1, skip_group_check=True)
                    if k % 2 == 1:
                        ins.then_inc(raised, 1)
                for k in range(CHUNKS):
                    e, part = divmod(k, 2)
                    pe.wait_ge(activated, i * CHUNKS + (k + 1))
                    if k == 0:
                        pe.wait_ge(results_ready, i * 2)
                    for j in range(2):
                        ins = nc.tensor.matmul(env.bank[4 + e // 2][:, ((e % 2) * 2 + j) * D:((e % 2) * 2 + j + 1) * D], lhsT=hidden[:, k, j * P:(j + 1) * P], rhs=env.w("f1_w2", k),
                                               start=e % 2 == 0 and part == 0 and j == 0, stop=e % 2 == 1 and part == 1 and j == 1, skip_group_check=True)
                    if k % 4 == 3:
                        ins.then_inc(lowered, 1)

        @block.scalar
        def _(act):
            with act.Fori(0, NT // 2) as i:
                for u in range(2):
                    act.wait_ge(logits, i * 2 + (u + 1))
                    nc.scalar.activation(W[:, u, :, :], E[:, u, :, :], ACT.Exp).then_inc(weights, 1)
                for k in range(CHUNKS):
                    if k % 2 == 0:
                        act.wait_ge(raised, i * (CHUNKS // 2) + (k // 2 + 1))
                    if k == 0:
                        act.wait_ge(lowered, i * 2)
                    nc.scalar.activation(hidden[:, k, :], up_bank(k), ACT.Gelu, bias=env.col("f1_b1", k)).then_inc(activated, 1)
                for b in range(2):
                    act.wait_ge(lowered, i * 2 + (b + 1))
                    if b == 0:
                        act.wait_ge(results_stored, i * 16)
                    nc.scalar.activation(results[:, 2 * b:2 * b + 2, :, :].rearrange("p e j d -> p (e j d)"), env.bank[4 + b][:, :], ACT.Copy).then_inc(results_ready, 1)
            def more(t, c):
                act.wait_ge(of_logits, c)
                nc.scalar.activation(W[:, 0, :, :], E[:, 0, :, :], ACT.Exp).then_inc(of_weights, 1)

            further_rounds(act, lambda t: None, more)

        @block.vector
        def _(dve):
            setup = Chain(dve, began, 0, 12)
            own = env.own_rows
            dve.wait_ge(own_in, 16 * NT)
            setup(nc.vector.tensor_tensor(M[:, :, :], own[:, :, 16:20], own[:, :, 20:ROW], ALU.add))
            setup(nc.vector.scalar_tensor_tensor(M[:, :, :], M[:, :, :], SLOPE, M[:, :, :], ALU.mult, ALU.max))
            setup(nc.vector.memset(DEN[:, :, :], 1.0))
            setup(nc.vector.tensor_copy(ACC[:, :, :], own[:, :, 0:16]))
            setup(nc.vector.tensor_scalar(env.rounds_f[:, :], env.tile_rounds[:, :], -1.0, 0.0, ALU.add, ALU.max))
            setup(nc.vector.tensor_tensor_scan(env.rounds_f2[:, 1:NT + 1], env.ones_nt[:, :], env.rounds_f[:, :], 0.0, ALU.mult, ALU.add))
            setup(nc.vector.tensor_copy(env.rounds_before[:, 1:NT], env.rounds_f2[:, 1:NT]))
            groups = env.tile_groups[:, :].rearrange("p (i u) -> p u i", u=2)
            for u in range(2):
                setup(nc.vector.tensor_scalar(env.groups_f[:, u, :], groups[:, u, :], float(16 * SLOT_GROUP), None, ALU.mult))
                setup(nc.vector.tensor_tensor_scan(env.groups_sum[:, u, :], env.ones_nt[:, 0:NT // 2], env.groups_f[:, u, :], 0.0, ALU.mult, ALU.add))
            setup(nc.vector.tensor_copy(env.rows_due[:, :, :], env.groups_sum[:, :, :]))
            setup.end()

            def weigh(link, t, u, penalty, slots_sem, slots_count, logits_sem, weights_sem, count):
                g, e, w = G[:, u, :, :], E[:, u, 0:SLOTS, :], W[:, u, 0:SLOTS, :]
                m, den, acc = M[:, bass.ds(t, 1), :], DEN[:, bass.ds(t, 1), :], ACC[:, bass.ds(t, 1), :]
                m, den, acc = (v.rearrange("p o h -> p (o h)") for v in (m, den, acc))
                ad = env.own_rows[:, bass.ds(t, 1), 20:ROW].to_broadcast([P, SLOTS, HEADS])
                dve.wait_ge(slots_sem, slots_count)
                link(nc.vector.tensor_tensor(e, g[:, :, 16:20], ad, ALU.add))
                link(nc.vector.tensor_tensor(e, e, penalty.unsqueeze(2).to_broadcast([P, SLOTS, HEADS]), ALU.add))
                link(nc.vector.scalar_tensor_tensor(e, e, SLOPE, e, ALU.mult, ALU.max))
                link(nc.vector.tensor_reduce(mr[:, :], e.rearrange("p j h -> p h j"), AX.X, ALU.max))
                link(nc.vector.tensor_tensor(mn[:, :], m, mr[:, :], ALU.max))
                link(nc.vector.tensor_tensor(E[:, u, SLOTS, :], m, mn[:, :], ALU.subtract))
                link(nc.vector.tensor_tensor(m, m, mr[:, :], ALU.max))
                nc.vector.tensor_tensor(e, e, mn[:, :].unsqueeze(1).to_broadcast([P, SLOTS, HEADS]), ALU.subtract).then_inc(logits_sem, 1)
                dve.wait_ge(weights_sem, count)
                fade = W[:, u, SLOTS, :]
                link(nc.vector.tensor_reduce(ds_[:, :], w.rearrange("p j h -> p h j"), AX.X, ALU.add))
                link(nc.vector.tensor_tensor(den, den, fade, ALU.mult))
                link(nc.vector.tensor_tensor(den, den, ds_[:, :], ALU.add))
                link(nc.vector.tensor_tensor(PR[:, :, :].rearrange("p j (h x) -> p j h x", x=EXPERTS1),
                                             g[:, :, 0:16].rearrange("p j (h x) -> p j h x", x=EXPERTS1),
                                             w.unsqueeze(3).to_broadcast([P, SLOTS, HEADS, EXPERTS1]), ALU.mult))
                link(nc.vector.tensor_reduce(s16[:, :], PR[:, :, :].rearrange("p j f -> p f j"), AX.X, ALU.add))
                av = acc.rearrange("p (h x) -> p h x", x=EXPERTS1)
                link(nc.vector.tensor_tensor(av, av, fade.unsqueeze(2).to_broadcast([P, HEADS, EXPERTS1]), ALU.mult))
                link(nc.vector.tensor_tensor(acc, acc, s16[:, :], ALU.add))

            dve.wait_ge(cleared, 1)
            for u in range(2):
                nc.vector.nop().then_inc(rows_used[u], 1)
            with dve.Fori(0, NT // 2) as i:
                for u in range(2):
                    t = i * 2 + u
                    link = Chain(dve, step, i * (2 * ROUND_STEPS) + u * ROUND_STEPS, ROUND_STEPS)
                    pen = env.slot_penalty[:, bass.ds(t, 1), :].rearrange("p o s -> p (o s)")
                    due = dve.value_load(env.rows_due[0:1, u, bass.ds(i, 1)], min_val=16 * SLOT_GROUP, max_val=16 * SLOTS * NT // 2)
                    weigh(link, t, u, pen, rows_in[u], due, logits, weights, i * 2 + (u + 1))
                    link(dve.nop())
                    nc.vector.nop().then_inc(rows_used[u], 1)
                    link(dve.nop())
                    link.end()
            def first(t):
                link = Chain(dve, of_step, 0, SLOT_BITS + 2)
                start = env.start_of[:, bass.ds(t, 1)]
                for b in range(SLOT_BITS):
                    link(nc.vector.tensor_scalar(of_bits[:, b:b + 1], start, b, 1, ALU.logical_shift_right, ALU.bitwise_and))
                link(nc.vector.tensor_scalar(of_row[:, :], start, SLOT_BITS, None, ALU.logical_shift_right))
                link(nc.vector.tensor_scalar(of_row[:, :], of_row[:, :], 1, None, ALU.add))
                link.end()
                dve.sem_clear(of_step)

            def more(t, c):
                link = Chain(dve, of_step, 0, 2 * SLOT_BITS + 5 + 14)
                nc.vector.tensor_scalar(of_row[:, :], of_row[:, :], 1.0, float(KEY_ROWS + 1), ALU.add, ALU.min).then_inc(of_index, 1)
                dve.wait_ge(of_keys_in, c)
                for b in range(SLOT_BITS - 1, -1, -1):
                    w = SLOTS + (1 << b) - 1
                    link(nc.vector.tensor_copy(of_tmp[:, 0:w], of_keys[:, (1 << b):(1 << b) + w]))
                    link(nc.vector.copy_predicated(of_keys[:, 0:w], of_bits[:, b:b + 1].to_broadcast([P, w]), of_tmp[:, 0:w]))
                ki = of_keys[:, 0:SLOTS].bitcast(I32)
                link(nc.vector.tensor_scalar(of_dst[:, :], ki, SRC_BITS, (1 << DST_BITS) - 1, ALU.logical_shift_right, ALU.bitwise_and))
                link(nc.vector.tensor_scalar(of_slot[:, :], ki, NODES - 1, None, ALU.bitwise_and))
                link(nc.vector.tensor_tensor(of_pen[:, :], of_dst[:, :], env.node_id[:, bass.ds(t, 1)].to_broadcast([P, SLOTS]), ALU.not_equal))
                link(nc.vector.scalar_tensor_tensor(of_slot[:, :], of_pen[:, :], float(NODES), of_slot[:, :], ALU.mult, ALU.add))
                link(nc.vector.tensor_scalar(of_pen[:, :], of_pen[:, :], -BIG, None, ALU.mult))
                dve.sem_inc(of_slots, 1)
                weigh(link, t, 0, of_pen[:, :], of_rows_in, c, of_logits, of_weights, c)
                link.end()
                dve.sem_clear(of_step)

            further_rounds(dve, first, more)
            fin = Chain(dve, env.att_fin, 0, 4)
            fin(nc.vector.tensor_scalar(DEN[:, :, :], DEN[:, :, :], 1e-16, None, ALU.add))
            fin(nc.vector.reciprocal(DEN[:, :, :], DEN[:, :, :]))
            a4 = ACC[:, :, :].rearrange("p t (h x) -> p (t h) x", x=EXPERTS1)
            fin(nc.vector.tensor_tensor(a4, a4, DEN[:, :, :].rearrange("p t h -> p (t h)").unsqueeze(2).to_broadcast([P, NT * HEADS, EXPERTS1]), ALU.mult))
            fin(nc.vector.tensor_tensor(ACC[:, :, :], ACC[:, :, :], env.b_gat[:, :].unsqueeze(1).to_broadcast([P, NT, 16]), ALU.add))


class Steps:
    def __init__(self, eng, done, names):
        self.done, self.names, self.next, self.eng = done, list(names), 0, eng
        self.index = {n: k for k, n in enumerate(self.names)}
        assert len(self.index) == len(self.names)
        self.per = len(self.names)

    def begin(self, eng):
        eng.sem_inc(self.done, self.per)

    def did(self, ins, name):
        assert self.names[self.next % self.per] == name, (self.names[self.next % self.per], name)
        self.next += 1
        ins.then_inc(self.done, 1)

    def count(self, name, i):
        return i * self.per + (self.per + self.index[name] + 1)


class Link:
    def __init__(self, eng, sem, i, per):
        self.eng, self.sem, self.base, self.per, self.n = eng, sem, i * per, per, 0

    def __call__(self, ins):
        self.n += 1
        ins.then_inc(self.sem, 1)
        self.eng.wait_ge(self.sem, self.base + self.n)

    def end(self):
        self.eng.sem_inc(self.sem, self.per - self.n)
        self.eng.wait_ge(self.sem, self.base + self.per)


class Norms:
    def __init__(self, nc, env, ready, done, per):
        self.nc, self.env, self.ready, self.done, self.per, self.k, self.i = nc, env, ready, done, per, 0, 0

    def invert(self, dve, ins):
        self.k += 1
        ins.then_inc(self.ready, 1)
        dve.wait_ge(self.done, self.i * self.per + self.k)

    def serve(self, pool, i):
        for k in range(self.per):
            pool.wait_ge(self.ready, i * self.per + (k + 1))
            self.nc.gpsimd.tensor_tensor(self.env.ln_rstd[:, :], self.env.ln_var[:, :], self.env.minus_half[:, 0:GT], ALU.pow).then_inc(self.done, 1)


def bcast(ap, shape, axis):
    return ap.unsqueeze(axis).to_broadcast(shape)


def layer_norm(nc, env, link, x, out, scale_shift=None):
    st, mv = env.ln_stats, env.ln_mv
    for j in range(GT):
        ins = nc.vector.bn_stats(st[:, j, :], x[:, j, :])
    link(ins)
    link.eng.sem_inc(env.pause, 1)
    for j in range(GT):
        ins = nc.vector.bn_aggr(mv[:, j, :], st[:, j, :])
    link(ins)
    env.norms.invert(link.eng, nc.vector.tensor_scalar(env.ln_var[:, :], mv[:, :, 1], LN_EPS, None, ALU.add))
    for j in range(GT):
        ins = nc.vector.tensor_scalar(out[:, j, :], x[:, j, :], mv[:, j, 0:1], env.ln_rstd[:, j:j + 1], ALU.subtract, ALU.mult)
    if scale_shift is not None:
        link(ins)
        link(nc.vector.tensor_tensor(out, out, bcast(scale_shift[0], [P, GT, D], 1), ALU.mult))
        ins = nc.vector.tensor_tensor(out, out, bcast(scale_shift[1], [P, GT, D], 1), ALU.add)
    return ins


def top_two(nc, env, link, scores, n, tiles, tmp):
    shape = [P, tiles, n]
    full = lambda t: t[:, 0:tiles, 0:n]
    one = lambda t: t[:, 0:tiles]

    def mark(vals, top, where):
        link(nc.vector.tensor_reduce(one(top), vals, AX.X, ALU.max))
        link(nc.vector.tensor_tensor(full(tmp.tie), vals, bcast(one(top), shape, 2), ALU.is_equal))
        link(nc.vector.tensor_tensor(full(tmp.tie), full(tmp.tie), bcast(env.earlier[:, 0:n], shape, 1), ALU.mult))
        link(nc.vector.tensor_reduce(one(tmp.best), full(tmp.tie), AX.X, ALU.max))
        link(nc.vector.tensor_tensor(full(where), full(tmp.tie), bcast(one(tmp.best), shape, 2), ALU.is_equal))

    mark(scores, tmp.max1, tmp.first)
    link(nc.vector.scalar_tensor_tensor(full(tmp.rest), full(tmp.first), -BIG, scores, ALU.mult, ALU.add))
    mark(full(tmp.rest), tmp.max2, tmp.second)
    return nc.vector.tensor_tensor(one(tmp.diff), one(tmp.max2), one(tmp.max1), ALU.subtract)


def gate_weights(nc, link, out, n, tiles, tmp):
    shape = [P, tiles, n]
    full = lambda t: t[:, 0:tiles, 0:n]
    one = lambda t: t[:, 0:tiles]
    link(nc.vector.tensor_scalar(one(tmp.w1), one(tmp.diff_exp), 1.0, None, ALU.add))
    link(nc.vector.reciprocal(one(tmp.w1), one(tmp.w1)))
    link(nc.vector.tensor_tensor(one(tmp.w2), one(tmp.diff_exp), one(tmp.w1), ALU.mult))
    link(nc.vector.tensor_tensor(full(tmp.first), full(tmp.first), bcast(one(tmp.w1), shape, 2), ALU.mult))
    link(nc.vector.tensor_tensor(full(tmp.second), full(tmp.second), bcast(one(tmp.w2), shape, 2), ALU.mult))
    return nc.vector.tensor_tensor(out, full(tmp.first), full(tmp.second), ALU.add)


def turn(nc, bank, src, ident, n=P):
    for j in range(GT):
        ins = nc.tensor.transpose(bank[0:n, j * P:(j + 1) * P], src[:, j, 0:n], ident[:, :])
    return ins


def copy(nc, out, in_):
    return nc.vector.tensor_scalar(out, in_, 1.0, None, ALU.mult)


def tiles_of(ap):
    return ap.rearrange("p (j n) -> p j n", j=GT)


STREAMS = 2
TURNS = GROUPS // STREAMS


def by_stage(stages):
    return [f"{n}@{s}" for names in stages for s in range(STREAMS) for n in names]


class StreamA:
    def __init__(self, sb, s, turned, out):
        w = lambda n: sb(f"{n}_{s}", [P, GT, D])
        self.s, self.turned, self.out = s, turned, out
        self.X, self.XH, self.ADJ, self.ADJT, self.XT, self.NMP = (w(n) for n in ("x", "xh", "adj", "adjt", "xt", "nmp"))
        self.AG, self.CV, self.XC, self.EX, self.MS = (w(n) for n in ("agg", "conv", "xconv", "dist_exp", "msg"))
        self.T1, self.O, self.NN, self.Z, self.R = self.AG, self.CV, self.XC, self.EX, self.MS
        self.H1P = sb(f"h1p_{s}", [P, GT, P + 2 * CONV_PAD])
        self.GATE, self.ROWL = sb(f"gate_{s}", [P, GT, EXPERTS0]), sb(f"rows_{s}", [P, GT, ROW])


def phase_a(nc, env):
    N0 = EXPERTS0
    expert_steps = [s for t in range(N0 + 2) for s in ([f"u1_{t}"] if t < N0 else []) + ([f"u2_{t-1}"] if 0 < t <= N0 else []) + ([f"y_{t-2}"] if t >= 2 else [])]
    hidden_steps = [s for t in range(N0 + 1) for s in ([f"h1_{t}"] if t < N0 else []) + ([f"h2_{t-1}"] if t > 0 else [])]
    tensor_names = by_stage([["adjT", "l0agg", "l0out"], ["xt1", "rh", "lg"] + expert_steps + ["gt", "gb"],
                             ["xt2", "c1", "se", "dist", "sqm", "msg"], ["c2", "nmp", "ghn", "r", "z", "gin"], ["ot"], ["xt3", "hh"]])
    scalar_names = by_stage([["adjT", "l0agg"], ["xt1", "rh", "l0exp", "g0exp"] + hidden_steps + ["gt"],
                             ["xt2", "se", "se2", "sq", "c1", "nsq", "ex", "ms"], ["xc", "nmp", "r", "z", "nn"], ["xt3"]])
    vector_names = by_stage([["xh0"], ["l0out", "xh1"], ["lg", "probs_in", "g0diff", "gate"] + [f"comb_{e}" for e in range(N0)] + ["gb", "xh2"],
                             ["att"], ["cv", "t1", "o"], ["ot", "xh3"], ["rows"]])
    LINKS = 240

    with ExitStack() as ctx:
        sb = lambda n, s: ctx.enter_context(nc.sbuf_tensor("a_" + n, s, F32))
        sem = lambda n: ctx.enter_context(nc.semaphore("a_" + n))
        ten, sca, vec = (Steps(None, sem(n), s) for n, s in (("tensor_step", tensor_names), ("scalar_step", scalar_names), ("vector_step", vector_names)))
        link_sem, margins = sem("vector_link"), sem("margins_cleared")
        adj_in, rows_out = ([sem(f"{n}_{s}") for s in range(STREAMS)] for n in ("adj_loaded", "rows_stored"))
        B = env.bank
        U1, U2, Y = (B[1], B[2]), (B[3], B[7]), (B[4], B[5])
        streams = [StreamA(sb, s, (B[0], B[6])[s], Y[s]) for s in range(STREAMS)]
        U = sb("u", [P, GT, D])
        H1 = [sb(f"h1_{k}", [P, GT * P]) for k in range(2)]
        H2 = [sb(f"h2_{k}", [P, GT * P]) for k in range(2)]
        RH = sb("rh", [ROUTER_H, GT * P])
        GTR = sb("gate_rows", [N0, GT * P])
        LG, PB = (sb(n, [P, GT, N0]) for n in ("lg", "pb"))
        lsum, NSQ = sb("lsum", [P, GT]), sb("nsq", [P, GT])
        SE, SE2, SQ = (sb(n, [3, GT * P]) for n in ("se", "se2", "sq"))
        PROD = sb("prod", [P, GT, 16])
        flat = lambda t: t[:, :, :].rearrange("p j n -> p (j n)")
        env.norms = norms = Norms(nc, env, sem("var_ready"), sem("rstd_ready"), 4 * STREAMS)
        block = ctx.enter_context(nc.Block())

        @block.sync
        def _(sp):
            with sp.Fori(0, TURNS) as i:
                for st in streams:
                    s = st.s
                    sp.wait_ge(ten.done, ten.count(f"adjT@{s}", i - 1))
                    sp.dma_start(st.ADJ[:, :, :], env.adj_dram[bass.ds(i * (STREAMS * GT) + s * GT, GT), :, :].rearrange("g n m -> n g m")).then_inc(adj_in[s], 16)
                for st in streams:
                    s = st.s
                    sp.wait_ge(vec.done, vec.count(f"rows@{s}", i))
                    sp.dma_start(env.table_dram[bass.ds(i * (STREAMS * GT * P) + s * GT * P, GT * P), :].rearrange("(t p) f -> p t f", p=P), st.ROWL[:, :, :]).then_inc(rows_out[s], 16)
            for s in range(STREAMS):
                sp.wait_ge(rows_out[s], 16 * TURNS)

        @block.gpsimd
        def _(pool):
            with pool.Fori(0, TURNS) as i:
                norms.serve(pool, i)

        @block.tensor
        def _(pe):
            ten.begin(pe)

            def mm(out, lhsT, rhs, start, stop):
                return nc.tensor.matmul(out, lhsT=lhsT, rhs=rhs, start=start, stop=stop, skip_group_check=True)

            with pe.Fori(0, TURNS) as i:
                after = lambda who, name: pe.wait_ge(who.done, who.count(name, i))

                def turned(st, name):
                    after(vec, f"xh{name[2]}@{st.s}")
                    ten.did(turn(nc, st.turned, st.XH, env.ident), f"{name}@{st.s}")
                    after(sca, f"{name}@{st.s}")

                for st in streams:
                    s = st.s
                    pe.wait_ge(adj_in[s], i * 16 + 16)
                    after(vec, f"xh0@{s}")
                    ten.did(turn(nc, st.turned, st.ADJ, env.ident), f"adjT@{s}")
                    after(sca, f"adjT@{s}")
                    for j in range(GT):
                        ins = mm(B[1 + s][:, j * P:(j + 1) * P], st.XH[:, j, :], st.ADJT[:, j, :], j == 0, j == GT - 1)
                    ten.did(ins, f"l0agg@{s}")
                    after(sca, f"l0agg@{s}")
                    for j in range(GT):
                        o = st.out[:, j * P:(j + 1) * P]
                        mm(o, st.AG[:, j, :], env.w("l0_w"), j == 0, False)
                        ins = mm(o, env.ones[0:1, :], env.row("l0_bias"), False, j == GT - 1)
                    ten.did(ins, f"l0out@{s}")
                for st in streams:
                    s, XT = st.s, flat(st.XT)
                    turned(st, "xt1")
                    ten.did(mm(B[3][0:ROUTER_H, :], env.w("rw1"), XT, True, True), f"rh@{s}")
                    after(sca, f"rh@{s}")
                    for j in range(GT):
                        o = st.turned[:, j * N0:(j + 1) * N0]
                        mm(o, RH[:, j * P:(j + 1) * P], env.rw2[:, :], j == 0, False)
                        ins = mm(o, env.ones[0:1, :], env.row("rb2"), False, j == GT - 1)
                    ten.did(ins, f"lg@{s}")
                    for t in range(N0 + 2):
                        if t < N0:
                            if t >= 2:
                                after(sca, f"h1_{t-2}@{s}")
                            ten.did(mm(U1[t % 2][:, :], env.w("ew1", t), XT, True, True), f"u1_{t}@{s}")
                        if 0 < t <= N0:
                            after(sca, f"h1_{t-1}@{s}")
                            ten.did(mm(U2[(t - 1) % 2][:, :], env.w("ew2", t - 1), H1[(t - 1) % 2][:, :], True, True), f"u2_{t-1}@{s}")
                        if t >= 2:
                            e = t - 2
                            after(sca, f"h2_{e}@{s}")
                            if e >= 2:
                                after(vec, f"comb_{e-2}@{s}")
                            elif s == 1 and e == 0:
                                after(vec, f"comb_{N0-1}@0")
                            elif s == 0 and e == 1:
                                after(vec, "l0out@1")
                            for j in range(GT):
                                ins = mm(Y[e % 2][:, j * P:(j + 1) * P], H2[e % 2][:, j * P:(j + 1) * P], env.w("ew3", e), j == 0, j == GT - 1)
                            ten.did(ins, f"y_{e}@{s}")
                    after(vec, f"gate@{s}")
                    ten.did(turn(nc, B[3], st.GATE, env.ident, N0), f"gt@{s}")
                    after(sca, f"gt@{s}")
                    for j in range(GT):
                        ins = mm(st.turned[:, j * P:(j + 1) * P], GTR[:, j * P:(j + 1) * P], env.eb3[:, :], j == 0, j == GT - 1)
                    ten.did(ins, f"gb@{s}")
                for st in streams:
                    s, XT = st.s, flat(st.XT)
                    turned(st, "xt2")
                    ten.did(mm(B[1][:, :], env.w("conv1"), XT, True, True), f"c1@{s}")
                    ten.did(mm(B[2][0:3, :], env.w("w_se"), XT, True, True), f"se@{s}")
                    after(sca, f"sq@{s}")
                    for j in range(GT):
                        o, c = B[3][:, j * P:(j + 1) * P], slice(j * P, (j + 1) * P)
                        mm(o, SE[:, c], SE2[:, c], j == 0, False)
                        ins = mm(o, env.neg_ones[:, :], SQ[:, c], False, j == GT - 1)
                    ten.did(ins, f"dist@{s}")
                    for j in range(GT):
                        ins = mm(B[7][:, j:j + 1], SQ[:, j * P:(j + 1) * P], env.neg_ones[:, 0:1], j == 0, j == GT - 1)
                    ten.did(ins, f"sqm@{s}")
                    if s == 0:
                        after(vec, f"comb_{N0-1}@1")
                    for j in range(GT):
                        o = st.out[:, j * P:(j + 1) * P]
                        mm(o, XT[:, j * P:(j + 1) * P], env.w("w_msg"), j == 0, False)
                        ins = mm(o, env.ones[0:1, :], env.row("b_msg"), False, j == GT - 1)
                    ten.did(ins, f"msg@{s}")
                for st in streams:
                    s, XT = st.s, flat(st.XT)
                    after(sca, f"ms@{s}")
                    for k in range(CONV_K):
                        ins = mm(tiles_of(st.out[:, :]), env.w("conv2", k), st.H1P[:, :, k:k + P], k == 0, k == CONV_K - 1)
                    ten.did(ins, f"c2@{s}")
                    after(vec, f"att@{s}" if s == 0 else "t1@0")
                    for j in range(GT):
                        ins = mm(B[2][:, j * P:(j + 1) * P], st.MS[:, j, :], st.EX[:, j, :], j == 0, j == GT - 1)
                    ten.did(ins, f"nmp@{s}")
                    if s == 0:
                        after(sca, f"ex@{STREAMS-1}")
                    ten.did(mm(B[3][:, :], env.w("w_hh", 2), XT, True, True), f"ghn@{s}")
                    after(sca, f"nmp@{s}")
                    for gate, bank in ((0, B[7]), (1, B[1]), (2, st.out)):
                        if gate < 2:
                            mm(bank[:, :], env.w("w_hh", gate), XT, True, False)
                        mm(bank[:, :], env.w("w_ih", 3 + gate), flat(st.NMP), gate == 2, False)
                        ins = mm(bank[:, :], env.w("w_ih", gate), flat(st.XC), False, True)
                        ten.did(ins, f"{('r', 'z', 'gin')[gate]}@{s}")
                for st in streams:
                    after(vec, f"o@{st.s}")
                    ten.did(turn(nc, st.turned, st.O, env.ident), f"ot@{st.s}")
                for st in streams:
                    turned(st, "xt3")
                    for j in range(GT):
                        ins = mm(B[1 + st.s][:, j * 16:(j + 1) * 16], st.XT[:, j, :], env.w("w_gat"), j == 0, j == GT - 1)
                    ten.did(ins, f"hh@{st.s}")

        @block.scalar
        def _(act):
            act.wait_ge(margins, 1)
            sca.begin(act)
            go = nc.scalar.activation
            with act.Fori(0, TURNS) as i:
                after = lambda who, name: act.wait_ge(who.done, who.count(name, i))

                def turned(st, name):
                    after(ten, f"{name}@{st.s}")
                    sca.did(go(st.XT[:, :, :], tiles_of(st.turned[:, :]), ACT.Copy), f"{name}@{st.s}")

                for st in streams:
                    after(ten, f"adjT@{st.s}")
                    sca.did(go(st.ADJT[:, :, :], tiles_of(st.turned[:, :]), ACT.Copy), f"adjT@{st.s}")
                    after(ten, f"l0agg@{st.s}")
                    sca.did(go(flat(st.AG), B[1 + st.s][:, :], ACT.Copy), f"l0agg@{st.s}")
                for st in streams:
                    s = st.s
                    turned(st, "xt1")
                    after(ten, f"rh@{s}")
                    sca.did(go(RH[:, :], B[3][0:ROUTER_H, :], ACT.Relu, bias=env.col("rb1")[0:ROUTER_H, :]), f"rh@{s}")
                    after(vec, f"lg@{s}")
                    sca.did(go(PB[:, :, :], LG[:, :, :], ACT.Exp), f"l0exp@{s}")
                    after(vec, f"g0diff@{s}")
                    sca.did(go(env.top.diff_exp[:, 0:GT], env.top.diff[:, 0:GT], ACT.Exp), f"g0exp@{s}")
                    for t in range(N0 + 1):
                        if t < N0:
                            after(ten, f"u1_{t}@{s}")
                            sca.did(go(H1[t % 2][:, :], U1[t % 2][:, :], ACT.Relu, bias=env.col("eb1", t)), f"h1_{t}@{s}")
                        if t > 0:
                            after(ten, f"u2_{t-1}@{s}")
                            sca.did(go(H2[(t - 1) % 2][:, :], U2[(t - 1) % 2][:, :], ACT.Relu, bias=env.col("eb2", t - 1)), f"h2_{t-1}@{s}")
                    after(ten, f"gt@{s}")
                    sca.did(go(GTR[:, :], B[3][0:N0, :], ACT.Copy), f"gt@{s}")
                for st in streams:
                    s = st.s
                    turned(st, "xt2")
                    after(ten, f"se@{s}")
                    sca.did(go(SE[:, :], B[2][0:3, :], ACT.Identity, bias=env.col("b_se")[0:3, :]), f"se@{s}")
                    act.wait_ge(sca.done, sca.count(f"se@{s}", i))
                    sca.did(go(SE2[:, :], SE[:, :], ACT.Copy, scale=2.0), f"se2@{s}")
                    sca.did(go(SQ[:, :], SE[:, :], ACT.Square), f"sq@{s}")
                    sca.did(go(st.H1P[:, :, CONV_PAD:CONV_PAD + P], tiles_of(B[1][:, :]), ACT.Relu, bias=env.bn_shift[:, 0:1], scale=env.bn_scale[:, 0:1]), f"c1@{s}")
                    after(ten, f"sqm@{s}")
                    sca.did(go(NSQ[:, :], B[7][:, 0:GT], ACT.Copy), f"nsq@{s}")
                    act.wait_ge(sca.done, sca.count(f"nsq@{s}", i))
                    for j in range(GT):
                        ins = go(st.EX[:, j, :], B[3][:, j * P:(j + 1) * P], ACT.Exp, bias=NSQ[:, j:j + 1])
                    sca.did(ins, f"ex@{s}")
                    after(ten, f"msg@{s}")
                    sca.did(go(st.MS[:, :, :], tiles_of(st.out[:, :]), ACT.Relu), f"ms@{s}")
                for st in streams:
                    s = st.s
                    after(vec, f"cv@{s}")
                    sca.did(go(st.XC[:, :, :], st.CV[:, :, :], ACT.Relu, bias=env.bn_shift[:, 1:2]), f"xc@{s}")
                    after(ten, f"nmp@{s}")
                    sca.did(go(flat(st.NMP), B[2][:, :], ACT.Copy), f"nmp@{s}")
                    after(ten, f"r@{s}")
                    sca.did(go(flat(st.R), B[7][:, :], ACT.Tanh, bias=env.gru_bias[:, 0:1], scale=0.5), f"r@{s}")
                    after(ten, f"z@{s}")
                    sca.did(go(flat(st.Z), B[1][:, :], ACT.Tanh, bias=env.gru_bias[:, 1:2], scale=0.5), f"z@{s}")
                    after(vec, f"t1@{s}")
                    sca.did(go(st.NN[:, :, :], st.T1[:, :, :], ACT.Tanh, bias=env.col("b_ih", 2)), f"nn@{s}")
                for st in streams:
                    turned(st, "xt3")

        @block.vector
        def _(dve):
            v = nc.vector
            for st in streams:
                ins = v.memset(st.H1P[:, :, :], 0.0)
            ins.then_inc(margins, 1)
            dve.wait_ge(margins, 1)
            vec.begin(dve)
            with dve.Fori(0, TURNS) as i:
                link = Link(dve, link_sem, i, LINKS)
                norms.i = i
                after = lambda who, name: dve.wait_ge(who.done, who.count(name, i))

                def did(ins, name):
                    vec.did(ins, name)
                    dve.wait_ge(vec.done, vec.count(name, i))

                norm = lambda st: layer_norm(nc, env, link, st.X, st.XH[:, :, :])
                tiles = lambda st: bass.ds(i * (STREAMS * GT) + st.s * GT, GT)
                for st in streams:
                    link(copy(nc, st.X[:, :, :], env.x[:, tiles(st), :]))
                    did(norm(st), f"xh0@{st.s}")
                for st in streams:
                    X = st.X[:, :, :]
                    after(ten, f"l0out@{st.s}")
                    bank = tiles_of(st.out[:, :])
                    link(v.tensor_scalar(U[:, :, :], bank, 0.0, env.prelu[:, :], ALU.min, ALU.mult))
                    did(v.scalar_tensor_tensor(U[:, :, :], bank, 0.0, U[:, :, :], ALU.max, ALU.add), f"l0out@{st.s}")
                    link(v.tensor_tensor(X, X, U[:, :, :], ALU.add))
                    did(norm(st), f"xh1@{st.s}")
                for st in streams:
                    s, X, GATE = st.s, st.X, st.GATE
                    after(ten, f"lg@{s}")
                    lg = st.turned[:, 0:GT * N0].rearrange("p (j e) -> p j e", j=GT)
                    s4 = [P, GT, N0]
                    link(v.tensor_reduce(lsum[:, :], lg, AX.X, ALU.max))
                    did(v.tensor_tensor(LG[:, :, :], lg, bcast(lsum[:, :], s4, 2), ALU.subtract), f"lg@{s}")
                    after(sca, f"l0exp@{s}")
                    link(v.tensor_reduce(lsum[:, :], PB[:, :, :], AX.X, ALU.add))
                    link(v.reciprocal(lsum[:, :], lsum[:, :]))
                    did(v.tensor_tensor(PB[:, :, :], PB[:, :, :], bcast(lsum[:, :], s4, 2), ALU.mult), f"probs_in@{s}")
                    did(top_two(nc, env, link, PB[:, :, :], N0, GT, env.top), f"g0diff@{s}")
                    after(sca, f"g0exp@{s}")
                    did(gate_weights(nc, link, GATE[:, :, :], N0, GT, env.top), f"gate@{s}")
                    for e in range(N0):
                        after(ten, f"y_{e}@{s}")
                        for j in range(GT):
                            ins = v.scalar_tensor_tensor(X[:, j, :], Y[e % 2][:, j * P:(j + 1) * P], GATE[:, j, e:e + 1], X[:, j, :], ALU.mult, ALU.add)
                        did(ins, f"comb_{e}@{s}")
                    after(ten, f"gb@{s}")
                    did(v.tensor_tensor(X[:, :, :], X[:, :, :], tiles_of(st.turned[:, :]), ALU.add), f"gb@{s}")
                    did(norm(st), f"xh2@{s}")
                for st in streams:
                    after(sca, f"ex@{st.s}")
                    did(v.tensor_tensor(st.EX[:, :, :], st.EX[:, :, :], st.ADJT[:, :, :], ALU.mult), f"att@{st.s}")
                for st in streams:
                    s = st.s
                    R, T1, Z, O, XT, NN = (t[:, :, :] for t in (st.R, st.T1, st.Z, st.O, st.XT, st.NN))
                    after(ten, f"c2@{s}")
                    did(v.scalar_tensor_tensor(st.CV[:, :, :], tiles_of(st.out[:, :]), env.bn_scale[:, 1:2], XT, ALU.mult, ALU.add), f"cv@{s}")
                    after(sca, f"r@{s}")
                    link(v.tensor_scalar(R, R, 0.5, 0.5, ALU.mult, ALU.add))
                    link(v.scalar_tensor_tensor(T1, tiles_of(B[3][:, :]), env.col("b_hh", 2), R, ALU.add, ALU.mult))
                    after(ten, f"gin@{s}")
                    did(v.tensor_tensor(T1, T1, tiles_of(st.out[:, :]), ALU.add), f"t1@{s}")
                    after(sca, f"nn@{s}")
                    link(v.tensor_scalar(Z, Z, 0.5, 0.5, ALU.mult, ALU.add))
                    link(v.tensor_tensor(O, XT, NN, ALU.subtract))
                    link(v.tensor_tensor(O, O, Z, ALU.mult))
                    did(v.tensor_tensor(O, O, NN, ALU.add), f"o@{s}")
                for st in streams:
                    after(ten, f"ot@{st.s}")
                    did(v.tensor_tensor(st.X[:, :, :], st.X[:, :, :], tiles_of(st.turned[:, :]), ALU.add), f"ot@{st.s}")
                    link(copy(nc, env.x[:, tiles(st), :], st.X[:, :, :]))
                    did(norm(st), f"xh3@{st.s}")
                for st in streams:
                    after(ten, f"hh@{st.s}")
                    ROWL = st.ROWL
                    link(copy(nc, env.xt_all[:, tiles(st), :], st.XT[:, :, :]))
                    link(v.tensor_copy(ROWL[:, :, 0:16], B[1 + st.s][:, 0:GT * 16].rearrange("p (j f) -> p j f", j=GT)))
                    for att, at in ((env.att_src, 16), (env.att_dst, 20)):
                        link(v.tensor_tensor(PROD[:, :, :], ROWL[:, :, 0:16], bcast(att, [P, GT, 16], 1), ALU.mult))
                        for j in range(GT):
                            ins = v.tensor_reduce(ROWL[:, j, at:at + HEADS], PROD[:, j, :].rearrange("p (h x) -> p h x", x=EXPERTS1), AX.X, ALU.add)
                        if at == 16:
                            link(ins)
                    did(ins, f"rows@{st.s}")
                link.end()
                for s in range(STREAMS):
                    dve.wait_ge(rows_out[s], i * 16 + 16)


class Experts:
    def __init__(self, tag, experts, chunks, w1, w2, b1, b2, func):
        self.tag, self.experts, self.chunks, self.total = tag, experts, chunks, experts * chunks
        self.w1, self.w2, self.b1, self.b2, self.func = w1, w2, b1, b2, func

    def tensor_names(self):
        out = []
        for k in range(self.total + 1):
            out += [f"{self.tag}_up_{k}"] if k < self.total else []
            out += [f"{self.tag}_down_{k-1}"] if k > 0 else []
        return out + [f"{self.tag}_gt", f"{self.tag}_gb"]

    def scalar_names(self):
        return [f"{self.tag}_h_{k}" for k in range(self.total)] + [f"{self.tag}_gt"]

    def vector_names(self):
        return [f"{self.tag}_comb_{e}" for e in range(self.experts)] + [f"{self.tag}_gb"]


class Stream:
    def __init__(self, sb, s, bank, tiles):
        self.s, self.turned = s, bank
        self.X, self.XH, self.ADJ, self.ADJT, self.SM, self.OUT, self.XT, self.AG = tiles
        self.GTR, self.GATE = sb(f"gate_rows_{s}", [EMAX, GT * P]), sb(f"gate_{s}", [P, GT, EMAX])
        self.nmx, self.ssum = sb(f"nmx_{s}", [P, GT]), sb(f"ssum_{s}", [P, GT])


def phase_c(nc, env):
    f2 = Experts("f2", EXPERTS2 + 1, 4, "f2_w1", "f2_w2", "f2_b1", env.f2_b2, ACT.Gelu)
    f3 = Experts("f3", EXPERTS3, 4, "f3_w1", "f3_w2", "f3_b1", env.f3_b2, ACT.Relu)
    tensor_names = by_stage([["f1_gt", "f1_gb"], ["g2_adjT", "g2_xt", "agg", "conv"], ["f2_xt", "f2_lg"] + f2.tensor_names(),
                             ["g3_xt", "inter", "sim"], ["pt", "ov"], ["f3_xt", "f3_lg"] + f3.tensor_names()])
    scalar_names = by_stage([["f1_gt"], ["g2_adjT", "g2_xt", "agg"], ["f2_xt", "f2_exp"] + f2.scalar_names(),
                             ["g3_xt", "inter"], ["soft", "pt"], ["f3_xt", "f3_exp"] + f3.scalar_names()])
    vector_names = by_stage([["f1_gate"], ["f1_sum", "f1_gb", "g2_xh"], ["conv", "f2_xh"], ["f2_diff", "f2_gate"] + f2.vector_names() + ["g3_xh"],
                             ["masked"], ["ov", "f3_xh"], ["f3_diff", "f3_gate"] + f3.vector_names() + ["out"]])
    LINKS = 300
    with ExitStack() as ctx:
        sb = lambda n, s, d=F32: ctx.enter_context(nc.sbuf_tensor("c_" + n, s, d))
        sem = lambda n: ctx.enter_context(nc.semaphore("c_" + n))
        ten, sca, vec = (Steps(None, sem(n), s) for n, s in (("tensor_step", tensor_names), ("scalar_step", scalar_names), ("vector_step", vector_names)))
        link_sem = sem("vector_link")
        adj_in, mask_in, results_in, stored = ([sem(f"{n}_{s}") for s in range(STREAMS)] for n in ("adj_loaded", "mask_loaded", "results_loaded", "out_stored"))
        B = env.bank
        U, Y = (B[1], B[2], B[3]), (B[4], B[5])
        streams = [Stream(sb, s, (B[0], B[6])[s], env.left_tiles[8 * s:8 * s + 8]) for s in range(STREAMS)]
        H = [sb(f"h_{k}", [P, GT * P]) for k in range(3)]
        LG, mx = sb("lg", [P, GT, EMAX]), sb("mx", [P, GT])
        MI = [sb(f"mask_int_{s}", [P, GT, P], I32) for s in range(STREAMS)]
        MK, MB = sb("mask", [P, GT, P]), sb("mask_bias", [P, GT, P])
        RES = [env.results_of(s) for s in range(STREAMS)]
        env.norms = norms = Norms(nc, env, sem("var_ready"), sem("rstd_ready"), 5 * STREAMS)
        flat = lambda t: t[:, :, :].rearrange("p j n -> p (j n)")
        block = ctx.enter_context(nc.Block())

        @block.gpsimd
        def _(pool):
            with pool.Fori(0, TURNS) as i:
                norms.serve(pool, i)

        @block.sync
        def _(sp):
            with sp.Fori(0, TURNS) as i:
                for st in streams:
                    s = st.s
                    sp.wait_ge(vec.done, vec.count(f"f1_sum@{s}", i - 1))
                    sp.dma_start(RES[s][:, :, :, :, :].rearrange("p h e j d -> p h (e j d)"),
                                 env.results_dram[bass.ds(i * (STREAMS * GT // 2) + s * (GT // 2), GT // 2), :, :, :, :].rearrange("h p e j d -> p h (e j d)")).then_inc(results_in[s], 16)
                for st in streams:
                    s = st.s
                    graphs = bass.ds(i * (STREAMS * GT) + s * GT, GT)
                    sp.wait_ge(vec.done, vec.count(f"masked@{s}", i - 1))
                    sp.dma_start(st.ADJ[:, :, :], env.adj_dram[graphs, :, :].rearrange("g n m -> n g m")).then_inc(adj_in[s], 16)
                    sp.dma_start(MI[s][:, :, :], env.mask_dram[graphs, :].partition_broadcast(P)).then_inc(mask_in[s], 16)
                for st in streams:
                    s = st.s
                    graphs = bass.ds(i * (STREAMS * GT) + s * GT, GT)
                    sp.wait_ge(vec.done, vec.count(f"out@{s}", i))
                    sp.dma_start(env.out_dram[graphs, :, :].rearrange("g n d -> n g d"), st.OUT[:, :, :]).then_inc(stored[s], 16)
            for s in range(STREAMS):
                sp.wait_ge(stored[s], 16 * TURNS)

        @block.tensor
        def _(pe):
            ten.begin(pe)
            mm = nc.tensor.matmul
            with pe.Fori(0, TURNS) as i:
                after = lambda who, name: pe.wait_ge(who.done, who.count(name, i))

                def turned(st, name):
                    after(vec, f"{name}h@{st.s}")
                    ten.did(turn(nc, st.turned, st.XH, env.ident), f"{name}t@{st.s}")
                    after(sca, f"{name}t@{st.s}")

                def biases(st, tag, n, b2):
                    ten.did(turn(nc, B[7], st.GATE, env.ident, n), f"{tag}_gt@{st.s}")
                    after(sca, f"{tag}_gt@{st.s}")
                    for j in range(GT):
                        ins = mm(st.turned[:, j * P:(j + 1) * P], lhsT=st.GTR[0:n, j * P:(j + 1) * P], rhs=b2[:, :], start=j == 0, stop=j == GT - 1, skip_group_check=True)
                    ten.did(ins, f"{tag}_gb@{st.s}")

                def experts(st, f, out_free):
                    s, XT = st.s, flat(st.XT)
                    for k in range(f.total + 1):
                        if k < f.total:
                            if k >= 3:
                                after(sca, f"{f.tag}_h_{k-3}@{s}")
                            ten.did(mm(U[k % 3][:, :], lhsT=env.w(f.w1, k), rhs=XT, start=True, stop=True), f"{f.tag}_up_{k}@{s}")
                        if k > 0:
                            c = k - 1
                            e, part = divmod(c, f.chunks)
                            after(sca, f"{f.tag}_h_{c}@{s}")
                            if c == 0:
                                after(vec, out_free)
                            if part == 0 and e >= 2:
                                after(vec, f"{f.tag}_comb_{e-2}@{s}")
                            for j in range(GT):
                                ins = mm(Y[e % 2][:, j * P:(j + 1) * P], lhsT=H[c % 3][:, j * P:(j + 1) * P], rhs=env.w(f.w2, c),
                                         start=j == 0 and part == 0, stop=j == GT - 1 and part == f.chunks - 1, skip_group_check=True)
                            ten.did(ins, f"{f.tag}_down_{c}@{s}")
                    after(vec, f"{f.tag}_gate@{s}")
                    biases(st, f.tag, f.experts, f.b2)

                def free_after(st, f, name):
                    return f"{name}@1" if st.s == 0 else f"{f.tag}_comb_{f.experts - 1}@0"

                def router(st, f, n, w, bias):
                    XT = flat(st.XT)
                    for j in range(GT):
                        o = B[7][:, j * n:(j + 1) * n]
                        ins = mm(o, lhsT=XT[:, j * P:(j + 1) * P], rhs=env.w(w), start=j == 0, stop=bias is None and j == GT - 1, skip_group_check=True)
                        if bias is not None:
                            ins = mm(o, lhsT=env.ones[0:1, :], rhs=env.row(bias), start=False, stop=j == GT - 1, skip_group_check=True)
                    ten.did(ins, f"{f.tag}_lg@{st.s}")

                for st in streams:
                    after(vec, f"f1_gate@{st.s}")
                    biases(st, "f1", EXPERTS1, env.f1_b2)
                for st in streams:
                    s, AG, XT = st.s, flat(st.AG), flat(st.XT)
                    pe.wait_ge(adj_in[s], i * 16 + 16)
                    after(vec, f"g2_xh@{s}")
                    ten.did(turn(nc, st.turned, st.ADJ, env.ident), f"g2_adjT@{s}")
                    after(sca, f"g2_adjT@{s}")
                    turned(st, "g2_x")
                    for j in range(GT):
                        ins = mm(U[s][:, j * P:(j + 1) * P], lhsT=st.XH[:, j, :], rhs=st.ADJT[:, j, :], start=j == 0, stop=j == GT - 1, skip_group_check=True)
                    ten.did(ins, f"agg@{s}")
                    after(sca, f"agg@{s}")
                    for j in range(GT):
                        o, c = Y[s][:, j * P:(j + 1) * P], slice(j * P, (j + 1) * P)
                        mm(o, lhsT=AG[:, c], rhs=env.w("w_rel"), start=j == 0, stop=False, skip_group_check=True)
                        mm(o, lhsT=XT[:, c], rhs=env.w("w_root"), start=False, stop=False, skip_group_check=True)
                        ins = mm(o, lhsT=env.ones[0:1, :], rhs=env.row("b_rel"), start=False, stop=j == GT - 1, skip_group_check=True)
                    ten.did(ins, f"conv@{s}")
                for st in streams:
                    turned(st, "f2_x")
                    router(st, f2, EXPERTS2, "f2_wr", None)
                    experts(st, f2, free_after(st, f2, "conv"))
                for st in streams:
                    s, XT = st.s, flat(st.XT)
                    turned(st, "g3_x")
                    ten.did(mm(B[3][:, :], lhsT=env.w("g3_w"), rhs=XT, start=True, stop=True), f"inter@{s}")
                    after(sca, f"inter@{s}")
                    for j in range(GT):
                        c = slice(j * P, (j + 1) * P)
                        ins = mm(U[s][:, c], lhsT=flat(st.AG)[:, c], rhs=XT[:, c], start=j == 0, stop=j == GT - 1, skip_group_check=True)
                    ten.did(ins, f"sim@{s}")
                for st in streams:
                    s = st.s
                    after(sca, f"soft@{s}")
                    ten.did(turn(nc, B[3], st.SM, env.ident), f"pt@{s}")
                    after(sca, f"pt@{s}")
                    after(vec, f"f2_comb_{EXPERTS2}@1")
                    for j in range(GT):
                        ins = mm(Y[s][:, j * P:(j + 1) * P], lhsT=st.AG[:, j, :], rhs=st.XH[:, j, :], start=j == 0, stop=j == GT - 1, skip_group_check=True)
                    ten.did(ins, f"ov@{s}")
                for st in streams:
                    turned(st, "f3_x")
                    router(st, f3, EXPERTS3, "f3_wg", "f3_bg")
                    experts(st, f3, free_after(st, f3, "ov"))

        @block.scalar
        def _(act):
            sca.begin(act)
            go = nc.scalar.activation
            with act.Fori(0, TURNS) as i:
                after = lambda who, name: act.wait_ge(who.done, who.count(name, i))

                def turned(st, name):
                    after(ten, f"{name}@{st.s}")
                    sca.did(go(st.XT[:, :, :], tiles_of(st.turned[:, :]), ACT.Copy), f"{name}@{st.s}")

                def gates(st, tag, n):
                    after(ten, f"{tag}_gt@{st.s}")
                    sca.did(go(st.GTR[0:n, :], B[7][0:n, :], ACT.Copy), f"{tag}_gt@{st.s}")

                def experts(st, f):
                    s = st.s
                    for k in range(f.total):
                        after(ten, f"{f.tag}_up_{k}@{s}")
                        if k >= 3:
                            after(ten, f"{f.tag}_down_{k-3}@{s}")
                        sca.did(go(H[k % 3][:, :], U[k % 3][:, :], f.func, bias=env.col(f.b1, k)), f"{f.tag}_h_{k}@{s}")
                    gates(st, f.tag, f.experts)

                def pair(st, tag):
                    after(vec, f"{tag}_diff@{st.s}")
                    sca.did(go(env.top.diff_exp[:, 0:GT], env.top.diff[:, 0:GT], ACT.Exp), f"{tag}_exp@{st.s}")

                for st in streams:
                    gates(st, "f1", EXPERTS1)
                for st in streams:
                    after(ten, f"g2_adjT@{st.s}")
                    sca.did(go(st.ADJT[:, :, :], tiles_of(st.turned[:, :]), ACT.Copy), f"g2_adjT@{st.s}")
                    turned(st, "g2_xt")
                    after(ten, f"agg@{st.s}")
                    sca.did(go(flat(st.AG), U[st.s][:, :], ACT.Copy), f"agg@{st.s}")
                for st in streams:
                    turned(st, "f2_xt")
                    pair(st, "f2")
                    experts(st, f2)
                for st in streams:
                    turned(st, "g3_xt")
                    after(ten, f"inter@{st.s}")
                    sca.did(go(flat(st.AG), B[3][:, :], ACT.Copy), f"inter@{st.s}")
                for st in streams:
                    s = st.s
                    after(vec, f"masked@{s}")
                    for j in range(GT):
                        ins = go(st.SM[:, j, :], st.SM[:, j, :], ACT.Exp, bias=st.nmx[:, j:j + 1], accum_out=st.ssum[:, j:j + 1])
                    sca.did(ins, f"soft@{s}")
                    after(ten, f"pt@{s}")
                    sca.did(go(flat(st.AG), B[3][:, :], ACT.Copy), f"pt@{s}")
                for st in streams:
                    turned(st, "f3_xt")
                    pair(st, "f3")
                    experts(st, f3)

        @block.vector
        def _(dve):
            vec.begin(dve)
            v = nc.vector
            with dve.Fori(0, TURNS) as i:
                link = Link(dve, link_sem, i, LINKS)
                norms.i = i
                after = lambda who, name: dve.wait_ge(who.done, who.count(name, i))

                def did(ins, name):
                    vec.did(ins, name)
                    dve.wait_ge(vec.done, vec.count(name, i))

                def experts(st, f):
                    X = st.X
                    for e in range(f.experts):
                        after(ten, f"{f.tag}_down_{(e + 1) * f.chunks - 1}@{st.s}")
                        for j in range(GT):
                            ins = v.scalar_tensor_tensor(X[:, j, :], Y[e % 2][:, j * P:(j + 1) * P], st.GATE[:, j, e:e + 1], X[:, j, :], ALU.mult, ALU.add)
                        did(ins, f"{f.tag}_comb_{e}@{st.s}")
                    after(ten, f"{f.tag}_gb@{st.s}")
                    did(v.tensor_tensor(X[:, :, :], X[:, :, :], tiles_of(st.turned[:, :]), ALU.add), f"{f.tag}_gb@{st.s}")

                def router(st, f, n, first):
                    after(ten, f"{f.tag}_lg@{st.s}")
                    link(v.tensor_copy(LG[:, :, 0:n], B[7][:, 0:GT * n].rearrange("p (j e) -> p j e", j=GT)))
                    did(top_two(nc, env, link, LG[:, :, 0:n], n, GT, env.top), f"{f.tag}_diff@{st.s}")
                    if first:
                        link(v.memset(st.GATE[:, :, 0:1], 1.0))
                    after(sca, f"{f.tag}_exp@{st.s}")
                    did(gate_weights(nc, link, st.GATE[:, :, first:first + n], n, GT, env.top), f"{f.tag}_gate@{st.s}")

                norm = lambda st, *more: layer_norm(nc, env, link, st.X, st.XH[:, :, :], *more)
                for st in streams:
                    tiles = bass.ds(i * (STREAMS * GT) + st.s * GT, GT)
                    link(copy(nc, st.X[:, :, :], env.x[:, tiles, :]))
                    did(copy(nc, st.GATE[:, :, 0:EXPERTS1], env.gates1[:, tiles, :]), f"f1_gate@{st.s}")
                for st in streams:
                    dve.wait_ge(results_in[st.s], i * 16 + 16)
                    X = st.X
                    for e in range(EXPERTS1):
                        for j in range(GT):
                            ins = v.scalar_tensor_tensor(X[:, j, :], RES[st.s][:, j // 2, e, j % 2, :], st.GATE[:, j, e:e + 1], X[:, j, :], ALU.mult, ALU.add)
                        if e < EXPERTS1 - 1:
                            link(ins)
                    did(ins, f"f1_sum@{st.s}")
                    after(ten, f"f1_gb@{st.s}")
                    did(v.tensor_tensor(X[:, :, :], X[:, :, :], tiles_of(st.turned[:, :]), ALU.add), f"f1_gb@{st.s}")
                    link(layer_norm(nc, env, link, st.X, st.OUT[:, :, :]))
                    link(v.tensor_tensor(st.X[:, :, :], st.X[:, :, :], st.OUT[:, :, :], ALU.add))
                    did(layer_norm(nc, env, link, st.OUT, st.XH[:, :, :], (env.gamma, env.beta)), f"g2_xh@{st.s}")
                for st in streams:
                    after(ten, f"conv@{st.s}")
                    did(v.scalar_tensor_tensor(st.X[:, :, :], tiles_of(Y[st.s][:, :]), 0.0, st.X[:, :, :], ALU.max, ALU.add), f"conv@{st.s}")
                    did(norm(st), f"f2_xh@{st.s}")
                for st in streams:
                    router(st, f2, EXPERTS2, 1)
                    experts(st, f2)
                    did(norm(st), f"g3_xh@{st.s}")
                for st in streams:
                    SM = st.SM
                    dve.wait_ge(mask_in[st.s], i * 16 + 16)
                    link(v.tensor_copy(MK[:, :, :], MI[st.s][:, :, :]))
                    link(v.tensor_scalar(MK[:, :, :], MK[:, :, :], 0.0, None, ALU.not_equal))
                    link(v.tensor_scalar(MB[:, :, :], MK[:, :, :], -1.0, BIG, ALU.add, ALU.mult))
                    after(ten, f"sim@{st.s}")
                    link(v.tensor_tensor(SM[:, :, :], tiles_of(U[st.s][:, :]), st.ADJ[:, :, :], ALU.mult))
                    link(v.tensor_tensor(SM[:, :, :], SM[:, :, :], MK[:, :, :], ALU.mult))
                    link(v.tensor_tensor(SM[:, :, :], SM[:, :, :], MB[:, :, :], ALU.add))
                    link(v.tensor_reduce(mx[:, :], SM[:, :, :], AX.X, ALU.max))
                    did(v.tensor_scalar(st.nmx[:, :], mx[:, :], -1.0, None, ALU.mult), f"masked@{st.s}")
                for st in streams:
                    after(ten, f"ov@{st.s}")
                    link(v.reciprocal(st.ssum[:, :], st.ssum[:, :]))
                    for j in range(GT):
                        ins = v.scalar_tensor_tensor(st.X[:, j, :], Y[st.s][:, j * P:(j + 1) * P], st.ssum[:, j:j + 1], st.X[:, j, :], ALU.mult, ALU.add)
                    did(ins, f"ov@{st.s}")
                    did(norm(st), f"f3_xh@{st.s}")
                for st in streams:
                    router(st, f3, EXPERTS3, 0)
                    experts(st, f3)
                    did(v.tensor_copy(st.OUT[:, :, :], st.X[:, :, :]), f"out@{st.s}")
                link.end()
                for s in range(STREAMS):
                    dve.wait_ge(stored[s], i * 16 + 16)


class Top:
    def __init__(self, sb, tiles, n):
        wide, narrow = [P, tiles, n], [P, tiles]
        self.first, self.second, self.tie, self.rest = sb("top_first", wide), sb("top_second", wide), sb("top_tie", wide), sb("top_rest", wide)
        self.max1, self.max2, self.best = sb("top_max1", narrow), sb("top_max2", narrow), sb("top_best", narrow)
        self.diff, self.diff_exp = sb("top_diff", narrow), sb("top_diff_exp", narrow)
        self.w1, self.w2 = sb("top_w1", narrow), sb("top_w2", narrow)


class Names:
    pass


W_A = [("l0_w", 1, 128), ("rw1", 1, 64), ("ew1", 6, 128), ("ew2", 6, 128), ("ew3", 6, 128), ("conv1", 1, 128), ("conv2", 17, 128),
       ("w_se", 1, 3), ("w_msg", 1, 128), ("w_hh", 3, 128), ("w_ih", 6, 128), ("w_gat", 1, 16)]
W_F1 = [("f1_w1", 8, 128), ("f1_w2", 8, 128)]
W_C = [("w_rel", 1, 128), ("w_root", 1, 128), ("f2_wr", 1, 8), ("f2_w1", 36, 128), ("f2_w2", 36, 128),
       ("g3_w", 1, 128), ("f3_wg", 1, 8), ("f3_w1", 32, 128), ("f3_w2", 32, 128)]
COLS = [("rb1", 1), ("eb1", 6), ("eb2", 6), ("b_se", 1), ("bn1_g", 1), ("bn1_b", 1), ("bn1_m", 1), ("bn1_v", 1), ("bn2_g", 1), ("bn2_b", 1),
        ("bn2_m", 1), ("bn2_v", 1), ("b_ih", 3), ("b_hh", 3), ("f1_b1", 8), ("f2_b1", 36), ("f3_b1", 32)]
ROWS = [("l0_bias", 128), ("rb2", 6), ("b_msg", 128), ("b_rel", 128), ("f3_bg", 8)]
SPREAD = [("prelu", 1), ("att_src", 16), ("att_dst", 16), ("b_gat", 16), ("gat_gamma", 16), ("gat_beta", 16), ("gamma", 128), ("beta", 128)]


def offsets(table):
    out, at = {}, 0
    for name, *dims in table:
        out[name] = (at, dims[-1])
        at += dims[0] * dims[-1] if len(dims) > 1 else dims[0]
    return out, at


def setup(nc, env, d):
    with ExitStack() as ctx:
        sem = lambda n: ctx.enter_context(nc.semaphore("s_" + n))
        loaded, made, step, var_in, scaled = sem("loaded"), sem("constants_made"), sem("vector_step"), sem("bn_variance_ready"), sem("bn_scale_ready")
        block = ctx.enter_context(nc.Block())

        @block.sync
        def _(sp):
            sp.dma_start(env.cols[:, :], d["cols"]).then_inc(loaded, 16)
            sp.dma_start(env.spread[:, :], d["spread"].partition_broadcast(P)).then_inc(loaded, 16)
            sp.dma_start(env.rows[:, :], d["rows"].rearrange("(o n) -> o n", o=1)).then_inc(loaded, 16)
            for name, t in (("rw2", env.rw2), ("eb3", env.eb3), ("f1_b2", env.f1_b2), ("f2_b2", env.f2_b2), ("f3_b2", env.f3_b2)):
                sp.dma_start(t[:, :], d[name]).then_inc(loaded, 16)
            sp.dma_start(env.x[:, :, :], d["x"].rearrange("g n d -> n g d")).then_inc(loaded, 16)
            sp.wait_ge(loaded, 16 * 9)

        @block.gpsimd
        def _(pool):
            g = nc.gpsimd
            g.memset(env.ident[:, :], 0.0).then_inc(made, 1)
            pool.wait_ge(made, 1)
            g.affine_select(out=env.ident[:, :], in_=env.ident[:, :], compare_op=ALU.not_equal, fill=1.0, base=0,
                            pattern=[[-1, P]], channel_multiplier=1).then_inc(made, 1)
            g.memset(env.minus_half[:, :], -0.5).then_inc(made, 1)
            g.iota(env.earlier_i[:, :], pattern=[[-1, EMAX]], base=EMAX, channel_multiplier=0).then_inc(made, 1)
            pool.wait_ge(var_in, 1)
            g.tensor_tensor(env.bn_scale[:, :], env.bn_scale[:, :], env.minus_half[:, 0:2], ALU.pow).then_inc(scaled, 1)

        @block.vector
        def _(dve):
            v = nc.vector
            n = [0]

            def link(ins):
                n[0] += 1
                ins.then_inc(step, 1)
                dve.wait_ge(step, n[0])

            v.memset(env.ones[:, :], 1.0)
            v.memset(env.neg_ones[:, :], -1.0)
            v.memset(env.rounds_before[:, 0:1], 0)
            link(v.memset(env.ones_nt[:, :], 1.0))
            dve.wait_ge(made, 4)
            link(v.tensor_copy(env.earlier[:, :], env.earlier_i[:, :]))
            dve.wait_ge(loaded, 16 * 9)
            for k, tag in enumerate(("bn1", "bn2")):
                ins = v.tensor_scalar(env.bn_scale[:, k:k + 1], env.col(tag + "_v"), 1e-5, None, ALU.add)
            ins.then_inc(var_in, 1)
            dve.wait_ge(scaled, 1)
            for k, tag in enumerate(("bn1", "bn2")):
                s, h = env.bn_scale[:, k:k + 1], env.bn_shift[:, k:k + 1]
                link(v.tensor_tensor(s, s, env.col(tag + "_g"), ALU.mult))
                link(v.tensor_tensor(h, s, env.col(tag + "_m"), ALU.mult))
                link(v.tensor_tensor(h, env.col(tag + "_b"), h, ALU.subtract))
            for k in range(2):
                link(v.tensor_tensor(env.gru_bias[:, k:k + 1], env.col("b_ih", k), env.col("b_hh", k), ALU.add))
            link(v.tensor_scalar(env.gru_bias[:, :], env.gru_bias[:, :], 0.5, None, ALU.mult))


def gates_l1(nc, env):
    with ExitStack() as ctx:
        sb = lambda n, s: ctx.enter_context(nc.sbuf_tensor("g_" + n, s, F32))
        step, diff, ex, var_in, rstd = (ctx.enter_context(nc.semaphore("g_" + n)) for n in ("vector_step", "diff_ready", "exp_ready", "var_ready", "rstd_ready"))
        T = sb("centered", [P, NT, 16])
        S = sb("squared", [P, NT, 16])
        mean, var = sb("mean", [P, NT]), sb("var", [P, NT])
        top = Top(sb, NT, EXPERTS1)
        score = sb("score", [P, NT, EXPERTS1])
        PICK, PICKED = env.halves[0], env.halves[1]
        block = ctx.enter_context(nc.Block())

        @block.gpsimd
        def _(pool):
            pool.wait_ge(var_in, 1)
            nc.gpsimd.tensor_tensor(var[:, :], var[:, :], env.minus_half[:, :], ALU.pow).then_inc(rstd, 1)

        @block.scalar
        def _(act):
            act.wait_ge(diff, 1)
            nc.scalar.activation(top.diff_exp[:, :], top.diff[:, :], ACT.Exp).then_inc(ex, 1)

        @block.vector
        def _(dve):
            v = nc.vector
            n = [0]

            def link(ins):
                n[0] += 1
                ins.then_inc(step, 1)
                dve.wait_ge(step, n[0])

            s16 = [P, NT, 16]
            A = env.att_acc
            link(v.tensor_reduce(mean[:, :], A[:, :, :], AX.X, ALU.add))
            link(v.tensor_scalar(mean[:, :], mean[:, :], 1.0 / 16, None, ALU.mult))
            link(v.tensor_tensor(T[:, :, :], A[:, :, :], bcast(mean[:, :], s16, 2), ALU.subtract))
            link(v.tensor_tensor(S[:, :, :], T[:, :, :], T[:, :, :], ALU.mult))
            link(v.tensor_reduce(var[:, :], S[:, :, :], AX.X, ALU.add))
            v.tensor_scalar(var[:, :], var[:, :], 1.0 / 16, LN_EPS, ALU.mult, ALU.add).then_inc(var_in, 1)
            dve.wait_ge(rstd, 1)
            link(v.tensor_tensor(T[:, :, :], T[:, :, :], bcast(var[:, :], s16, 2), ALU.mult))
            link(v.tensor_tensor(T[:, :, :], T[:, :, :], bcast(env.spread_of("gat_gamma"), s16, 1), ALU.mult))
            link(v.tensor_tensor(T[:, :, :], T[:, :, :], bcast(env.spread_of("gat_beta"), s16, 1), ALU.add))
            link(v.tensor_reduce(score[:, :, :], T[:, :, :].rearrange("p t (h x) -> p t x h", x=EXPERTS1), AX.X, ALU.add))
            link(v.tensor_scalar(score[:, :, :], score[:, :, :], 1.0 / HEADS, None, ALU.mult))
            top_two(nc, env, link, score[:, :, :], EXPERTS1, NT, top).then_inc(diff, 1)
            dve.wait_ge(ex, 1)
            link(gate_weights(nc, link, score[:, :, :], EXPERTS1, NT, top))
            cube = [P, NT, NT]
            link(v.tensor_tensor(PICK[:, :, :], env.tile_id[:, :].unsqueeze(2).to_broadcast(cube), env.place_tile[:, :].unsqueeze(1).to_broadcast(cube), ALU.is_equal))
            for e in range(EXPERTS1):
                link(v.tensor_tensor(PICKED[:, :, :], PICK[:, :, :], score[:, :, e].unsqueeze(1).to_broadcast(cube), ALU.mult))
                link(v.tensor_reduce(env.gates1[:, :, e], PICKED[:, :, :], AX.X, ALU.add))


def program(nc, d):
    env = Names()
    with ExitStack() as ctx:
        sb = lambda n, s, dt=F32: ctx.enter_context(nc.sbuf_tensor(n, s, dt))
        sem = lambda n: ctx.enter_context(nc.semaphore(n))

        cols, ncols = offsets(COLS)
        rows, nrows = offsets(ROWS)
        spread, nspread = offsets(SPREAD)
        env.x = sb("x", [P, NT, D])
        env.cols = sb("cols", [P, ncols])
        env.spread = sb("spread", [P, nspread])
        env.rows = sb("rows", [1, nrows])
        env.rw2 = sb("rw2", [ROUTER_H, EXPERTS0])
        env.eb3 = sb("eb3", [EXPERTS0, D])
        env.f1_b2 = sb("f1_b2", [EXPERTS1, D])
        env.f2_b2 = sb("f2_b2", [EXPERTS2 + 1, D])
        env.f3_b2 = sb("f3_b2", [EXPERTS3, D])
        env.ident = sb("ident", [P, P])
        env.ones = sb("ones", [1, P])
        env.neg_ones = sb("neg_ones", [3, P])
        env.earlier_i = sb("earlier_i", [P, EMAX], I32)
        env.earlier = sb("earlier", [P, EMAX])
        env.bn_scale = sb("bn_scale", [P, 2])
        env.bn_shift = sb("bn_shift", [P, 2])
        env.gru_bias = sb("gru_bias", [P, 2])
        env.ln_stats = sb("ln_stats", [P, GT, 6])
        env.ln_mv = sb("ln_mv", [P, GT, 2])
        env.ln_rstd = sb("ln_rstd", [P, GT])
        env.ln_var = sb("ln_var", [P, GT])
        env.minus_half = sb("minus_half", [P, NT])
        env.own_rows = sb("own_rows", [P, NT, ROW])
        env.tile_id = sb("tile_id", [P, NT])
        env.place_tile = sb("place_tile", [P, NT])
        env.gates1 = sb("gates1", [P, NT, EXPERTS1])
        env.att_acc = sb("att_acc", [P, NT, 16])
        env.start_of = sb("start_of", [P, NT1], I32)
        env.node_id = sb("node_id", [P, NT1], I32)
        env.slot_row = sb("slot_row", [P, NT, SLOTS], I32)
        env.slot_penalty = sb("slot_penalty", [P, NT, SLOTS])
        env.tile_groups = sb("tile_groups", [P, NT], I32)
        env.tile_rounds = sb("tile_rounds", [P, NT], I32)
        env.rounds_before = sb("rounds_before", [P, NT], I32)
        env.ones_nt = sb("ones_nt", [P, NT])
        env.top = Top(sb, GT, EMAX)
        env.spread_of = lambda n: env.spread[:, spread[n][0]:spread[n][0] + spread[n][1]]
        env.col = lambda n, k=0: env.cols[:, cols[n][0] + k:cols[n][0] + k + 1]
        env.row = lambda n: env.rows[0:1, rows[n][0]:rows[n][0] + dict(ROWS)[n]]
        env.prelu, env.gamma, env.beta = env.spread_of("prelu"), env.spread_of("gamma"), env.spread_of("beta")
        env.att_src, env.att_dst, env.b_gat = env.spread_of("att_src"), env.spread_of("att_dst"), env.spread_of("b_gat")
        env.bank = [ctx.enter_context(nc.psum_tensor(f"bank{k}", [P, GT * P], F32)) for k in range(8)]
        dram = lambda n, s, dt: nc.dram_tensor(n, s, dt, kind="Internal").ap()
        env.sorted_pairs = dram("sorted_pairs", [KEY_ROWS + 2, 2 * SLOTS], F32)
        env.start_dram = dram("start_dram", [NT1 * P], I32)
        env.results_dram = dram("results_dram", [NT // 2, P, EXPERTS1, 2, D], F32)
        env.table_dram = dram("table_dram", [NODES, ROW], F32)
        env.adj_dram, env.mask_dram, env.out_dram = d["adj"], d["nodemask"], d["out"]
        env.sign_ready, env.idx_sem, env.att_fin, env.pause = sem("sign_ready"), sem("indices_copied"), sem("aggregate_step"), sem("pause")

        def weights(scope, name, table):
            at, width = offsets(table)
            tensor = scope.enter_context(nc.sbuf_tensor(name, [P, width], F32))
            return (lambda n, k=0: tensor[:, at[n][0] + k * at[n][1]:at[n][0] + (k + 1) * at[n][1]]), (tensor[:, :], d[name])

        room = sb("room", [P, NT * P])
        env.xt_all = room[:, :].rearrange("p (t n) -> p t n", t=NT)
        env.halves = [room[:, k * NT * NT:(k + 1) * NT * NT].rearrange("p (a b) -> p a b", a=NT) for k in range(2)]
        env.results_of = lambda s: room[:, s * GT * EXPERTS1 * D:(s + 1) * GT * EXPERTS1 * D].rearrange("p (h e j d) -> p h e j d", h=GT // 2, e=EXPERTS1, j=2)
        left = [room[:, NT * P // 2:], env.slot_penalty[:, :, :].rearrange("p t s -> p (t s)"), env.slot_row[:, :, :].rearrange("p t s -> p (t s)").bitcast(F32)]
        env.left_tiles = [v[:, k * GT * D:(k + 1) * GT * D].rearrange("p (j n) -> p j n", j=GT) for v, tiles in zip(left, (8, 4, 4)) for k in range(tiles)]
        w_f1, load_f1 = weights(ctx, "weights_f1", W_F1)
        setup(nc, env, d)
        phases_a = ctx.enter_context(ExitStack())
        w_a, load_a = weights(phases_a, "weights_a", W_A)
        with ExitStack() as part:
            sbp = lambda n, s, dt=F32: part.enter_context(nc.sbuf_tensor(n, s, dt))
            half = NT * P // 2
            env.keys_a, env.keys_b = room[:, 0:half], room[:, half:2 * half]
            env.end_of = sbp("end_of", [P, NT], I32)
            env.part_id = sbp("part_id", [P, 1], I32)
            env.sign_i = sbp("sign_i", [P, 7], I32)
            env.sign = sbp("sign", [P, 7])
            env.part_id_f = sbp("part_id_f", [P, 1])
            env.lane_id_i, env.lane_id = sbp("lane_id_i", [P, P], I32), sbp("lane_id", [P, P])
            env.later_lane, env.all_lanes = sbp("later_lane", [P, P]), sbp("all_lanes", [P, P])
            env.tail_i = sbp("tail_i", [P, 2 * SLOTS], I32)
            env.tail_keys = sbp("tail_keys", [P, 2 * SLOTS])
            env.first_keys, env.field = sbp("first_keys", [P, P], I32), sbp("field", [P, P], I32)
            env.first_tile, env.first_lane = sbp("first_tile", [P, P]), sbp("first_lane", [P, P])
            env.tile_hot = sbp("tile_hot", [P, P, NT], BF16)
            env.counts, env.tiles_before = sbp("counts", [P, NT1]), sbp("tiles_before", [P, NT1])
            env.node_key = sbp("node_key", [P, NT1], I32)
            env.cnt = sbp("cnt", [P, NT1])
            env.row_f = sbp("row_f", [P, NT1])
            env.row_index = sbp("row_index", [P, NT1], I32)
            env.start_f = sbp("start_f", [P, NT1])
            env.key_row_index = sbp("key_row_index", [P, NT], I32)
            env.key_rows = sbp("key_rows", [P, NT, 2 * SLOTS])
            env.shift_bit = sbp("shift_bit", [P, NT], I32)
            env.degree_in = sbp("degree_in", [P, NT])
            env.rank_a = sbp("rank_a", [P, NT])
            env.rank_b = sbp("rank_b", [P, NT])
            env.rank_i = sbp("rank_i", [P, NT], I32)
            env.tile_id_i = sbp("tile_id_i", [P, NT], I32)
            env.degree = sbp("degree", [P, NT])
            env.deg_max = sbp("deg_max", [P, NT])
            env.tile_groups_f = sbp("tile_groups_f", [P, NT])
            with nc.sbuf_tensor("search_room", [P, 2, NT1 * 2 * SLOTS], F32) as search_room:
                cube = lambda k, a, b: search_room[:, k, 0:a * b].rearrange("p (a b) -> p a b", a=a)
                env.lane_hot = search_room[:, :, :].rearrange("p k n -> p (k n)")[:, 0:P * P // 2].bitcast(BF16).rearrange("p (a b) -> p a b", a=P)
                env.first_rows, env.shifted, env.pick = cube(0, NT1, 2 * SLOTS), cube(0, NT, 2 * SLOTS), cube(0, NT, NT)
                env.is_below, env.picked, env.slot_dst = cube(1, NT1, SLOTS), cube(1, NT, NT), cube(1, NT, SLOTS).bitcast(I32)
                sort_edges(nc, env, d["edge_index"], (load_f1, load_a))
        env.w = w_a
        phase_a(nc, env)
        phases_a.close()

        w_c, load_c = weights(ctx, "weights_c", W_C)
        with ExitStack() as part:
            sbp = lambda n, s, dt=F32: part.enter_context(nc.sbuf_tensor(n, s, dt))
            env.att_max = sbp("att_max", [P, NT, 4])
            env.att_den = sbp("att_den", [P, NT, 4])
            env.rounds_f = sbp("rounds_f", [P, NT])
            env.rounds_f2 = sbp("rounds_f2", [P, NT + 1])
            env.groups_f = sbp("groups_f", [P, 2, NT // 2])
            env.groups_sum = sbp("groups_sum", [P, 2, NT // 2])
            env.rows_due = sbp("rows_due", [P, 2, NT // 2], I32)
            env.idx_now = sbp("idx_now", [P, 2, SLOTS], I32)
            env.w = w_f1
            attend(nc, env, load_c)
        gates_l1(nc, env)
        env.w = w_c
        phase_c(nc, env)


def kernel(**inputs):
    import numpy as np
    import concourse.bacc as bacc
    from concourse.bass_utils import run_bass_kernel_spmd

    a = {k: np.asarray(v) for k, v in inputs.items()}
    flat = lambda t: np.ascontiguousarray(t).reshape(P, -1)
    stack = lambda t: flat(np.transpose(t, (1, 0, 2)))
    rows_in = lambda t: flat(np.transpose(t.reshape(-1, P, t.shape[-1]), (1, 0, 2)))
    col = lambda t: np.ascontiguousarray(t.reshape(-1, P).T)

    def short_col(t):
        out = np.zeros((P, 1), t.dtype)
        out[:t.size, 0] = t
        return out

    g, f = "L1_gnn_", "L1_ffn_"
    weights_a = np.concatenate([
        a["L0_gnn_W"], a["L0_ffn_router_w1"], stack(a["L0_ffn_expert_w1"]), stack(a["L0_ffn_expert_w2"]), stack(a["L0_ffn_expert_w3"]),
        a[g + "conv1_w"][:, :, 0].T, flat(np.transpose(a[g + "conv2_w"], (1, 2, 0))), a[g + "w_se"].T, a[g + "w_msg"].T,
        a[g + "w_hh"].T, flat(np.concatenate([a[g + "w_ih"][:, :P].T, a[g + "w_ih"][:, P:].T], axis=1)), a[f + "W_gat"]], axis=1)
    weights_f1 = np.concatenate([stack(a[f + "W1"]), rows_in(a[f + "W2"].reshape(-1, P))], axis=1)
    weights_c = np.concatenate([
        a["L2_gnn_W_rel"], a["L2_gnn_W_root"], a["L2_ffn_Wr"],
        a["L2_ffn_W1s"], stack(a["L2_ffn_W1p"]), rows_in(a["L2_ffn_W2s"]), rows_in(a["L2_ffn_W2p"].reshape(-1, P)),
        a["L3_gnn_W"], a["L3_ffn_Wg"].T, flat(np.transpose(a["L3_ffn_W1"], (2, 0, 1))),
        rows_in(np.ascontiguousarray(np.transpose(a["L3_ffn_W2"], (0, 2, 1))).reshape(-1, P))], axis=1)
    cols = np.concatenate([
        short_col(a["L0_ffn_router_b1"]), col(a["L0_ffn_expert_b1"]), col(a["L0_ffn_expert_b2"]), short_col(a[g + "b_se"]),
        *[col(a[g + n]) for n in ("bn1_g", "bn1_b", "bn1_m", "bn1_v", "bn2_g", "bn2_b", "bn2_m", "bn2_v", "b_ih", "b_hh")],
        col(a[f + "b1"]), col(a["L2_ffn_b1s"]), col(a["L2_ffn_b1p"]), col(a["L3_ffn_b1"])], axis=1)
    arrays = {
        "x": a["x"], "adj": a["adj"], "nodemask": a["nodemask"], "edge_index": a["L1_ffn_edge_index"],
        "weights_a": weights_a, "weights_f1": weights_f1, "weights_c": weights_c, "cols": cols,
        "rows": np.concatenate([a[n] for n in ("L0_gnn_bias", "L0_ffn_router_b2", g + "b_msg", "L2_gnn_b_rel", "L3_ffn_bg")]),
        "spread": np.concatenate([a["L0_gnn_prelu_a"].reshape(1)] + [a[n].reshape(-1) for n in (
            f + "att_src", f + "att_dst", f + "b_gat", f + "ln_gamma", f + "ln_beta", "L2_gnn_ln_gamma", "L2_gnn_ln_beta")]),
        "rw2": a["L0_ffn_router_w2"], "eb3": a["L0_ffn_expert_b3"], "f1_b2": a[f + "b2"],
        "f2_b2": np.concatenate([a["L2_ffn_b2s"].reshape(1, P), a["L2_ffn_b2p"]], axis=0), "f3_b2": a["L3_ffn_b2"]}
    arrays = {k: np.ascontiguousarray(v) for k, v in arrays.items()}
    nc = bacc.Bacc("TRN2", target_bir_lowering=False, num_devices=1)
    d = {k: nc.dram_tensor(f"in_{k}", v.shape, mybir.dt.from_np(v.dtype), kind="ExternalInput").ap() for k, v in arrays.items()}
    d["out"] = nc.dram_tensor("out", a["x"].shape, F32, kind="ExternalOutput").ap()
    program(nc, d)
    result = run_bass_kernel_spmd(nc, [{f"in_{k}": v for k, v in arrays.items()}], core_ids=[0])
    return result.results[0]["out"]
```
